# Optimizing a Trainium2 kernel written in Bass

```python
import numpy as np
import jax
import jax.numpy as jnp

def _softmax(x, axis=-1):
    return jax.nn.softmax(x, axis=axis)

def _gelu(x):
    return jax.nn.gelu(x, approximate=True)

def _silu(x):
    return jax.nn.silu(x)

def _sigmoid(x):
    return jax.nn.sigmoid(x)

def _layernorm(x, axis=-1, eps=1e-05):
    m = jnp.mean(x, axis=axis, keepdims=True)
    v = jnp.var(x, axis=axis, keepdims=True)
    return (x - m) / jnp.sqrt(v + eps)

def _scatter_add(tgt, idx, src, axis=0):
    return tgt.at[idx].add(src)

def _segment_sum(src, seg, n):
    return jax.ops.segment_sum(src, seg, n)
kernel_name = 'mk_perceiver_d1_seqx_r4_9545d5'

def setup_inputs(seed: int=0):
    np.random.seed(seed)
    _w = jnp.asarray

    def _rec_inputs():
        import jax
        import jax.numpy as jnp
        _rk = jax.random.key(seed)
        x = -0.0003929 + 0.9999 * jax.random.normal(jax.random.fold_in(_rk, 1), (2, 256, 256), jnp.float32)
        _lenS = 256 - jax.random.randint(jax.random.fold_in(_rk, 7), (2,), 0, max(1, 256 // 4) + 1, jnp.int32)
        _lenS2 = 4096 - jax.random.randint(jax.random.fold_in(_rk, 8), (2,), 0, max(1, 4096 // 4) + 1, jnp.int32)
        _ctx_512P = jax.random.normal(jax.random.fold_in(_rk, 11), (2, 16, 128), jnp.float32)
        _ctx_512c = jax.random.dirichlet(jax.random.fold_in(_rk, 511), 0.3 * jnp.ones((16,), jnp.float32), (2, 4096))
        _ctx_512t = jnp.einsum('bsk,bkd->bsd', _ctx_512c, _ctx_512P)
        _ctx_512t = _ctx_512t * jax.lax.rsqrt(jnp.mean(jnp.square(_ctx_512t)) + 1e-12) * 0.953939
        ctx_512 = -1.39393e-06 + 0.999914 * (_ctx_512t + 0.3 * jax.random.normal(jax.random.fold_in(_rk, 611), (2, 4096, 128), jnp.float32))
        return (x, ctx_512)
    x, ctx_512 = _rec_inputs()

    def _L0_xattn_setup():
        import jax, jax.numpy as jnp
        import numpy as np
        HEADS = 16
        D_MODEL = 256
        IMG_MODEL = 128
        D_K = D_MODEL // HEADS
        key = jax.random.key(seed)
        ks = jax.random.split(key, 12)
        B, LQ, LKV = (8, 512, 256)
        s_dm = 1.0 / np.sqrt(D_MODEL)
        s_im = 1.0 / np.sqrt(IMG_MODEL)
        return {'q': jax.random.normal(ks[0], (B, LQ, D_MODEL), jnp.float32), 'k': jax.random.normal(ks[1], (B, LKV, IMG_MODEL), jnp.float32), 'v': jax.random.normal(ks[2], (B, LKV, IMG_MODEL), jnp.float32), 'Wq': jax.random.normal(ks[3], (D_MODEL, D_MODEL), jnp.float32) * s_dm, 'bq': jnp.zeros((D_MODEL,), jnp.float32), 'Wk': jax.random.normal(ks[4], (IMG_MODEL, D_MODEL), jnp.float32) * s_im, 'bk': jnp.zeros((D_MODEL,), jnp.float32), 'Wv': jax.random.normal(ks[5], (IMG_MODEL, D_MODEL), jnp.float32) * s_im, 'bv': jnp.zeros((D_MODEL,), jnp.float32), 'Wo': jax.random.normal(ks[6], (D_MODEL, D_MODEL), jnp.float32) * s_dm, 'bo': jnp.zeros((D_MODEL,), jnp.float32)}
    _L0_xattn_all = _L0_xattn_setup()
    _L0_xattn_in = {k: v for k, v in _L0_xattn_all.items() if k in ('Wq', 'bq', 'Wk', 'bk', 'Wv', 'bv', 'Wo', 'bo')}
    del _L0_xattn_all

    def _L0_attn_setup():
        import math
        import jax, jax.numpy as jnp
        import numpy as np
        from jax.scipy.special import logsumexp
        B, L, D_MODEL = (2, 256, 256)
        H = 16
        DH = D_MODEL // H
        M = 24
        WINDOW = 128
        MASK_VAL = -10000.0
        EPS = 0.0001
        SCALE = 1.0 / math.sqrt(DH)

        def _sb_features(x, proj, is_query):
            xh = x * math.sqrt(SCALE)
            x_dash = jnp.einsum('bhld,md->bhlm', xh, proj)
            diag = 0.5 * jnp.sum(xh * xh, axis=-1, keepdims=True)
            log_feat = x_dash - diag
            if is_query:
                stab = jax.lax.stop_gradient(jnp.max(log_feat, axis=-1, keepdims=True))
            else:
                stab = jax.lax.stop_gradient(jnp.max(log_feat, axis=(-2, -1), keepdims=True))
            prime = jnp.exp(log_feat - stab) + EPS
            return (prime, stab)

        def _local_mask(L):
            i = jnp.arange(L)[:, None]
            j = jnp.arange(L)[None, :]
            keep = (j <= i) & (j >= i - WINDOW)
            return jnp.where(keep, 0.0, MASK_VAL).astype(jnp.float32)
        if __name__ == '__main__':
            o = reference(**setup_inputs())
            print(o.shape, o.dtype)
        key = jax.random.key(seed)
        ks = jax.random.split(key, 4)
        x = jax.random.normal(ks[0], (B, L, D_MODEL), dtype=jnp.float32)
        Wqkv_w = jax.random.normal(ks[1], (3 * D_MODEL, D_MODEL), dtype=jnp.float32) * D_MODEL ** (-0.5)
        Wqkv_b = jnp.zeros((3 * D_MODEL,), dtype=jnp.float32)
        proj = jax.random.normal(ks[2], (M, DH), dtype=jnp.float32)
        out_w = jax.random.normal(ks[3], (D_MODEL, D_MODEL), dtype=jnp.float32) * D_MODEL ** (-0.5)
        out_b = jnp.zeros((D_MODEL,), dtype=jnp.float32)
        return {'x': x, 'Wqkv_w': Wqkv_w, 'Wqkv_b': Wqkv_b, 'proj': proj, 'out_w': out_w, 'out_b': out_b}
    _L0_attn_all = _L0_attn_setup()
    _L0_attn_in = {k: v for k, v in _L0_attn_all.items() if k in ('Wqkv_w', 'Wqkv_b', 'proj', 'out_w', 'out_b')}
    del _L0_attn_all

    def _L0_ffn_setup():
        import jax, jax.numpy as jnp
        import numpy as np
        D_MODEL = 256
        N_HEADS = 16
        N_KV = 4
        NUM_REP = N_HEADS // N_KV
        HEAD_DIM = D_MODEL // N_HEADS
        N_EXPERTS = 8
        TOP_K = 2
        CAP_FACTOR = 1.25
        EPS_NORM = 1e-06

        def _rmsnorm(x, w):
            var = jnp.mean(x * x, axis=-1, keepdims=True)
            return w * (x * jax.lax.rsqrt(var + EPS_NORM))

        def _gqa(x, qw, qb, kw, kb, vw, vb, ow, ob):
            B, S, D = x.shape
            q = (x @ qw + qb).reshape(B, S, N_HEADS, HEAD_DIM).transpose(0, 2, 1, 3)
            k = (x @ kw + kb).reshape(B, S, N_KV, HEAD_DIM).transpose(0, 2, 1, 3)
            v = (x @ vw + vb).reshape(B, S, N_KV, HEAD_DIM).transpose(0, 2, 1, 3)
            k = jnp.repeat(k, NUM_REP, axis=1)
            v = jnp.repeat(v, NUM_REP, axis=1)
            scores = jnp.einsum('bhqd,bhkd->bhqk', q, k) / np.sqrt(HEAD_DIM).astype(np.float32)
            attn = jax.nn.softmax(scores, axis=-1)
            out = jnp.einsum('bhqk,bhkd->bhqd', attn, v)
            out = out.transpose(0, 2, 1, 3).reshape(B, S, D)
            return out @ ow + ob

        def _moe(x, gate_w, w1, w2):
            B, S, D = x.shape
            T = B * S
            x_flat = x.reshape(T, D)
            capacity = int(CAP_FACTOR * T * TOP_K / N_EXPERTS)
            logits = x_flat @ gate_w
            probs = jax.nn.sigmoid(logits)
            _, sel = jax.lax.top_k(probs, TOP_K)
            w_topk = jnp.take_along_axis(probs, sel, axis=1)
            w_topk = w_topk / (jnp.sum(w_topk, axis=-1, keepdims=True) + 1e-06)
            flat_sel = sel.reshape(-1)
            em = jax.nn.one_hot(flat_sel, N_EXPERTS, dtype=jnp.int32)
            ranks = jnp.take_along_axis(jnp.cumsum(em, axis=0), flat_sel[:, None], axis=1)[:, 0] - 1
            valid = ranks < capacity
            slot = flat_sel * capacity + ranks
            scatter_idx = jnp.where(valid, slot, N_EXPERTS * capacity)
            x_rep = jnp.repeat(x_flat, TOP_K, axis=0)
            padded = jnp.zeros((N_EXPERTS * capacity + 1, D), x.dtype).at[scatter_idx].set(x_rep)
            padded_x = padded[:N_EXPERTS * capacity].reshape(N_EXPERTS, capacity, D)
            h = jax.nn.gelu(jnp.einsum('ecd,edf->ecf', padded_x, w1), approximate=False)
            out_padded = jnp.einsum('ecf,efd->ecd', h, w2).reshape(N_EXPERTS * capacity, D)
            gather_idx = jnp.where(valid, slot, 0)
            out_rep = jnp.where(valid[:, None], out_padded[gather_idx], 0.0)
            out_w = out_rep * w_topk.reshape(-1)[:, None]
            return out_w.reshape(T, TOP_K, D).sum(axis=1).reshape(B, S, D)
        key = jax.random.key(seed)
        ks = jax.random.split(key, 12)
        s = 0.02
        return {'x': jax.random.normal(ks[0], (4, 256, D_MODEL), jnp.float32), 'qw': jax.random.normal(ks[1], (D_MODEL, D_MODEL), jnp.float32) * s, 'qb': jnp.zeros((D_MODEL,), jnp.float32), 'kw': jax.random.normal(ks[2], (D_MODEL, N_KV * HEAD_DIM), jnp.float32) * s, 'kb': jnp.zeros((N_KV * HEAD_DIM,), jnp.float32), 'vw': jax.random.normal(ks[3], (D_MODEL, N_KV * HEAD_DIM), jnp.float32) * s, 'vb': jnp.zeros((N_KV * HEAD_DIM,), jnp.float32), 'ow': jax.random.normal(ks[4], (D_MODEL, D_MODEL), jnp.float32) * s, 'ob': jnp.zeros((D_MODEL,), jnp.float32), 'gate_w': jax.random.normal(ks[5], (D_MODEL, N_EXPERTS), jnp.float32) * s, 'w1': jax.random.normal(ks[6], (N_EXPERTS, D_MODEL, 512), jnp.float32) * s, 'w2': jax.random.normal(ks[7], (N_EXPERTS, 512, D_MODEL), jnp.float32) * s, 'norm1_w': jnp.ones((D_MODEL,), jnp.float32), 'norm2_w': jnp.ones((D_MODEL,), jnp.float32)}
    _L0_ffn_all = _L0_ffn_setup()
    _L0_ffn_in = {k: v for k, v in _L0_ffn_all.items() if k in ('qw', 'qb', 'kw', 'kb', 'vw', 'vb', 'ow', 'ob', 'gate_w', 'w1', 'w2', 'norm1_w', 'norm2_w')}
    del _L0_ffn_all
    return {'x': x, 'ctx_512': ctx_512, 'L0_xattn_Wq': _L0_xattn_in['Wq'], 'L0_xattn_bq': _L0_xattn_in['bq'], 'L0_xattn_Wk': _L0_xattn_in['Wk'], 'L0_xattn_bk': _L0_xattn_in['bk'], 'L0_xattn_Wv': _L0_xattn_in['Wv'], 'L0_xattn_bv': _L0_xattn_in['bv'], 'L0_xattn_Wo': _L0_xattn_in['Wo'], 'L0_xattn_bo': _L0_xattn_in['bo'], 'L0_attn_Wqkv_w': _L0_attn_in['Wqkv_w'], 'L0_attn_Wqkv_b': _L0_attn_in['Wqkv_b'], 'L0_attn_proj': _L0_attn_in['proj'], 'L0_attn_out_w': _L0_attn_in['out_w'], 'L0_attn_out_b': _L0_attn_in['out_b'], 'L0_ffn_qw': _L0_ffn_in['qw'], 'L0_ffn_qb': _L0_ffn_in['qb'], 'L0_ffn_kw': _L0_ffn_in['kw'], 'L0_ffn_kb': _L0_ffn_in['kb'], 'L0_ffn_vw': _L0_ffn_in['vw'], 'L0_ffn_vb': _L0_ffn_in['vb'], 'L0_ffn_ow': _L0_ffn_in['ow'], 'L0_ffn_ob': _L0_ffn_in['ob'], 'L0_ffn_gate_w': _L0_ffn_in['gate_w'], 'L0_ffn_w1': _L0_ffn_in['w1'], 'L0_ffn_w2': _L0_ffn_in['w2'], 'L0_ffn_norm1_w': _L0_ffn_in['norm1_w'], 'L0_ffn_norm2_w': _L0_ffn_in['norm2_w']}

def reference(x, ctx_512, L0_xattn_Wq, L0_xattn_bq, L0_xattn_Wk, L0_xattn_bk, L0_xattn_Wv, L0_xattn_bv, L0_xattn_Wo, L0_xattn_bo, L0_attn_Wqkv_w, L0_attn_Wqkv_b, L0_attn_proj, L0_attn_out_w, L0_attn_out_b, L0_ffn_qw, L0_ffn_qb, L0_ffn_kw, L0_ffn_kb, L0_ffn_vw, L0_ffn_vb, L0_ffn_ow, L0_ffn_ob, L0_ffn_gate_w, L0_ffn_w1, L0_ffn_w2, L0_ffn_norm1_w, L0_ffn_norm2_w):
    import jax
    import jax.numpy as jnp

    def _L0_xattn_ref(q, k, v, Wq, bq, Wk, bk, Wv, bv, Wo, bo):
        import jax, jax.numpy as jnp
        import numpy as np
        HEADS = 16
        D_MODEL = 256
        IMG_MODEL = 128
        D_K = D_MODEL // HEADS
        B, LQ, _ = q.shape
        LKV = k.shape[1]
        qh = (q @ Wq + bq).reshape(B, LQ, HEADS, D_K).transpose(0, 2, 1, 3)
        kh = (k @ Wk + bk).reshape(B, LKV, HEADS, D_K).transpose(0, 2, 1, 3)
        vh = (v @ Wv + bv).reshape(B, LKV, HEADS, D_K).transpose(0, 2, 1, 3)
        scale = 1.0 / np.sqrt(D_K)
        scores = jnp.einsum('bhqd,bhkd->bhqk', qh, kh) * scale
        attn = jax.nn.softmax(scores, axis=-1)
        out = jnp.einsum('bhqk,bhkd->bhqd', attn, vh)
        concat = out.transpose(0, 2, 1, 3).reshape(B, LQ, D_MODEL)
        return concat @ Wo + bo

    def _L0_attn_ref(x, Wqkv_w, Wqkv_b, proj, out_w, out_b):
        import math
        import jax, jax.numpy as jnp
        import numpy as np
        from jax.scipy.special import logsumexp
        B, L, D_MODEL = (2, 256, 256)
        H = 16
        DH = D_MODEL // H
        M = 24
        WINDOW = 128
        MASK_VAL = -10000.0
        EPS = 0.0001
        SCALE = 1.0 / math.sqrt(DH)

        def _sb_features(x, proj, is_query):
            xh = x * math.sqrt(SCALE)
            x_dash = jnp.einsum('bhld,md->bhlm', xh, proj)
            diag = 0.5 * jnp.sum(xh * xh, axis=-1, keepdims=True)
            log_feat = x_dash - diag
            if is_query:
                stab = jax.lax.stop_gradient(jnp.max(log_feat, axis=-1, keepdims=True))
            else:
                stab = jax.lax.stop_gradient(jnp.max(log_feat, axis=(-2, -1), keepdims=True))
            prime = jnp.exp(log_feat - stab) + EPS
            return (prime, stab)

        def _local_mask(L):
            i = jnp.arange(L)[:, None]
            j = jnp.arange(L)[None, :]
            keep = (j <= i) & (j >= i - WINDOW)
            return jnp.where(keep, 0.0, MASK_VAL).astype(jnp.float32)
        if __name__ == '__main__':
            o = reference(**setup_inputs())
            print(o.shape, o.dtype)
        b, l, dm = x.shape
        qkv = (x @ Wqkv_w.T + Wqkv_b).reshape(b, l, 3, H, DH)
        q = jnp.transpose(qkv[:, :, 0], (0, 2, 1, 3))
        k = jnp.transpose(qkv[:, :, 1], (0, 2, 1, 3))
        v = jnp.transpose(qkv[:, :, 2], (0, 2, 1, 3))
        q_prime, q_ls = _sb_features(q, proj, is_query=True)
        k_prime, k_ls = _sb_features(k, proj, is_query=False)
        global_scale = q_ls + k_ls
        global_out_cumsum = jnp.einsum('bhnm,bhnm->bhn', q_prime, jnp.cumsum(k_prime, axis=-2))
        kv = jnp.cumsum(k_prime[..., :, :, None] * v[..., :, None, :], axis=-3)
        global_out = jnp.einsum('bhlm,bhlmd->bhld', q_prime, kv)
        mask = _local_mask(l)
        g_scores = jnp.einsum('bhmd,bhnd->bhmn', q_prime, k_prime) * SCALE + mask
        global_qk = jnp.where(g_scores <= 0, 0.0, g_scores)
        l_scores = jnp.einsum('bhmd,bhnd->bhmn', q, k) * SCALE + mask
        QK_lse = logsumexp(l_scores, axis=-1, keepdims=True)
        gqk_sum = jnp.sum(global_qk, axis=-1, keepdims=True)
        g_log_norm = jnp.log(jnp.clip(global_out_cumsum[..., None] - gqk_sum, 1e-24)) + global_scale
        log_norm = jnp.logaddexp(QK_lse, g_log_norm)
        g_prime_scale = jnp.exp(global_scale - log_norm)
        local_score = jax.nn.softmax(l_scores - log_norm, axis=-1) - global_qk * g_prime_scale
        out = jnp.einsum('bhmn,bhnd->bhmd', local_score, v) + global_out * g_prime_scale
        ctx = jnp.transpose(out, (0, 2, 1, 3)).reshape(b, l, dm)
        return ctx @ out_w.T + out_b

    def _L0_ffn_ref(x, qw, qb, kw, kb, vw, vb, ow, ob, gate_w, w1, w2, norm1_w, norm2_w):
        import jax, jax.numpy as jnp
        import numpy as np
        D_MODEL = 256
        N_HEADS = 16
        N_KV = 4
        NUM_REP = N_HEADS // N_KV
        HEAD_DIM = D_MODEL // N_HEADS
        N_EXPERTS = 8
        TOP_K = 2
        CAP_FACTOR = 1.25
        EPS_NORM = 1e-06

        def _rmsnorm(x, w):
            var = jnp.mean(x * x, axis=-1, keepdims=True)
            return w * (x * jax.lax.rsqrt(var + EPS_NORM))

        def _gqa(x, qw, qb, kw, kb, vw, vb, ow, ob):
            B, S, D = x.shape
            q = (x @ qw + qb).reshape(B, S, N_HEADS, HEAD_DIM).transpose(0, 2, 1, 3)
            k = (x @ kw + kb).reshape(B, S, N_KV, HEAD_DIM).transpose(0, 2, 1, 3)
            v = (x @ vw + vb).reshape(B, S, N_KV, HEAD_DIM).transpose(0, 2, 1, 3)
            k = jnp.repeat(k, NUM_REP, axis=1)
            v = jnp.repeat(v, NUM_REP, axis=1)
            scores = jnp.einsum('bhqd,bhkd->bhqk', q, k) / np.sqrt(HEAD_DIM).astype(np.float32)
            attn = jax.nn.softmax(scores, axis=-1)
            out = jnp.einsum('bhqk,bhkd->bhqd', attn, v)
            out = out.transpose(0, 2, 1, 3).reshape(B, S, D)
            return out @ ow + ob

        def _moe(x, gate_w, w1, w2):
            B, S, D = x.shape
            T = B * S
            x_flat = x.reshape(T, D)
            capacity = int(CAP_FACTOR * T * TOP_K / N_EXPERTS)
            logits = x_flat @ gate_w
            probs = jax.nn.sigmoid(logits)
            _, sel = jax.lax.top_k(probs, TOP_K)
            w_topk = jnp.take_along_axis(probs, sel, axis=1)
            w_topk = w_topk / (jnp.sum(w_topk, axis=-1, keepdims=True) + 1e-06)
            flat_sel = sel.reshape(-1)
            em = jax.nn.one_hot(flat_sel, N_EXPERTS, dtype=jnp.int32)
            ranks = jnp.take_along_axis(jnp.cumsum(em, axis=0), flat_sel[:, None], axis=1)[:, 0] - 1
            valid = ranks < capacity
            slot = flat_sel * capacity + ranks
            scatter_idx = jnp.where(valid, slot, N_EXPERTS * capacity)
            x_rep = jnp.repeat(x_flat, TOP_K, axis=0)
            padded = jnp.zeros((N_EXPERTS * capacity + 1, D), x.dtype).at[scatter_idx].set(x_rep)
            padded_x = padded[:N_EXPERTS * capacity].reshape(N_EXPERTS, capacity, D)
            h = jax.nn.gelu(jnp.einsum('ecd,edf->ecf', padded_x, w1), approximate=False)
            out_padded = jnp.einsum('ecf,efd->ecd', h, w2).reshape(N_EXPERTS * capacity, D)
            gather_idx = jnp.where(valid, slot, 0)
            out_rep = jnp.where(valid[:, None], out_padded[gather_idx], 0.0)
            out_w = out_rep * w_topk.reshape(-1)[:, None]
            return out_w.reshape(T, TOP_K, D).sum(axis=1).reshape(B, S, D)
        src = x + _gqa(x, qw, qb, kw, kb, vw, vb, ow, ob)
        src = _rmsnorm(src, norm1_w)
        src = src + _moe(src, gate_w, w1, w2)
        return _rmsnorm(src, norm2_w)
    x = x + _L0_xattn_ref(_layernorm(x, axis=-1), ctx_512, ctx_512, L0_xattn_Wq, L0_xattn_bq, L0_xattn_Wk, L0_xattn_bk, L0_xattn_Wv, L0_xattn_bv, L0_xattn_Wo, L0_xattn_bo)
    x = x + _L0_attn_ref(_layernorm(x, axis=-1), L0_attn_Wqkv_w, L0_attn_Wqkv_b, L0_attn_proj, L0_attn_out_w, L0_attn_out_b)
    x = x + _L0_ffn_ref(_layernorm(x, axis=-1), L0_ffn_qw, L0_ffn_qb, L0_ffn_kw, L0_ffn_kb, L0_ffn_vw, L0_ffn_vb, L0_ffn_ow, L0_ffn_ob, L0_ffn_gate_w, L0_ffn_w1, L0_ffn_w2, L0_ffn_norm1_w, L0_ffn_norm2_w)
    return x

_drawn_inputs = setup_inputs


def setup_inputs(seed=0):
    import zlib

    import numpy as np

    out = dict(_drawn_inputs(seed))
    spreads = {'L0_xattn_bq': (0.0, 0.272),
     'L0_xattn_bk': (0.0, 0.8),
     'L0_xattn_bv': (0.0, 0.1),
     'L0_xattn_bo': (0.0, 0.1),
     'L0_attn_Wqkv_b': (0.0, 0.1),
     'L0_attn_out_b': (0.0, 0.1),
     'L0_ffn_qb': (0.0, 0.8),
     'L0_ffn_kb': (0.0, 0.8),
     'L0_ffn_vb': (0.0, 0.647),
     'L0_ffn_ob': (0.0, 0.1),
     'L0_ffn_norm1_w': (1.0, 0.2),
     'L0_ffn_norm2_w': (1.0, 0.2)}
    factors = {'L0_ffn_qw': 8.0,
     'L0_ffn_kw': 8.0,
     'L0_ffn_gate_w': 3.049,
     'L0_ffn_w1': 2.814,
     'L0_ffn_w2': 2.738}
    for name, (base, spread) in spreads.items():
        noise = np.random.default_rng([zlib.crc32(name.encode()), seed]).standard_normal(out[name].shape)
        drawn = base * np.exp(spread * noise) if base else spread * noise
        out[name] = jnp.asarray(drawn.astype(out[name].dtype))
    for name, factor in factors.items():
        out[name] = (out[name] * factor).astype(out[name].dtype)
    return out
```

```python
from contextlib import ExitStack

import concourse.bass as bass
from concourse import mybir

F32 = mybir.dt.float32
BF16 = mybir.dt.bfloat16
F16 = mybir.dt.float16
ALU = mybir.AluOpType
ACT = mybir.ActivationFunctionType
AX = mybir.AxisListType

P = 128
B, L, D = 2, 256, 256
H, DH = 16, 16
NK, DC = 4096, 128
RT = B * L // P
KT = D // P
GH = 4
NG = B * H // GH
M = 24
E, FF, CAP = 8, 512, 160
TPB = NK // P
VW = DH + 1
SCALE = 0.25

QSLOT = "hmhmlh"
KSLOT = "hhmmhl"
NS = len(QSLOT)
SROWS = NS * DH
MROWS = SROWS + 3

LEAD = 5
SPG = TPB
UPG = 64
S0 = -(SPG + LEAD) - 12
SEND = NG * SPG


def aux_of(s):
    out = []
    if s < 0:
        if 0 <= s - S0 < 8:
            out.append(("K", s - S0))
        if s - S0 >= 12 and (s - S0 - 12) % 3 == 0 and (s - S0 - 12) // 3 < 8:
            out.append(("V", (s - S0 - 12) // 3))
    elif s < 64 * 3 + 34 + 8:
        v, r = divmod(s - 38, 4)
        if r == 0 and v >= 0 and v % 16 < 8 and v // 16 < 3:
            out.append(("V", 8 * (v // 16 + 1) + v % 16))
        c, r = divmod(s - 4, 4)
        if r == 0 and c >= 0 and c % 16 < 8 and c // 16 < 3:
            out.append(("K", 8 * (c // 16 + 1) + c % 16))
    for g in range(NG):
        if s == SPG * (g - 1) - LEAD - 2:
            out.append(("QS", g))
        if s == SPG * g - 3:
            out.append(("QT", g))
        if s == SPG * (g + 1) + 4:
            out.append(("OT", g))
    return out


AUX = [(s, kind, i) for s in range(S0, SEND + 8) for kind, i in aux_of(s)]
AUX_NO = {(kind, i): n for n, (s, kind, i) in enumerate(AUX)}
assert len(AUX_NO) == 32 + 32 + 3 * NG


def units_of(s):
    first = UPG + 2 * (s + LEAD)
    return range(max(first, 0), max(min(first + 2, UPG * NG), 0))


def build(nc, t_in, out, stop=None):
    with ExitStack() as ctx:
        def sb(name, shape, dt=F32):
            return ctx.enter_context(nc.sbuf_tensor(name, shape, dt))

        def sem(name):
            return ctx.enter_context(nc.semaphore(name))

        ps = ctx.enter_context(nc.psum_tensor("ps", [P, 8, 512], F32))

        identf = sb("identf", [P, P])
        identb = sb("identb", [P, P], BF16)
        onesf = sb("onesf", [P, P])
        X = sb("X", [P, RT, D])
        lnx = sb("lnx", [P, RT, D])
        lnT = sb("lnT", [P, KT, B * L])
        bst = sb("bst", [P, RT, 6])
        mv = sb("mv", [P, RT, 2])
        ve = sb("ve", [P, RT])
        sd = sb("sd", [P, RT])
        rs = sb("rs", [P, RT])

        wq = sb("wq", [P, KT, D])
        wo = sb("wo", [P, KT, D])
        wk = sb("wk", [P, D])
        wv = sb("wv", [P, D])
        bqr = sb("bqr", [1, D])
        bor = sb("bor", [1, D])
        bkc = sb("bkc", [P, 2])
        bvb = sb("bvb", [P, D])
        big = sb("big", [P, 2, GH, NK], BF16)
        stack = big
        ctxn = stack[:, 1, :, :].rearrange("p j n -> p (j n)").bitcast(F32).rearrange(
            "p (b t c) -> p b t c", b=B, c=DC)
        ctxT = sb("ctxT", [P, B, NK])
        kpt = sb("kpt", [P, 3, NK], BF16)
        kh, km, kl = kpt[:, 0, :], kpt[:, 1, :], kpt[:, 2, :]
        kparts = {"h": kh, "m": km, "l": kl}
        kr = sb("kr", [P, 2, 512])
        Vg = sb("Vg", [P, 2, TPB * GH * VW + 32 - VW])
        PT = sb("PT", [P, 3, GH * L])
        qf = lnx
        qpt = sb("qpt", [P, 3, RT, D], BF16)
        qh, qm, ql = qpt[:, 0], qpt[:, 1], qpt[:, 2]
        qparts = {"h": qh, "m": qm, "l": ql}
        Qg = sb("Qg", [P, 2, 2 * GH, P], BF16)
        QS = sb("QS", [P, 2, 2 * GH * P], BF16)
        QT = sb("QT", [P, 2, 2 * GH * P], BF16)
        mx = sb("mx", [P, 2, 2 * GH, 8])
        nm = sb("nm", [P, 2 * GH])
        nr = sb("nr", [P, 2 * GH])
        OTs = sb("OTs", [P, L])
        rec = sb("rec", [P, 2, GH])
        att = sb("att", [P, RT, D])

        ST = [ps[:, 0:2, :], ps[:, 2:4, :]]
        SM = [ps[:, 4, :], ps[:, 5, :]]
        ACC = ps[:, 6, :]
        AUXB = ps[:, 7, :]

        s_x = sem("s_x")
        s_w1 = sem("s_w1")
        s_ctx = [sem(f"s_ctx{i}") for i in range(8)]
        s_const = sem("s_const")
        s_pool = sem("s_pool")
        s_dve = sem("s_dve")
        s_act = sem("s_act")
        s_var = sem("s_var")
        s_std = sem("s_std")
        s_ln = sem("s_ln")
        s_lnT = sem("s_lnT")
        s_lnTc = sem("s_lnTc")
        s_q = sem("s_q")
        s_qf = sem("s_qf")
        s_qp = sem("s_qp")
        s_ct = sem("s_ct")
        s_ctc = [sem("s_ctc_act"), sem("s_ctc_dve")]
        s_stack = [[sem(f"s_stack{p}{h}") for h in range(2)] for p in range(2)]
        s_ones = sem("s_ones")
        s_sm = sem("s_sm")
        s_red = sem("s_red")
        s_st = sem("s_st")
        s_exp = sem("s_exp")
        s_pv = sem("s_pv")
        s_acc = sem("s_acc")
        s_aux = sem("s_aux")
        s_auxd = sem("s_auxd")
        s_khd = sem("s_khd")
        s_kl = sem("s_kl")
        s_qg = sem("s_qg")
        s_mp = sem("s_mp")
        s_out = sem("s_out")

        count = {"dve": 0, "act": 0, "pool": 0}

        def link_dve(ins):
            count["dve"] += 1
            ins.then_inc(s_dve, 1)
            nc.vector.wait_ge(s_dve, count["dve"])

        def link_act(ins):
            count["act"] += 1
            ins.then_inc(s_act, 1)
            nc.scalar.wait_ge(s_act, count["act"])

        def link_pool(ins):
            count["pool"] += 1
            ins.then_inc(s_pool, 1)
            nc.gpsimd.wait_ge(s_pool, count["pool"])

        xin = t_in["x"].rearrange("b (r p) d -> p (b r) d", p=P)
        cin = t_in["ctx_512"].rearrange("b (p t) c -> p b t c", p=P)

        def view(tensor_words, at, shape, dt=F32):
            n = 1
            for x in shape[1:]:
                n *= x
            words = n if dt == F32 else n // 2
            v = tensor_words[:, at:at + words]
            if dt != F32:
                v = v.bitcast(dt)
            if len(shape) == 2:
                return v
            names = "abcd"[:len(shape) - 1]
            return v.rearrange(f"p ({' '.join(names)}) -> p {' '.join(names)}",
                               **{c: x for c, x in zip(names, shape[1:])})

        bigw = big.rearrange("p a j n -> p (a j n)").bitcast(F32)
        ctxw = ctxT.rearrange("p b n -> p (b n)")
        kw_ = kpt.rearrange("p a n -> p (a n)").bitcast(F32)
        vgw = Vg.rearrange("p g n -> p (g n)")
        ptw = PT.rearrange("p a n -> p (a n)")
        QN = view(bigw, 0, [P, RT, H, P], BF16)
        KN = view(bigw, 4096, [P, RT, H, P], BF16)
        FQ = view(bigw, 8192, [P, RT, H, P], BF16)
        FK = view(bigw, 12288, [P, RT, H, P], BF16)
        wqkvT = view(bigw, 12288, [P, KT, 3 * D])
        w1 = view(ctxw, 0, [P, E, KT, FF])
        w2 = view(bigw, 8192, [P, E, FF // P, D])
        QK = view(kw_, 0, [P, RT, 2 * D])
        fq = view(kw_, 2048, [P, RT, H, M])
        fk = view(kw_, 3584, [P, RT, H, M])
        FKL = view(kw_, 5120, [P, RT, H, M], BF16)
        PG = view(kw_, 0, [P, 2, GH * L])
        As = view(kw_, 2048, [P, RT, H, VW])
        Gs = view(kw_, 3136, [P, RT, H, VW])
        xT = view(vgw, 0, [P, 2, KT, B * L])
        xsq = view(vgw, 2048, [P, 2, KT, B * L])
        KSg = view(vgw, 0, [P, 2, 2 * GH * P], BF16)
        FQT = view(vgw, 1024, [P, 2, 2 * GH * P], BF16)
        FKT = view(vgw, 2048, [P, 2, 2 * GH * P], BF16)
        FKLT = view(vgw, 3072, [P, 2, 2 * GH * P], BF16)
        V2 = view(qpt.rearrange("p a r d -> p (a r d)").bitcast(F32), 0, [P, RT, H * VW + 32 - VW])
        hT = view(kw_, 0, [P, 2, FF // P, B * L])
        acc = view(ptw, 0, [P, RT, D])
        krw = kr.rearrange("p a n -> p (a n)")
        wraw = view(bigw, 0, [P, 8, D])
        woT2 = view(ptw, 2048, [P, KT, D])
        projb = view(ptw, 1024, [P, 2, 8 * M])
        OTg = view(ptw, 2560, [P, L])
        wn1 = view(ptw, 1024, [P, D])
        wn2 = view(ptw, 1280, [P, D])
        gate = view(ptw, 1536, [P, KT, E])
        lowb = view(ptw, 1600, [P, 2, P], BF16)
        maskq = view(krw, 0, [P, 2, L], F16)
        maskk = view(krw, 256, [P, 2, L], F16)
        wmask = view(krw, 512, [P, 2, L])
        small = Qg.rearrange("p a r n -> p (a r n)").bitcast(F32)
        identh = sb("identh", [P, P], F16)
        rows = sb("rows", [1, 6 * D + 128])

        CB = [ps[:, i, :] for i in range(4)]
        NCT = B * TPB // 4
        LB = [ps[:, 4 + i, :] for i in range(2)]
        QB = [ps[:, 6 + i, 0:256] for i in range(2)]
        with nc.Block() as block:
            @block.sync
            def _(sp):
                sp.dma_start(X[:, :, :], xin).then_inc(s_x, 16)
                for i in range(8):
                    b, q = divmod(i, 4)
                    sp.dma_start(ctxn[:, b, 8 * q:8 * q + 8, :], cin[:, b, 8 * q:8 * q + 8, :]).then_inc(s_ctx[i], 16)

            @block.gpsimd
            def _(pool):
                pool.memset(onesf[:, :], 1.0).then_inc(s_const, 1)
                link_pool(pool.memset(identf[:, :], 0.0))
                link_pool(pool.affine_select(out=identf[:, :], in_=identf[:, :], compare_op=ALU.not_equal, fill=1.0,
                                             base=0, pattern=[[-1, P]], channel_multiplier=1))
                pool.tensor_copy(identb[:, :], identf[:, :]).then_inc(s_const, 1)
                pool.memset(Qg[:, :, :, :], 0.0).then_inc(s_const, 1)
                pool.memset(Vg[:, :, :], 1.0).then_inc(s_const, 1)
                pool.wait_ge(s_const, 4)
                pool.memset(stack[SROWS:MROWS, 0, :, :], 1.0).then_inc(s_ones, 1)

            @block.scalar
            def _(act):
                act.dma_start(wq[:, :, :], t_in["L0_xattn_Wq"].rearrange("(k p) n -> p k n", p=P)).then_inc(s_w1, 16)
                act.dma_start(bqr[:, :], t_in["L0_xattn_bq"].rearrange("(a n) -> a n", a=1)).then_inc(s_w1, 16)
                act.dma_start(wk[:, :], t_in["L0_xattn_Wk"]).then_inc(s_w1, 16)
                act.dma_start(bkc[:, :], t_in["L0_xattn_bk"].rearrange("(k p) -> p k", p=P),
                              allow_slow_non_contiguous=True).then_inc(s_w1, 16)
                act.dma_start(wv[:, :], t_in["L0_xattn_Wv"]).then_inc(s_w1, 16)
                act.dma_start(bvb[:, :], t_in["L0_xattn_bv"].partition_broadcast(P)).then_inc(s_w1, 16)
                act.dma_start(wo[:, :, :], t_in["L0_xattn_Wo"].rearrange("(k p) n -> p k n", p=P)).then_inc(s_w1, 16)
                act.dma_start(bor[:, :], t_in["L0_xattn_bo"].rearrange("(a n) -> a n", a=1)).then_inc(s_w1, 16)
                act.wait_ge(s_var, 1)
                act.activation(sd[:, :], ve[:, :], ACT.Sqrt).then_inc(s_std, 1)
                for k in range(KT):
                    act.wait_ge(s_lnT, k + 1)
                    act.activation(lnT[:, k, :], LB[k], ACT.Copy).then_inc(s_lnTc, 1)
                for R in range(RT):
                    act.wait_ge(s_q, R + 1)
                    act.activation(qf[:, R, :], QB[R % 2], ACT.Copy).then_inc(s_qf, 1)
                for n in range(0, NCT, 2):
                    act.wait_ge(s_ct, n + 1)
                    b, c = divmod(n, NCT // B)
                    act.activation(ctxT[:, b, 512 * c:512 * c + 512], CB[n % 4], ACT.Copy).then_inc(s_ctc[0], 1)

            @block.vector
            def _(dve):
                dve.wait_ge(s_x, 16)
                for R in range(RT):
                    link_dve(dve.bn_stats(bst[:, R, :], X[:, R, :]))
                    link_dve(dve.bn_aggr(mv[:, R, :], bst[:, R, :]))
                dve.tensor_scalar(ve[:, :], mv[:, :, 1], 1e-5, None, ALU.add).then_inc(s_var, 1)
                dve.wait_ge(s_std, 1)
                link_dve(dve.reciprocal(rs[:, :], sd[:, :]))
                for R in range(RT):
                    dve.tensor_scalar(lnx[:, R, :], X[:, R, :], mv[:, R, 0:1], rs[:, R:R + 1],
                                      ALU.subtract, ALU.mult).then_inc(s_ln, 1)
                for R in range(RT):
                    dve.wait_ge(s_qf, R + 1)
                    link_dve(dve.tensor_copy(qh[:, R, :], qf[:, R, :]))
                    link_dve(dve.tensor_tensor(qf[:, R, :], qf[:, R, :], qh[:, R, :], ALU.subtract))
                    link_dve(dve.tensor_copy(qm[:, R, :], qf[:, R, :]))
                    dve.tensor_tensor(ql[:, R, :], qf[:, R, :], qm[:, R, :], ALU.subtract).then_inc(s_qp, 1)
                for n in range(1, NCT, 2):
                    dve.wait_ge(s_ct, n + 1)
                    b, c = divmod(n, NCT // B)
                    dve.tensor_copy(ctxT[:, b, 512 * c:512 * c + 512], CB[n % 4]).then_inc(s_ctc[1], 1)

            @block.tensor
            def _(pe):
                pe.wait_ge(s_const, 2)
                pe.wait_ge(s_ln, RT)
                for k in range(KT):
                    for R in range(RT):
                        mm = pe.transpose(LB[k][:, P * R:P * R + P], lnx[:, R, P * k:P * k + P], identf[:, :])
                    mm.then_inc(s_lnT, 1)
                pe.wait_ge(s_w1, 128)
                pe.wait_ge(s_lnTc, KT)
                for R in range(RT):
                    if R >= 2:
                        pe.wait_ge(s_qf, R - 1)
                    for k in range(KT):
                        pe.matmul(QB[R % 2], lnT[:, k, P * R:P * R + P], wq[:, k, :], start=(k == 0), stop=False)
                    pe.matmul(QB[R % 2], onesf[0:1, :], bqr[:, :], start=False, stop=True).then_inc(s_q, 1)
                for n in range(NCT):
                    if n % 2 == 0:
                        pe.wait_ge(s_ctx[n // 2], 16)
                    if n >= 4:
                        pe.wait_ge(s_ctc[n % 2], (n - 4) // 2 + 1)
                    b, c = divmod(n, NCT // B)
                    for i in range(4):
                        mm = pe.transpose(CB[n % 4][:, P * i:P * i + P], ctxn[:, b, 4 * c + i, :], identf[:, :])
                    mm.then_inc(s_ct, 1)

        with nc.Block() as block:
            @block.sync
            def _(sp):
                for g in range(NG):
                    for half in range(2):
                        sp.wait_ge(s_kl, 8 * (g // 2) + 4 * half + 4)
                        if g >= 2:
                            sp.wait_ge(s_st, SPG * (g - 2) + 16 * (half + 1))
                        for j in range(GH):
                            r = 64 * (g % 2) + DH * j
                            for n in range(NS):
                                sp.dma_start(stack[DH * n:DH * n + DH, g % 2, j, 2048 * half:2048 * half + 2048],
                                             kparts[KSLOT[n]][r:r + DH, 2048 * half:2048 * half + 2048])\
                                  .then_inc(s_stack[g % 2][half], 16)

            @block.gpsimd
            def _(pool):
                pool.memset(stack[SROWS:MROWS, 1, :, :], 1.0).then_inc(s_ones, 1)
                pool.wait_ge(s_ones, 2)
                for s in range(S0, SEND):
                    for kind, i in aux_of(s):
                        if kind == "K":
                            c = i % 8
                            pool.wait_ge(s_auxd, AUX_NO[kind, i] + 1)
                            sl = slice(512 * c, 512 * c + 512)
                            if i >= 8:
                                for par in range(2):
                                    pool.wait_ge(s_stack[par][c // 4], 384 * (i // 8))
                            link_pool(pool.tensor_copy(km[:, sl], kr[:, i % 2, :]))
                            pool.tensor_tensor(kl[:, sl], kr[:, i % 2, :], km[:, sl], ALU.subtract).then_inc(s_kl, 1)
                    for g in range(NG):
                        if s == max(SPG * (g - 1) - LEAD - 6, S0):
                            b, hg = divmod(g, 4)
                            if g >= 2:
                                pool.wait_ge(s_auxd, AUX_NO["QT", g - 2] + 1)
                            for n in range(NS):
                                o = Qg[:, g % 2, :, DH * n:DH * n + DH].rearrange("p (j q) d -> p q j d", q=2)
                                src = qparts[QSLOT[n]][:, 2 * b:2 * b + 2, 64 * hg:64 * hg + 64].rearrange(
                                    "p q (j d) -> p q j d", d=DH)
                                for q in range(2):
                                    ins = pool.tensor_copy(o[:, q], src[:, q])
                            ins.then_inc(s_qg, 1)

            @block.scalar
            def _(act):
                for s in range(S0, SEND + 8):
                    if 0 <= s < SEND:
                        act.wait_ge(s_st, s + 1)
                        if s >= 3:
                            act.wait_ge(s_pv, s - 2)
                        act.activation(PT[:, s % 3, :], ST[s % 2], ACT.Exp, scale=SCALE).then_inc(s_exp, 1)
                    if s > SPG and s % SPG == 1:
                        g = s // SPG - 1
                        act.wait_ge(s_pv, SPG * (g + 1))
                        if g >= 1:
                            act.wait_ge(s_auxd, AUX_NO["OT", g - 1] + 1)
                        act.activation(OTs[:, :], ACC[:, 0:L], ACT.Copy).then_inc(s_acc, 1)
                    for kind, i in aux_of(s):
                        if kind == "K":
                            half, c = (i // 8) % 2, i % 8
                            act.wait_ge(s_aux, AUX_NO[kind, i] + 1)
                            if i >= 8:
                                for par in range(2):
                                    act.wait_ge(s_stack[par][c // 4], 384 * (i // 8))
                            act.activation(kh[:, 512 * c:512 * c + 512], AUXB, ACT.Identity,
                                           bias=bkc[:, half:half + 1]).then_inc(s_khd, 1)
                        if kind == "V":
                            hf, v = divmod(i, 8)
                            act.wait_ge(s_aux, AUX_NO[kind, i] + 1)
                            for gg in range(2):
                                if hf >= 1:
                                    act.wait_ge(s_pv, SPG * (2 * hf - 2 + gg) + 4 * v + 4)
                                o = Vg[:, gg, 4 * v * GH * VW:(4 * v + 4) * GH * VW].rearrange(
                                    "p (t j d) -> p t j d", t=4, d=VW)
                                src = AUXB.rearrange("p (t g j d) -> p t g j d", t=4, g=2, d=DH)
                                ins = act.activation(o[:, :, :, 0:DH], src[:, :, gg], ACT.Copy)
                            ins.then_inc(s_auxd, 1)

            @block.vector
            def _(dve):
                for s in range(S0, SEND + 8):
                    for n in units_of(s):
                        g, u = divmod(n, UPG)
                        dve.wait_ge(s_sm, n + 1)
                        dve.tensor_reduce(mx[:, g % 2, u % 8, u // 8:u // 8 + 1], SM[n % 2], AX.X,
                                          ALU.max).then_inc(s_red, 1)
                        if u == UPG - 1:
                            dve.wait_ge(s_red, n + 1)
                            q = Qg[:, g % 2, :, :]
                            link_dve(dve.tensor_reduce(nm[:, :], mx[:, g % 2, :, :], AX.X, ALU.max, negate=True))
                            link_dve(dve.tensor_copy(q[:, :, SROWS], nm[:, :]))
                            link_dve(dve.tensor_tensor(nr[:, :], nm[:, :], q[:, :, SROWS], ALU.subtract))
                            link_dve(dve.tensor_copy(q[:, :, SROWS + 1], nr[:, :]))
                            dve.tensor_tensor(q[:, :, SROWS + 2], nr[:, :], q[:, :, SROWS + 1],
                                              ALU.subtract).then_inc(s_mp, 1)
                    for kind, i in aux_of(s):
                        a = AUX_NO[kind, i]
                        if kind == "K":
                            dve.wait_ge(s_khd, i + 1)
                            if i >= 2:
                                dve.wait_ge(s_kl, i - 1)
                            half, c = (i // 8) % 2, i % 8
                            dve.scalar_tensor_tensor(out=kr[:, i % 2, :], in0=AUXB, scalar=bkc[:, half:half + 1],
                                                     in1=kh[:, 512 * c:512 * c + 512], op0=ALU.add,
                                                     op1=ALU.subtract).then_inc(s_auxd, 1)
                        if kind in ("QS", "QT"):
                            dve.wait_ge(s_aux, a + 1)
                            dve.tensor_copy((QS if kind == "QS" else QT)[:, i % 2, :],
                                            AUXB.bitcast(BF16)).then_inc(s_auxd, 1)
                        if kind == "OT":
                            b, hg = divmod(i, 4)
                            dve.wait_ge(s_aux, a + 1)
                            o = AUXB[:, 0:2 * P].rearrange("p (q j d) -> p q j d", q=2, d=32)
                            link_dve(dve.reciprocal(rec[:, :, :], o[:, :, :, DH]))
                            dst = att[:, 2 * b:2 * b + 2, 64 * hg:64 * hg + 64].rearrange("p q (j d) -> p q j d", d=DH)
                            for q in range(2):
                                ins = dve.tensor_tensor(dst[:, q], o[:, q, :, 0:DH],
                                                        rec[:, q, :].unsqueeze(2).broadcast_to([P, GH, DH]), ALU.mult)
                            ins.then_inc(s_auxd, 1)

            @block.tensor
            def _(pe):
                pe.wait_ge(s_ones, 1)
                for s in range(S0, SEND + 8):
                    if 0 <= s < SEND:
                        g, t = divmod(s, SPG)
                        if s >= 2:
                            pe.wait_ge(s_exp, s - 1)
                        if t == 0:
                            pe.wait_ge(s_auxd, AUX_NO["QT", g] + 1)
                        for j in range(GH):
                            mm = pe.matmul(ST[s % 2][:, j // 2, 256 * (j % 2):256 * (j % 2) + 256],
                                           stack[0:MROWS, g % 2, j, P * t:P * t + P],
                                           QT[0:MROWS, g % 2, L * j:L * j + L], start=True, stop=True)
                        mm.then_inc(s_st, 1)
                    if 2 <= s < SEND + 2:
                        g, t = divmod(s - 2, SPG)
                        pe.wait_ge(s_exp, s - 1)
                        if t == 0 and g >= 1:
                            pe.wait_ge(s_acc, g)
                        if t % 4 == 0:
                            pe.wait_ge(s_auxd, AUX_NO["V", 8 * (g // 2) + t // 4] + 1)
                        for j in range(GH):
                            v0 = (GH * t + j) * VW
                            mm = pe.matmul(ACC[32 * j:32 * j + 32, 0:L], Vg[:, g % 2, v0:v0 + 32],
                                           PT[:, (s - 2) % 3, L * j:L * j + L], start=(t == 0), stop=(t == SPG - 1))
                        mm.then_inc(s_pv, 1)
                    for n in units_of(s):
                        g, u = divmod(n, UPG)
                        c, r = divmod(u, 8)
                        if u == 0:
                            pe.wait_ge(s_auxd, AUX_NO["QS", g] + 1)
                            pe.wait_ge(s_ones, min(g + 1, 2))
                        if u % 32 == 0:
                            pe.wait_ge(s_stack[g % 2][u // 32], 384 * (g // 2 + 1))
                        if n >= 2:
                            pe.wait_ge(s_red, n - 1)
                        pe.matmul(SM[n % 2], QS[0:SROWS, g % 2, P * r:P * r + P],
                                  stack[0:SROWS, g % 2, r // 2, 512 * c:512 * c + 512],
                                  start=True, stop=True).then_inc(s_sm, 1)
                    for kind, i in aux_of(s):
                        a = AUX_NO[kind, i]
                        if a:
                            pe.wait_ge(s_auxd, a)
                        if kind == "K":
                            b, half = divmod(i // 8, 2)
                            c = i % 8
                            mm = pe.matmul(AUXB, wk[:, P * half:P * half + P], ctxT[:, b, 512 * c:512 * c + 512],
                                           start=True, stop=True)
                        if kind == "V":
                            b, half = divmod(i // 8, 2)
                            for q in range(4):
                                t = 4 * (i % 8) + q
                                mm = pe.matmul(AUXB[:, P * q:P * q + P], ctxT[:, b, P * t:P * t + P],
                                               wv[:, P * half:P * half + P], start=True, stop=True)
                        if kind in ("QS", "QT"):
                            pe.wait_ge(s_qg if kind == "QS" else s_mp, i + 1)
                            for r in range(2 * GH):
                                mm = pe.transpose(AUXB.bitcast(BF16)[:, P * r:P * r + P], Qg[:, i % 2, r, :],
                                                  identb[:, :])
                        if kind == "OT":
                            pe.wait_ge(s_acc, i + 1)
                            for q in range(2):
                                mm = pe.transpose(AUXB[:, P * q:P * q + P], OTs[:, P * q:P * q + P], identf[:, :])
                        mm.then_inc(s_aux, 1)

        def store_x(src):
            with nc.Block() as block:
                @block.sync
                def _(sp):
                    sp.dma_start(out.rearrange("b (r p) d -> p (b r) d", p=P), src).then_inc(s_out, 16)
                    sp.wait_ge(s_out, 16)
                    if stop in ("x1", "x2"):
                        sp.wait_ge(s_wl3, 128 if stop == "x2" else 112)
                        sp.wait_ge(s_wl4, 128)

        if stop == "att":
            return store_x(att[:, :, :])

        bqkv = rows[:, 0:3 * D]
        b_out2 = rows[:, 3 * D:4 * D]
        b_q3 = rows[:, 4 * D:5 * D]
        b_o3 = rows[:, 5 * D:6 * D]

        qls = small[:, 0:64].rearrange("p (r h) -> p r h", h=H)
        mkx = small[:, 64:128]
        kls = small[:, 128:160].rearrange("p (b h) -> p b h", h=H)
        nmall = small[:, 160:224].rearrange("p (r h) -> p r h", h=H)
        t0 = small[:, 224:288].rearrange("p (r h) -> p r h", h=H)
        t1 = small[:, 288:352].rearrange("p (r h) -> p r h", h=H)
        t2 = small[:, 352:416].rearrange("p (r h) -> p r h", h=H)
        t3 = small[:, 416:480].rearrange("p (r h) -> p r h", h=H)
        mkc = small[0:64, 480:481]
        mkr = small[0:1, 484:516]
        nrs = small[:, 516:524].rearrange("p (q j) -> p q j", j=GH)
        bkv = rows[:, 6 * D:6 * D + 128]

        s_wl = sem("s_wl")
        s_wp = sem("s_wp")
        s_wl3 = sem("s_wl3")
        s_wl4 = sem("s_wl4")
        s_wT = sem("s_wT")
        s_wTc = sem("s_wTc")
        s_cst2 = sem("s_cst2")
        s_attb = sem("s_attb")
        s_aT = sem("s_aT")
        s_aTc = sem("s_aTc")
        s_op = sem("s_op")
        s_xn = sem("s_xn")
        s_qkv = sem("s_qkv")
        s_qkvc = sem("s_qkvc")
        s_xt = sem("s_xt")
        s_xtc = sem("s_xtc")
        s_sq = sem("s_sq")
        s_f = sem("s_f")
        s_fr = sem("s_fr")
        s_fs = sem("s_fs")
        s_fe = sem("s_fe")
        s_mk = sem("s_mk")
        s_mkT = sem("s_mkT")
        s_mkc = sem("s_mkc")
        s_p = sem("s_p")
        s_ph = sem("s_ph")
        s_pc = sem("s_pc")
        s_b = sem("s_b")

        PB = [ps[:, i, 0:D] for i in (0, 1, 6, 7)]

        def ln_dve(dve, n, eps):
            for R in range(RT):
                link_dve(dve.bn_stats(bst[:, R, :], X[:, R, :]))
                link_dve(dve.bn_aggr(mv[:, R, :], bst[:, R, :]))
            dve.tensor_scalar(ve[:, :], mv[:, :, 1], eps, None, ALU.add).then_inc(s_var, 1)
            dve.wait_ge(s_std, n + 1)
            link_dve(dve.reciprocal(rs[:, :], sd[:, :]))
            for R in range(RT):
                dve.tensor_scalar(lnx[:, R, :], X[:, R, :], mv[:, R, 0:1], rs[:, R:R + 1],
                                  ALU.subtract, ALU.mult).then_inc(s_ln, 1)

        def ln_act(act, n):
            act.wait_ge(s_var, n + 1)
            act.activation(sd[:, :], ve[:, :], ACT.Sqrt).then_inc(s_std, 1)

        def rows_T_pe(pe, n, src):
            for k in range(KT):
                for R in range(RT):
                    mm = pe.transpose(LB[k][:, P * R:P * R + P], src[:, R, P * k:P * k + P], identf[:, :])
                mm.then_inc(s_lnT, 1)

        def rows_T_act(act, n):
            for k in range(KT):
                act.wait_ge(s_lnT, KT * n + k + 1)
                act.activation(lnT[:, k, :], LB[k], ACT.Copy).then_inc(s_lnTc, 1)

        def project_pe(pe, n, w, brow):
            for R in range(RT):
                o = PB[R]
                for k in range(KT):
                    pe.matmul(o, lnT[:, k, P * R:P * R + P], w[:, k, :], start=(k == 0), stop=False)
                pe.matmul(o, onesf[0:1, :], brow, start=False, stop=True).then_inc(s_op, 1)

        def residual_dve(dve, n):
            for R in range(RT):
                dve.wait_ge(s_op, RT * n + R + 1)
                link_dve(dve.tensor_tensor(X[:, R, :], X[:, R, :], PB[R],
                                           ALU.add))

        WB = [ps[:, 2, :], ps[:, 3, :]]
        with nc.Block() as block:
            @block.sync
            def _(sp):
                sp.dma_start(wraw[:, 0:6, :], t_in["L0_attn_Wqkv_w"].rearrange("(w p) k -> p w k", p=P)).then_inc(s_wl, 16)
                sp.dma_start(wraw[:, 6:8, :], t_in["L0_attn_out_w"].rearrange("(w p) k -> p w k", p=P)).then_inc(s_wl, 16)
                sp.dma_start(bqkv, t_in["L0_attn_Wqkv_b"].rearrange("(a n) -> a n", a=1)).then_inc(s_wl, 16)
                sp.dma_start(b_out2, t_in["L0_attn_out_b"].rearrange("(a n) -> a n", a=1)).then_inc(s_wl, 16)
                sp.dma_start(b_q3, t_in["L0_ffn_qb"].rearrange("(a n) -> a n", a=1)).then_inc(s_wl3, 16)
                sp.dma_start(b_o3, t_in["L0_ffn_ob"].rearrange("(a n) -> a n", a=1)).then_inc(s_wl3, 16)
                sp.dma_start(bkv[:, 0:64], t_in["L0_ffn_kb"].rearrange("(a n) -> a n", a=1)).then_inc(s_wl3, 16)
                sp.dma_start(bkv[:, 64:128], t_in["L0_ffn_vb"].rearrange("(a n) -> a n", a=1)).then_inc(s_wl3, 16)
                sp.dma_start(wq[:, :, :], t_in["L0_ffn_qw"].rearrange("(k p) n -> p k n", p=P)).then_inc(s_wl3, 16)
                kvw = t_in["L0_ffn_kw"].rearrange("(k p) n -> p k n", p=P)
                sp.dma_start(wk.rearrange("p (k n) -> p k n", k=4)[:, 0:2, :], kvw).then_inc(s_wl3, 16)
                sp.dma_start(wk.rearrange("p (k n) -> p k n", k=4)[:, 2:4, :],
                             t_in["L0_ffn_vw"].rearrange("(k p) n -> p k n", p=P)).then_inc(s_wl3, 16)
                for e in range(E):
                    sp.dma_start(w1[:, e, :, :], t_in["L0_ffn_w1"][e].rearrange("(k p) f -> p k f", p=P)).then_inc(s_wl4, 16)
                sp.wait_ge(s_cst2, 1)
                for j in range(8):
                    sp.dma_start(projb[DH * j:DH * j + DH, 0, M * j:M * j + M],
                                 t_in["L0_attn_proj"].rearrange("m d -> d m"),
                                 allow_slow_non_contiguous=True).then_inc(s_wp, 16)

            @block.gpsimd
            def _(pool):
                pool.memset(projb[:, :, :], 0.0).then_inc(s_cst2, 1)
                pool.memset(V2[:, :, :], 1.0).then_inc(s_b, 1)
                pool.wait_ge(s_cst2, 1)
                link_pool(pool.memset(projb[:, 1, :], -0.125))
                dg = projb[:, 1, :].rearrange("p (j m) -> p j m", m=M)
                link_pool(pool.affine_select(out=dg, in_=dg, compare_op=ALU.is_ge, fill=0.0, base=0,
                                             pattern=[[-DH, 8], [0, M]], channel_multiplier=1))
                pool.affine_select(out=dg, in_=dg, compare_op=ALU.is_ge, fill=0.0, base=DH - 1,
                                   pattern=[[DH, 8], [0, M]], channel_multiplier=-1).then_inc(s_cst2, 1)
                link_pool(pool.memset(maskq[:, :, :], 0.0))
                link_pool(pool.memset(maskk[:, :, :], 0.0))
                link_pool(pool.memset(wmask[:, :, :], 1.0))
                link_pool(pool.affine_select(out=maskq[:, :, :], in_=maskq[:, :, :], compare_op=ALU.is_ge,
                                             fill=-40000.0, base=0, pattern=[[P, 2], [-1, L]], channel_multiplier=1))
                link_pool(pool.affine_select(out=maskk[:, :, :], in_=maskk[:, :, :], compare_op=ALU.is_ge,
                                             fill=-40000.0, base=0, pattern=[[-P, 2], [1, L]], channel_multiplier=-1))
                link_pool(pool.affine_select(out=wmask[:, :, :], in_=wmask[:, :, :], compare_op=ALU.is_ge,
                                             fill=0.0, base=0, pattern=[[-P, 2], [1, L]], channel_multiplier=-1))
                link_pool(pool.affine_select(out=maskq[:, :, :], in_=maskq[:, :, :], compare_op=ALU.is_ge,
                                             fill=-40000.0, base=128, pattern=[[-P, 2], [1, L]],
                                             channel_multiplier=-1))
                link_pool(pool.affine_select(out=maskk[:, :, :], in_=maskk[:, :, :], compare_op=ALU.is_ge,
                                             fill=-40000.0, base=128, pattern=[[P, 2], [-1, L]],
                                             channel_multiplier=1))
                pool.tensor_copy(identh[:, :], identf[:, :]).then_inc(s_cst2, 1)
                pool.wait_ge(s_wT, 8)
                pool.memset(QN[:, :, :, SROWS:P], 0.0).then_inc(s_b, 1)
                pool.memset(KN[:, :, :, SROWS:P], 1.0).then_inc(s_b, 1)
                def slot(T, n, w=DH):
                    return T[:, :, :, w * n:w * n + w]
                pool.wait_ge(s_ph, 1)
                for n in (2, 5):
                    for R in range(RT):
                        pool.tensor_copy(slot(QN, n)[:, R], slot(QN, 0)[:, R]).then_inc(s_pc, 1)
                pool.wait_ge(s_ph, 2)
                for n in (1, 4):
                    for R in range(RT):
                        pool.tensor_copy(slot(KN, n)[:, R], slot(KN, 0)[:, R]).then_inc(s_pc, 1)
                pool.wait_ge(s_p, 2)
                for R in range(RT):
                    pool.tensor_copy(slot(QN, 3)[:, R], slot(QN, 1)[:, R]).then_inc(s_pc, 1)
                    pool.tensor_copy(slot(KN, 3)[:, R], slot(KN, 2)[:, R]).then_inc(s_pc, 1)
                pool.wait_ge(s_qkv, 2 * RT)
                pool.memset(FQ[:, :, :, 5 * M:P], 0.0).then_inc(s_b, 1)
                pool.memset(FK[:, :, :, 5 * M:P], 0.0).then_inc(s_b, 1)
                pool.wait_ge(s_p, 3)
                for R in range(RT):
                    pool.tensor_copy(slot(FQ, 2, M)[:, R], slot(FQ, 0, M)[:, R]).then_inc(s_pc, 1)
                    pool.tensor_copy(slot(FQ, 3, M)[:, R], slot(FQ, 1, M)[:, R]).then_inc(s_pc, 1)
                pool.wait_ge(s_p, 4)
                for R in range(RT):
                    pool.tensor_copy(slot(FK, 1, M)[:, R], slot(FK, 0, M)[:, R]).then_inc(s_pc, 1)
                    pool.tensor_copy(slot(FK, 4, M)[:, R], slot(FK, 0, M)[:, R]).then_inc(s_pc, 1)
                    pool.tensor_copy(slot(FK, 3, M)[:, R], slot(FK, 2, M)[:, R]).then_inc(s_pc, 1)

            @block.scalar
            def _(act):
                rows_T_act(act, 1)
                for w in range(8):
                    act.wait_ge(s_wT, w + 1)
                    o = wqkvT[:, :, P * w:P * w + P] if w < 6 else woT2[:, :, P * (w - 6):P * (w - 6) + P]
                    act.activation(o, WB[w % 2][:, 0:2 * P].rearrange("p (k n) -> p k n", k=KT), ACT.Copy).then_inc(s_wTc, 1)
                ln_act(act, 1)
                rows_T_act(act, 2)
                for R in range(RT):
                    act.wait_ge(s_qkv, 2 * R + 1)
                    act.activation(QK[:, R, :], ps[:, 2 * (R % 2), :], ACT.Copy).then_inc(s_qkvc, 1)
                    act.wait_ge(s_qkv, 2 * R + 2)
                    if R == 0:
                        act.wait_ge(s_b, 1)
                    act.activation(V2[:, R, 0:H * VW].rearrange("p (h d) -> p h d", d=VW)[:, :, 0:DH],
                                   ps[:, 2 * (R % 2) + 1, 0:D].rearrange("p (h d) -> p h d", d=DH),
                                   ACT.Copy).then_inc(s_qkvc, 1)
                act.wait_ge(s_qkvc, 2 * RT)
                for side, T in enumerate((QN, KN)):
                    act.activation(T[:, :, :, 0:DH], QK[:, :, D * side:D * side + D].rearrange(
                        "p r (h d) -> p r h d", d=DH), ACT.Copy).then_inc(s_ph, 1)
                for n in range(4):
                    side, k = divmod(n, KT)
                    act.wait_ge(s_xt, n + 1)
                    act.activation(xsq[:, side, k, :], ps[:, 4 + n, :], ACT.Square).then_inc(s_sq, 1)
                for side, f in enumerate((fq, fk)):
                    act.wait_ge(s_fs, side + 1)
                    act.activation(f[:, :, :, :], f[:, :, :, :], ACT.Exp).then_inc(s_fe, 1)

            @block.vector
            def _(dve):
                dve.wait_ge(s_w1, 128)
                for R in range(RT):
                    ins = dve.tensor_tensor(att[:, R, :], att[:, R, :], bvb[:, :], ALU.add)
                ins.then_inc(s_attb, 1)
                residual_dve(dve, 0)
                ln_dve(dve, 1, 1e-5)
                dve.wait_ge(s_cst2, 3)
                sc = acc[:, 0:2, :]
                link_dve(dve.tensor_scalar(sc, maskk[:, :, :], 0.0, 0.25, ALU.is_equal, ALU.mult))
                link_dve(dve.tensor_tensor(wmask[:, :, :], wmask[:, :, :], sc, ALU.subtract))
                for n in range(4):
                    side, k = divmod(n, KT)
                    dve.wait_ge(s_sq, n + 1)
                    dve.tensor_scalar(xT[:, side, k, :], ps[:, 4 + n, :], 0.5, None, ALU.mult).then_inc(s_xtc, 1)
                for side, f in enumerate((fq, fk)):
                    for R in range(RT):
                        pf = ps[:, R, 0:H * M].rearrange("p (h m) -> p h m", m=M)
                        dve.wait_ge(s_f, RT * side + R + 1)
                        if side == 0:
                            link_dve(dve.tensor_reduce(qls[:, R, :], pf, AX.X, ALU.max))
                            ins = dve.tensor_tensor(f[:, R, :, :], pf,
                                                    qls[:, R, :].unsqueeze(2).broadcast_to([P, H, M]), ALU.subtract)
                            ins.then_inc(s_fr, 1)
                        else:
                            dve.tensor_reduce(mkx[:, H * R:H * R + H], pf, AX.X, ALU.max).then_inc(s_mk, 1)
                    if side == 0:
                        dve.wait_ge(s_fr, RT)
                        dve.sem_inc(s_fs, 1)
                dve.wait_ge(s_mkT, 1)
                dve.tensor_reduce(mkc, ps[0:64, 4, 0:P], AX.X, ALU.max).then_inc(s_mkc, 1)
                dve.wait_ge(s_mkT, 2)
                dve.tensor_reduce(mkr.rearrange("p (b h) -> p b h", b=B),
                                  ps[0:1, 5, 0:64].rearrange("p (b q h) -> p b h q", b=B, q=2),
                                  AX.X, ALU.max).then_inc(s_mkc, 1)
                dve.wait_ge(s_mkT, 3)
                link_dve(dve.tensor_copy(kls, ps[:, 6, 0:32].rearrange("p (b h) -> p b h", b=B)))
                for R in range(RT):
                    pf = ps[:, R, 0:H * M].rearrange("p (h m) -> p h m", m=M)
                    ins = dve.tensor_tensor(fk[:, R, :, :], pf,
                                            kls[:, R // 2, :].unsqueeze(2).broadcast_to([P, H, M]), ALU.subtract)
                    link_dve(ins)
                dve.sem_inc(s_fs, 1)
                for side, (T, sm_, sl_) in enumerate(((QN, 1, 4), (KN, 2, 5))):
                    dve.wait_ge(s_ph, side + 1)
                    q = QK[:, :, D * side:D * side + D].rearrange("p r (h d) -> p r h d", d=DH)
                    for R in range(RT):
                        link_dve(dve.tensor_tensor(q[:, R], q[:, R], T[:, R, :, 0:DH], ALU.subtract))
                        link_dve(dve.tensor_copy(T[:, R, :, DH * sm_:DH * sm_ + DH], q[:, R]))
                        ins = dve.tensor_tensor(T[:, R, :, DH * sl_:DH * sl_ + DH], q[:, R],
                                                T[:, R, :, DH * sm_:DH * sm_ + DH], ALU.subtract)
                        if R < RT - 1:
                            link_dve(ins)
                    ins.then_inc(s_p, 1)
                dve.wait_ge(s_qkv, 2 * RT)
                dve.wait_ge(s_b, 5)
                for side, (f, T, h_, m_, l_) in enumerate(((fq, FQ, 0, 1, None), (fk, FK, 0, 2, None))):
                    dve.wait_ge(s_fe, side + 1)
                    link_dve(dve.tensor_scalar(f[:, :, :, :], f[:, :, :, :], 1e-4, None, ALU.add))
                    for R in range(RT):
                        link_dve(dve.tensor_copy(T[:, R, :, 0:M], f[:, R]))
                        link_dve(dve.tensor_tensor(f[:, R], f[:, R], T[:, R, :, 0:M], ALU.subtract))
                        link_dve(dve.tensor_copy(T[:, R, :, M * m_:M * m_ + M], f[:, R]))
                        lo = T[:, R, :, 4 * M:5 * M] if side == 0 else FKL[:, R]
                        ins = dve.tensor_tensor(lo, f[:, R], T[:, R, :, M * m_:M * m_ + M], ALU.subtract)
                        if R < RT - 1:
                            link_dve(ins)
                    ins.then_inc(s_p, 1)

            @block.tensor
            def _(pe):
                pe.wait_ge(s_attb, 1)
                rows_T_pe(pe, 1, att)
                pe.wait_ge(s_lnTc, 2 * KT)
                project_pe(pe, 0, wo, bor[:, :])
                pe.wait_ge(s_wl, 64)
                for w in range(8):
                    if w >= 2:
                        pe.wait_ge(s_wTc, w - 1)
                    for k in range(KT):
                        mm = pe.transpose(WB[w % 2][:, P * k:P * k + P], wraw[:, w, P * k:P * k + P], identf[:, :])
                    mm.then_inc(s_wT, 1)
                pe.wait_ge(s_ln, 2 * RT)
                rows_T_pe(pe, 2, lnx)
                pe.wait_ge(s_lnTc, 3 * KT)
                pe.wait_ge(s_wp, 16 * 8)
                pe.wait_ge(s_wTc, 8)
                for R in range(RT):
                    if R >= 2:
                        pe.wait_ge(s_qkvc, 2 * R - 2)
                    for part, (lo, hi) in enumerate(((0, 2 * D), (2 * D, 3 * D))):
                        o = ps[:, 2 * (R % 2) + part, 0:hi - lo]
                        for k in range(KT):
                            pe.matmul(o, lnT[:, k, P * R:P * R + P], wqkvT[:, k, lo:hi], start=(k == 0), stop=False)
                        pe.matmul(o, onesf[0:1, :], bqkv[:, lo:hi], start=False, stop=True).then_inc(s_qkv, 1)
                pe.wait_ge(s_qkvc, 2 * RT)
                for n in range(4):
                    side, k = divmod(n, KT)
                    for R in range(RT):
                        mm = pe.transpose(ps[:, 4 + n, P * R:P * R + P],
                                          QK[:, R, D * side + P * k:D * side + P * k + P], identf[:, :])
                    mm.then_inc(s_xt, 1)
                pe.wait_ge(s_xtc, 4)
                pe.wait_ge(s_sq, 4)
                pe.wait_ge(s_cst2, 2)
                for side in range(2):
                    for R in range(RT):
                        if side == 1:
                            pe.wait_ge(s_fr, R + 1)
                        for k in range(KT):
                            o = ps[:, R, 8 * M * k:8 * M * k + 8 * M]
                            pe.matmul(o, xT[:, side, k, P * R:P * R + P], projb[:, 0, :], start=True, stop=False)
                            mm = pe.matmul(o, xsq[:, side, k, P * R:P * R + P], projb[:, 1, :],
                                           start=False, stop=True)
                        mm.then_inc(s_f, 1)
                pe.wait_ge(s_mk, RT)
                pe.transpose(ps[0:64, 4, 0:P], mkx, identf[:, :]).then_inc(s_mkT, 1)
                pe.wait_ge(s_mkc, 1)
                pe.transpose(ps[0:1, 5, 0:64], mkc, identf[0:64, 0:64]).then_inc(s_mkT, 1)
                pe.wait_ge(s_mkc, 2)
                pe.matmul(ps[:, 6, 0:32], onesf[0:1, :], mkr, start=True, stop=True).then_inc(s_mkT, 1)

        if stop == "x1":
            return store_x(X[:, :, :])

        ts = {n: sem(n) for n in ("a_t", "a_td_act", "a_td_dve", "a_s", "a_sr", "a_mp", "a_st", "a_exp", "a_gm",
                                  "a_pv", "a_acc", "a_ot")}
        base = {n: 0 for n in ts}

        def attention(masked):
            uses = []
            for i in range(NG + 1):
                if i < NG:
                    uses += [("Q", i, "dve"), ("K", i, "act")]
                    if masked:
                        uses += [("FQ", i, "act"), ("FK", i, "dve"), ("FKL", i, "act")]
                if i >= 1:
                    uses += [("QT", i - 1, "dve"), ("O", i - 1, "dve")]
                    if masked:
                        uses += [("OG", i - 1, "dve")]
            use_no = {u[:2]: n for n, u in enumerate(uses)}

            def read(n):
                who = uses[n][2]
                return ts["a_td_" + who], base["a_td_" + who] + sum(u[2] == who for u in uses[:n + 1])

            def bank(n):
                return ps[:, n % 2, :]

            b0 = dict(base)
            NKJ = GH if masked else 1
            PTn = PT[:, 0:2, :]
            src = {"Q": QN, "K": KN, "FQ": FQ, "FK": FK}
            dst = {"Q": QS, "QT": QT, "K": KSg, "FQ": FQT, "FK": FKT, "FKL": FKLT}

            def sg_order(i):
                out = []
                if i < NG:
                    out += [("S", i, 0), ("S", i, 1)]
                if masked and i >= 1:
                    out += [("G", i - 1, 0), ("G", i - 1, 1)]
                return out
            sg = [u for i in range(NG + 1) for u in sg_order(i)]
            sg_no = {u: n for n, u in enumerate(sg)}

            with nc.Block() as block:
                if masked:
                    @block.sync
                    def _(sp):
                        sp.dma_start(wo[:, :, :], t_in["L0_ffn_ow"].rearrange("(k p) n -> p k n", p=P)).then_inc(s_wl3, 16)
                else:
                    @block.sync
                    def _(sp):
                        for e in range(E):
                            sp.dma_start(w2[:, e, :, :], t_in["L0_ffn_w2"][e].rearrange("(k p) f -> p k f", p=P))\
                              .then_inc(s_wl4, 16)

                @block.tensor
                def _(pe):
                    def rows_T(kind, g):
                        n = use_no[kind, g]
                        if n >= 2:
                            pe.wait_ge(*read(n - 2))
                        b, hg = divmod(g, 4)
                        o = bank(n).bitcast(BF16)
                        if kind == "QT":
                            pe.wait_ge(ts["a_mp"], b0["a_mp"] + g + 1)
                        for j in range(NKJ if kind == "K" else GH):
                            for q in range(2):
                                r = 2 * j + q
                                h = 4 * hg + j
                                if kind == "K" and not masked:
                                    h = hg
                                if kind == "FKL":
                                    mm = pe.transpose(o[0:M, P * r:P * r + P], FKL[:, 2 * b + q, h, :], identb[:, :])
                                else:
                                    T = QN if kind == "QT" else src[kind]
                                    mm = pe.transpose(o[:, P * r:P * r + P], T[:, 2 * b + q, h, :], identb[:, :])
                        mm.then_inc(ts["a_t"], 1)

                    def sg_bank(u):
                        n = sg_no[u]
                        if n >= 1:
                            pe.wait_ge(ts["a_sr"], b0["a_sr"] + n)
                        return ps[:, 2:4, :]

                    for i in range(NG + 1):
                        if i < NG:
                            rows_T("Q", i)
                            rows_T("K", i)
                            if masked:
                                rows_T("FQ", i)
                                rows_T("FK", i)
                                rows_T("FKL", i)
                            for q in range(2):
                                o = sg_bank(("S", i, q))
                                if q == 0:
                                    pe.wait_ge(*read(use_no["Q", i]))
                                    pe.wait_ge(*read(use_no["K", i]))
                                for a in range(2):
                                    if masked:
                                        pe.matmul(o[:, a, :], identh[:, :],
                                                  maskq[:, q, :].unsqueeze(1).broadcast_to([P, 2, L]),
                                                  start=True, stop=False, skip_group_check=True)
                                    for jj in range(2):
                                        j = 2 * a + jj
                                        jk = j if masked else 0
                                        mm = pe.matmul(o[:, a, L * jj:L * jj + L],
                                                       QS[0:SROWS, i % 2, P * (2 * j + q):P * (2 * j + q) + P],
                                                       KSg[0:SROWS, i % 2, L * jk:L * jk + L],
                                                       start=not masked, stop=True, skip_group_check=True)
                                mm.then_inc(ts["a_s"], 1)
                        if i >= 1:
                            g = i - 1
                            b, hg = divmod(g, 4)
                            rows_T("QT", g)
                            pe.wait_ge(*read(use_no["QT", g]))
                            for k in range(2):
                                n = 2 * g + k
                                if n >= 1:
                                    pe.wait_ge(ts["a_exp"], b0["a_exp"] + n)
                                for a in range(2):
                                    o = ps[:, 4 + a, :]
                                    if masked:
                                        pe.matmul(o, identh[:, :],
                                                  maskk[:, k, :].unsqueeze(1).broadcast_to([P, 2, L]),
                                                  start=True, stop=False, skip_group_check=True)
                                    for jj in range(2):
                                        j = 2 * a + jj
                                        jk = j if masked else 0
                                        mm = pe.matmul(o[:, L * jj:L * jj + L],
                                                       KSg[0:MROWS, g % 2, P * (2 * jk + k):P * (2 * jk + k) + P],
                                                       QT[0:MROWS, g % 2, L * j:L * j + L],
                                                       start=not masked, stop=True, skip_group_check=True)
                                mm.then_inc(ts["a_st"], 1)
                                if masked:
                                    o = sg_bank(("G", g, k))
                                    if k == 0:
                                        for kind in ("FQ", "FK", "FKL"):
                                            pe.wait_ge(*read(use_no[kind, g]))
                                    for j in range(GH):
                                        oj = o[:, j // 2, L * (j % 2):L * (j % 2) + L]
                                        r = P * (2 * j + k)
                                        pe.matmul(oj, FKT[0:5 * M, g % 2, r:r + P], FQT[0:5 * M, g % 2, L * j:L * j + L],
                                                  start=True, stop=False)
                                        mm = pe.matmul(oj, FKLT[0:M, g % 2, r:r + P], FQT[0:M, g % 2, L * j:L * j + L],
                                                       start=False, stop=True)
                                    mm.then_inc(ts["a_s"], 1)
                            if g >= 1:
                                pe.wait_ge(ts["a_acc"], b0["a_acc"] + (2 if masked else 1) * g)
                            for k in range(2):
                                n = 2 * g + k
                                for part in range(2 if masked else 1):
                                    if part == 0:
                                        pe.wait_ge(ts["a_exp"], b0["a_exp"] + n + 1)
                                    else:
                                        pe.wait_ge(ts["a_gm"], b0["a_gm"] + n + 1)
                                    for j in range(GH):
                                        h = 4 * hg + j if masked else hg
                                        mm = pe.matmul(ps[32 * j:32 * j + 32, 6 + part, 0:L],
                                                       V2[:, 2 * b + k, VW * h:VW * h + 32],
                                                       (PG if part else PTn)[:, k, L * j:L * j + L],
                                                       start=(k == 0), stop=(k == 1))
                                    mm.then_inc(ts["a_pv"], 1)
                            for kind in ("O", "OG") if masked else ("O",):
                                n = use_no[kind, g]
                                pe.wait_ge(*read(n - 2))
                                pe.wait_ge(ts["a_acc"], b0["a_acc"] + ((2 * g + 1 + (kind == "OG")) if masked else g + 1))
                                o_ = OTs if kind == "O" else OTg
                                for q in range(2):
                                    mm = pe.transpose(bank(n)[:, P * q:P * q + P], o_[:, P * q:P * q + P], identf[:, :])
                                mm.then_inc(ts["a_t"], 1)

                def copy_T(eng, who, kind, g):
                    n = use_no[kind, g]
                    eng.wait_ge(ts["a_t"], b0["a_t"] + n + 1)
                    pr = M if kind == "FKL" else P
                    w = 2 * P * (NKJ if kind == "K" else GH)
                    o, i_ = dst[kind][0:pr, g % 2, 0:w], bank(n).bitcast(BF16)[0:pr, 0:w]
                    if who == "act":
                        eng.activation(o, i_, ACT.Copy).then_inc(ts["a_td_act"], 1)
                    else:
                        eng.tensor_copy(o, i_).then_inc(ts["a_td_dve"], 1)

                @block.scalar
                def _(act):
                    for i in range(NG + 1):
                        if i < NG:
                            if i >= 2:
                                act.wait_ge(ts["a_pv"], b0["a_pv"] + (4 if masked else 2) * (i - 1))
                            copy_T(act, "act", "K", i)
                            if masked:
                                copy_T(act, "act", "FQ", i)
                                copy_T(act, "act", "FKL", i)
                        if i >= 1:
                            g = i - 1
                            for k in range(2):
                                n = 2 * g + k
                                act.wait_ge(ts["a_st"], b0["a_st"] + n + 1)
                                if n >= 2:
                                    act.wait_ge(ts["a_pv"], b0["a_pv"] + (4 if masked else 2) * g)
                                act.activation(PTn[:, k, :], ps[:, 4:6, :], ACT.Exp, scale=SCALE)\
                                   .then_inc(ts["a_exp"], 1)
                            act.wait_ge(ts["a_pv"], b0["a_pv"] + (4 if masked else 2) * (g + 1))
                            if g >= 1:
                                act.wait_ge(*read(use_no["O", g - 1]))
                            act.activation(OTs[:, :], ps[:, 6, 0:L], ACT.Copy).then_inc(ts["a_acc"], 1)
                            if masked:
                                if g >= 1:
                                    act.wait_ge(*read(use_no["OG", g - 1]))
                                act.activation(OTg[:, :], ps[:, 7, 0:L], ACT.Copy).then_inc(ts["a_acc"], 1)

                @block.vector
                def _(dve):
                    for i in range(NG + 1):
                        if i < NG:
                            b, hg = divmod(i, 4)
                            if i >= 2:
                                dve.wait_ge(ts["a_pv"], b0["a_pv"] + (4 if masked else 2) * (i - 1))
                            copy_T(dve, "dve", "Q", i)
                            if masked:
                                copy_T(dve, "dve", "FK", i)
                            for q in range(2):
                                n = sg_no["S", i, q]
                                dve.wait_ge(ts["a_s"], b0["a_s"] + n + 1)
                                dve.tensor_reduce(nmall[:, 2 * b + q, 4 * hg:4 * hg + 4],
                                                  ps[:, 2:4, :].rearrange("p a (j n) -> p (a j) n", n=L),
                                                  AX.X, ALU.max, negate=True).then_inc(ts["a_sr"], 1)
                            dve.wait_ge(ts["a_sr"], b0["a_sr"] + n + 1)
                            nm_ = nmall[:, 2 * b:2 * b + 2, 4 * hg:4 * hg + 4]
                            q_ = QN[:, 2 * b:2 * b + 2, 4 * hg:4 * hg + 4, :]
                            link_dve(dve.tensor_copy(q_[:, :, :, SROWS], nm_))
                            link_dve(dve.tensor_tensor(nrs, nm_, q_[:, :, :, SROWS], ALU.subtract))
                            link_dve(dve.tensor_copy(q_[:, :, :, SROWS + 1], nrs))
                            dve.tensor_tensor(q_[:, :, :, SROWS + 2], nrs, q_[:, :, :, SROWS + 1],
                                              ALU.subtract).then_inc(ts["a_mp"], 1)
                        if i >= 1:
                            g = i - 1
                            b, hg = divmod(g, 4)
                            copy_T(dve, "dve", "QT", g)
                            if masked:
                                for k in range(2):
                                    n = sg_no["G", g, k]
                                    dve.wait_ge(ts["a_s"], b0["a_s"] + n + 1)
                                    if g >= 1:
                                        dve.wait_ge(ts["a_pv"], b0["a_pv"] + 4 * g)
                                    dve.tensor_tensor(PG[:, k, :].rearrange("p (j n) -> p j n", n=L),
                                                      ps[:, 2:4, :].rearrange("p a (j n) -> p (a j) n", n=L),
                                                      wmask[:, k, :].unsqueeze(1).broadcast_to([P, GH, L]),
                                                      ALU.mult).then_inc(ts["a_gm"], 1)
                                    dve.wait_ge(ts["a_gm"], b0["a_gm"] + 2 * g + k + 1)
                                    dve.sem_inc(ts["a_sr"], 1)
                            for kind, S_ in (("O", As), ("OG", Gs)) if masked else (("O", As),):
                                n = use_no[kind, g]
                                dve.wait_ge(ts["a_t"], b0["a_t"] + n + 1)
                                o = bank(n)[:, 0:2 * P].rearrange("p (q j d) -> p q j d", q=2, d=32)
                                for q in range(2):
                                    ins = dve.tensor_copy(S_[:, 2 * b + q, 4 * hg:4 * hg + 4, :], o[:, q, :, 0:VW])
                                ins.then_inc(ts["a_td_dve"], 1)

            base["a_t"] += len(uses)
            for who in ("act", "dve"):
                base["a_td_" + who] += sum(u[2] == who for u in uses)
            base["a_s"] += len(sg)
            base["a_sr"] += len(sg)
            base["a_mp"] += NG
            base["a_st"] += 2 * NG
            base["a_exp"] += 2 * NG
            base["a_gm"] += 2 * NG if masked else 0
            base["a_pv"] += (4 if masked else 2) * NG
            base["a_acc"] += (2 if masked else 1) * NG

        attention(True)

        s5 = {n: sem(n) for n in ("c_ln1", "c_e1", "c_l2", "c_g", "c_q", "c_qc", "c_ph", "c_p", "c_pc", "c_v", "c_vc")}
        A16 = As[:, :, :, DH]
        Y = Gs[:, :, :, DH]
        with nc.Block() as block:
            @block.vector
            def _(dve):
                link_dve(dve.tensor_scalar(t1, Y, 1e-24, None, ALU.max))
                for R in range(RT):
                    ins = dve.tensor_tensor(t2[:, R, :], qls[:, R, :], kls[:, R // 2, :], ALU.add)
                link_dve(ins)
                dve.sem_inc(s5["c_ln1"], 1)
                dve.wait_ge(s5["c_l2"], 2)
                link_dve(dve.scalar_tensor_tensor(out=t0, in0=nmall, scalar=-SCALE, in1=t0, op0=ALU.mult, op1=ALU.add))
                link_dve(dve.tensor_tensor(t1, t1, t2, ALU.add))
                link_dve(dve.tensor_tensor(t3, t0, t1, ALU.max))
                link_dve(dve.tensor_tensor(t0, t0, t3, ALU.subtract))
                dve.tensor_tensor(t1, t1, t3, ALU.subtract).then_inc(s5["c_ln1"], 1)
                dve.wait_ge(s5["c_l2"], 4)
                dve.tensor_tensor(t0, t0, t1, ALU.add).then_inc(s5["c_ln1"], 1)
                dve.wait_ge(s5["c_l2"], 5)
                link_dve(dve.tensor_tensor(t0, t0, t3, ALU.add))
                dve.tensor_tensor(t0, t2, t0, ALU.subtract).then_inc(s5["c_ln1"], 1)
                link_dve(dve.reciprocal(t1, A16))
                dve.wait_ge(s5["c_l2"], 6)
                for R in range(RT):
                    a_ = att[:, R, :].rearrange("p (h d) -> p h d", d=DH)
                    link_dve(dve.tensor_tensor(a_, As[:, R, :, 0:DH], t1[:, R, :].unsqueeze(2).broadcast_to([P, H, DH]),
                                               ALU.mult))
                    g_ = Gs[:, R, :, 0:DH]
                    link_dve(dve.tensor_tensor(g_, g_, t0[:, R, :].unsqueeze(2).broadcast_to([P, H, DH]), ALU.mult))
                    ins = dve.tensor_tensor(a_, a_, g_, ALU.add)
                    link_dve(ins)
                dve.sem_inc(s_attb, 1)
                residual_dve(dve, 1)
                ln_dve(dve, 2, 1e-5)
                for R in range(RT):
                    dve.wait_ge(s5["c_v"], R + 1)
                    v_ = V2[:, R, 0:GH * VW].rearrange("p (h d) -> p h d", d=VW)
                    dve.tensor_copy(v_[:, :, 0:DH], ps[:, R, 256 + 64:256 + 128].rearrange("p (h d) -> p h d", d=DH))\
                       .then_inc(s5["c_vc"], 1)
                for side in range(2):
                    nh = H if side == 0 else GH
                    T, sm_, sl_ = (QN, 1, 4) if side == 0 else (KN, 2, 5)
                    dve.wait_ge(s5["c_ph"], RT)
                    for R in range(RT):
                        q = QK[:, R, D * side:D * side + DH * nh].rearrange("p (h d) -> p h d", d=DH)
                        link_dve(dve.tensor_tensor(q, q, T[:, R, 0:nh, 0:DH], ALU.subtract))
                        link_dve(dve.tensor_copy(T[:, R, 0:nh, DH * sm_:DH * sm_ + DH], q))
                        link_dve(dve.tensor_tensor(T[:, R, 0:nh, DH * sl_:DH * sl_ + DH], q,
                                                   T[:, R, 0:nh, DH * sm_:DH * sm_ + DH], ALU.subtract))
                dve.sem_inc(s5["c_p"], 1)

            @block.scalar
            def _(act):
                act.wait_ge(s5["c_ln1"], 1)
                act.activation(t0, A16, ACT.Ln).then_inc(s5["c_l2"], 1)
                act.activation(t1, t1, ACT.Ln).then_inc(s5["c_l2"], 1)
                act.wait_ge(s5["c_ln1"], 2)
                act.activation(t0, t0, ACT.Exp).then_inc(s5["c_l2"], 1)
                act.activation(t1, t1, ACT.Exp).then_inc(s5["c_l2"], 1)
                act.wait_ge(s5["c_ln1"], 3)
                act.activation(t0, t0, ACT.Ln).then_inc(s5["c_l2"], 1)
                act.wait_ge(s5["c_ln1"], 4)
                act.activation(t0, t0, ACT.Exp).then_inc(s5["c_l2"], 1)
                rows_T_act(act, 3)
                ln_act(act, 2)
                rows_T_act(act, 4)
                for R in range(RT):
                    act.wait_ge(s5["c_vc"], R + 1)
                    link_act(act.activation(QK[:, R, 0:D + 64], ps[:, R, 0:D + 64], ACT.Copy))
                    act.activation(QN[:, R, :, 0:DH], QK[:, R, 0:D].rearrange("p (h d) -> p h d", d=DH), ACT.Copy)
                    link_act(act.activation(KN[:, R, 0:GH, 0:DH], QK[:, R, D:D + 64].rearrange("p (h d) -> p h d", d=DH),
                                            ACT.Copy))
                    act.sem_inc(s5["c_ph"], 1)

            @block.gpsimd
            def _(pool):
                def slot(T, R, n, nh):
                    return T[:, R, 0:nh, DH * n:DH * n + DH]
                pool.wait_ge(s5["c_ph"], RT)
                for R in range(RT):
                    for n in (2, 5):
                        pool.tensor_copy(slot(QN, R, n, H), slot(QN, R, 0, H)).then_inc(s5["c_pc"], 1)
                    for n in (1, 4):
                        pool.tensor_copy(slot(KN, R, n, GH), slot(KN, R, 0, GH)).then_inc(s5["c_pc"], 1)
                pool.wait_ge(s5["c_p"], 1)
                for R in range(RT):
                    pool.tensor_copy(slot(QN, R, 3, H), slot(QN, R, 1, H)).then_inc(s5["c_pc"], 1)
                    pool.tensor_copy(slot(KN, R, 3, GH), slot(KN, R, 2, GH)).then_inc(s5["c_pc"], 1)

            @block.tensor
            def _(pe):
                pe.wait_ge(s_attb, 2)
                rows_T_pe(pe, 3, att)
                pe.wait_ge(s_lnTc, 4 * KT)
                project_pe(pe, 1, woT2, b_out2)
                pe.wait_ge(s_ln, 3 * RT)
                rows_T_pe(pe, 4, lnx)
                pe.wait_ge(s_lnTc, 5 * KT)
                pe.wait_ge(s_wl3, 128)
                kv = wk.rearrange("p (k n) -> p k n", k=4)
                for R in range(RT):
                    for lo, w, br in ((0, lambda k: wq[:, k, :], b_q3), (D, lambda k: kv[:, k, :], bkv[:, 0:64]),
                                      (D + 64, lambda k: kv[:, 2 + k, :], bkv[:, 64:128])):
                        hi = lo + br.shape[1]
                        for k in range(KT):
                            pe.matmul(ps[:, R, lo:hi], lnT[:, k, P * R:P * R + P], w(k), start=(k == 0), stop=False)
                        mm = pe.matmul(ps[:, R, lo:hi], onesf[0:1, :], br, start=False, stop=True)
                    mm.then_inc(s5["c_v"], 1)

        if stop == "x2":
            return store_x(X[:, :, :])
        attention(False)

        s7 = {n: sem(n) for n in ("m_wn", "m_dr", "m_ar", "m_ln", "m_lg", "m_sg", "m_M", "m_rk", "m_h", "m_g", "m_y",
                                  "m_acc", "m_c")}
        src_ = lnx

        def c8(at):
            return small[:, at:at + RT * E].rearrange("p (r e) -> p r e", e=E)

        def c1(at):
            return small[:, at:at + RT]

        pr, Ma, Mb, wt, ec, tmp = c8(0), c8(32), c8(64), c8(96), c8(128), c8(160)
        Mbf = small[:, 192:208].bitcast(BF16).rearrange("p (r e) -> p r e", e=E)
        top1, top2, rcp, cm = c1(224), c1(228), c1(232), c1(236)

        def bc(x):
            return x.unsqueeze(2).broadcast_to([P, RT, E])

        def rms_dve(dve, n, srcT, dstT, wn, k):
            for R in range(RT):
                link_dve(dve.bn_stats(bst[:, R, :], srcT[:, R, :]))
                link_dve(dve.bn_aggr(mv[:, R, :], bst[:, R, :]))
            link_dve(dve.tensor_tensor(ve[:, :], mv[:, :, 0], mv[:, :, 0], ALU.mult))
            link_dve(dve.scalar_tensor_tensor(out=ve[:, :], in0=ve[:, :], scalar=1e-6, in1=mv[:, :, 1],
                                              op0=ALU.add, op1=ALU.add))
            dve.sem_inc(s_var, 1)
            dve.wait_ge(s_std, n + 1)
            link_dve(dve.reciprocal(rs[:, :], sd[:, :]))
            for R in range(RT):
                link_dve(dve.scalar_tensor_tensor(out=dstT[:, R, :], in0=srcT[:, R, :], scalar=rs[:, R:R + 1],
                                                  in1=wn[:, :], op0=ALU.mult, op1=ALU.mult))
            dve.sem_inc(s7["m_ln"], 1)

        with nc.Block() as block:
            @block.sync
            def _(sp):
                sp.dma_start(wn1[:, :], t_in["L0_ffn_norm1_w"].partition_broadcast(P)).then_inc(s7["m_wn"], 16)
                sp.dma_start(wn2[:, :], t_in["L0_ffn_norm2_w"].partition_broadcast(P)).then_inc(s7["m_wn"], 16)
                sp.dma_start(gate[:, :, :], t_in["L0_ffn_gate_w"].rearrange("(k p) e -> p k e", p=P)).then_inc(s7["m_wn"], 16)
                sp.wait_ge(s7["m_ln"], 3)
                sp.dma_start(out.rearrange("b (r p) d -> p (b r) d", p=P), X[:, :, :]).then_inc(s_out, 16)
                sp.wait_ge(s_out, 16)

            @block.gpsimd
            def _(pool):
                link_pool(pool.memset(lowb[:, :, :], 1.0))
                link_pool(pool.affine_select(out=lowb[:, 0, :], in_=lowb[:, 0, :], compare_op=ALU.is_gt, fill=0.0,
                                             base=0, pattern=[[1, P]], channel_multiplier=-1))
                link_pool(pool.iota(ec[:, :, :], pattern=[[0, RT], [-1, E]], base=E, channel_multiplier=0,
                                    allow_small_or_imprecise_dtypes=True))
                pool.sem_inc(s7["m_c"], 1)

            @block.vector
            def _(dve):
                link_dve(dve.reciprocal(t1, A16))
                for R in range(RT):
                    a_ = att[:, R, :].rearrange("p (h d) -> p h d", d=DH)
                    link_dve(dve.tensor_tensor(a_, As[:, R, :, 0:DH], t1[:, R, :].unsqueeze(2).broadcast_to([P, H, DH]),
                                               ALU.mult))
                dve.sem_inc(s_attb, 1)
                for R in range(RT):
                    dve.wait_ge(s_op, RT * 2 + R + 1)
                    link_dve(dve.tensor_tensor(lnx[:, R, :], lnx[:, R, :], PB[R],
                                               ALU.add))
                dve.wait_ge(s7["m_wn"], 48)
                rms_dve(dve, 3, lnx, lnx, wn1, 0)
                dve.wait_ge(s7["m_sg"], 1)
                dve.wait_ge(s7["m_c"], 1)
                for first, (top, Mx) in enumerate(((top1, Ma), (top2, Mb))):
                    link_dve(dve.tensor_reduce(top, pr, AX.X, ALU.max))
                    link_dve(dve.tensor_tensor(tmp, pr, bc(top), ALU.is_equal))
                    link_dve(dve.tensor_tensor(tmp, tmp, ec, ALU.mult))
                    link_dve(dve.tensor_reduce(cm, tmp, AX.X, ALU.max))
                    link_dve(dve.tensor_tensor(Mx, tmp, bc(cm), ALU.is_equal))
                    if first == 0:
                        link_dve(dve.scalar_tensor_tensor(out=pr, in0=Ma, scalar=-4.0, in1=pr, op0=ALU.mult, op1=ALU.add))
                link_dve(dve.scalar_tensor_tensor(out=rcp, in0=top1, scalar=1e-6, in1=top2, op0=ALU.add, op1=ALU.add))
                link_dve(dve.reciprocal(rcp, rcp))
                link_dve(dve.tensor_tensor(tmp, Ma, bc(top1), ALU.mult))
                link_dve(dve.tensor_tensor(wt, Mb, bc(top2), ALU.mult))
                link_dve(dve.tensor_tensor(wt, wt, tmp, ALU.add))
                link_dve(dve.tensor_tensor(wt, wt, bc(rcp), ALU.mult))
                link_dve(dve.tensor_tensor(Mbf, Ma, Mb, ALU.add))
                dve.sem_inc(s7["m_M"], 1)
                dve.wait_ge(s7["m_rk"], 1)
                link_dve(dve.tensor_scalar(tmp, ps[:, 7, 0:RT * E].rearrange("p (r e) -> p r e", e=E), float(CAP), None,
                                           ALU.is_lt))
                link_dve(dve.tensor_tensor(wt, wt, tmp, ALU.mult))
                link_dve(dve.memset(acc[:, :, :], 0.0))
                for e in range(E):
                    for R in range(RT):
                        if R % 2 == 0:
                            dve.wait_ge(s7["m_y"], 2 * e + R // 2 + 1)
                        ins = dve.scalar_tensor_tensor(out=acc[:, R, :], in0=ps[:, 4 + 2 * (e % 2) + R // 2, 256 * (R % 2):256 * (R % 2) + 256],
                                                       scalar=wt[:, R, e:e + 1], in1=acc[:, R, :], op0=ALU.mult,
                                                       op1=ALU.add)
                        ins.then_inc(s7["m_acc"], 1)
                    dve.wait_ge(s7["m_acc"], RT * (e + 1))
                for R in range(RT):
                    link_dve(dve.tensor_tensor(lnx[:, R, :], lnx[:, R, :], acc[:, R, :], ALU.add))
                rms_dve(dve, 4, lnx, lnx, wn2, 1)
                for R in range(RT):
                    link_dve(dve.tensor_tensor(X[:, R, :], X[:, R, :], lnx[:, R, :], ALU.add))
                dve.sem_inc(s7["m_ln"], 1)

            @block.scalar
            def _(act):
                rows_T_act(act, 5)
                ln_act(act, 3)
                rows_T_act(act, 6)
                act.wait_ge(s7["m_lg"], 1)
                act.activation(pr, ps[:, 6, 0:RT * E].rearrange("p (r e) -> p r e", e=E), ACT.Sigmoid).then_inc(s7["m_sg"], 1)
                for e in range(E):
                    for f in range(FF // P):
                        n = 4 * e + f
                        act.wait_ge(s7["m_h"], n + 1)
                        if e >= 2:
                            act.wait_ge(s7["m_y"], 2 * (e - 1))
                        act.activation(hT[:, e % 2, f, :], ps[:, n % 4, :], ACT.Gelu).then_inc(s7["m_g"], 1)
                ln_act(act, 4)

            @block.tensor
            def _(pe):
                pe.wait_ge(s_attb, 3)
                rows_T_pe(pe, 5, att)
                pe.wait_ge(s_lnTc, 6 * KT)
                project_pe(pe, 2, wo, b_o3)
                pe.wait_ge(s7["m_ln"], 1)
                rows_T_pe(pe, 6, lnx)
                pe.wait_ge(s_lnTc, 7 * KT)
                for R in range(RT):
                    for k in range(KT):
                        mm = pe.matmul(ps[:, 6, E * R:E * R + E], lnT[:, k, P * R:P * R + P], gate[:, k, :],
                                       start=(k == 0), stop=(k == KT - 1))
                mm.then_inc(s7["m_lg"], 1)

                def up(e):
                    for f in range(FF // P):
                        n = 4 * e + f
                        if n >= 4:
                            pe.wait_ge(s7["m_g"], n - 3)
                        for k in range(KT):
                            mm = pe.matmul(ps[:, n % 4, :], w1[:, e, k, P * f:P * f + P], lnT[:, k, :],
                                           start=(k == 0), stop=(k == KT - 1))
                        mm.then_inc(s7["m_h"], 1)

                pe.wait_ge(s_wl4, 256)
                up(0)
                pe.wait_ge(s7["m_M"], 1)
                for R in range(RT):
                    for r in range(R + 1):
                        mm = pe.matmul(ps[:, 7, E * R:E * R + E], lowb[:, 0 if r == R else 1, :], Mbf[:, r, :],
                                       start=(r == 0), stop=(r == R))
                mm.then_inc(s7["m_rk"], 1)
                for e in range(E):
                    if e + 1 < E:
                        up(e + 1)
                    for R in range(RT):
                        if e == 1 and R == 0:
                            pe.wait_ge(s7["m_acc"], 1)
                        if R % 2 == 0 and e >= 2:
                            pe.wait_ge(s7["m_acc"], RT * (e - 1))
                        if R == 0:
                            pe.wait_ge(s7["m_g"], 4 * (e + 1))
                        for f in range(FF // P):
                            mm = pe.matmul(ps[:, 4 + 2 * (e % 2) + R // 2, 256 * (R % 2):256 * (R % 2) + 256],
                                           hT[:, e % 2, f, P * R:P * R + P], w2[:, e, f, :],
                                           start=(f == 0), stop=(f == FF // P - 1))
                        if R % 2 == 1:
                            mm.then_inc(s7["m_y"], 1)


_INS = ['x', 'ctx_512', 'L0_xattn_Wq', 'L0_xattn_bq', 'L0_xattn_Wk', 'L0_xattn_bk', 'L0_xattn_Wv', 'L0_xattn_bv',
        'L0_xattn_Wo', 'L0_xattn_bo', 'L0_attn_Wqkv_w', 'L0_attn_Wqkv_b', 'L0_attn_proj', 'L0_attn_out_w',
        'L0_attn_out_b', 'L0_ffn_qw', 'L0_ffn_qb', 'L0_ffn_kw', 'L0_ffn_kb', 'L0_ffn_vw', 'L0_ffn_vb', 'L0_ffn_ow',
        'L0_ffn_ob', 'L0_ffn_gate_w', 'L0_ffn_w1', 'L0_ffn_w2', 'L0_ffn_norm1_w', 'L0_ffn_norm2_w']


def kernel(**inputs):
    import numpy as _np
    import concourse.bacc as _bacc
    from concourse import mybir as _mybir
    from concourse.bass_utils import run_bass_kernel_spmd as _run

    nc = _bacc.Bacc("TRN2", target_bir_lowering=False, num_devices=1)
    arrays, aps = {}, {}
    for name in _INS:
        a = _np.ascontiguousarray(inputs[name])
        arrays[f"in_{name}_dram"] = a
        aps[name] = nc.dram_tensor(f"in_{name}_dram", a.shape, _mybir.dt.from_np(a.dtype), kind="ExternalInput").ap()
    out = nc.dram_tensor("out_0_dram", (B, L, D), F32, kind="ExternalOutput").ap()
    build(nc, aps, out)
    r = _run(nc, [arrays], core_ids=[0])
    return r.results[0]["out_0_dram"]
```

```python
from contextlib import ExitStack

import concourse.bass as bass
from concourse import mybir

F32 = mybir.dt.float32
BF16 = mybir.dt.bfloat16
F16 = mybir.dt.float16
ALU = mybir.AluOpType
ACT = mybir.ActivationFunctionType
AX = mybir.AxisListType

P = 128
B, L, D = 2, 256, 256
H, DH = 16, 16
NK, DC = 4096, 128
RT = B * L // P
KT = D // P
GH = 4
NG = B * H // GH
M = 24
E, FF, CAP = 8, 512, 160
TPB = NK // P
VW = DH + 1
SCALE = 0.25

QSLOT = "hmhmlh"
KSLOT = "hhmmhl"
NS = len(QSLOT)
SROWS = NS * DH
MROWS = SROWS + 3
SPS = 5
SPI, PLI = 16 * GH * SPS, 16 * GH * (NS - SPS)

LEAD = 5
SPG = TPB
UPG = 64
S0 = -(SPG + LEAD) - 1
SEND = NG * SPG


def aux_of(s):
    out = []
    if 1 <= s - S0 < 9:
        out.append(("C", s - S0 - 1))
    if s - S0 >= 10 and (s - S0 - 10) % 3 == 0 and (s - S0 - 10) // 3 < 8:
        out.append(("V", (s - S0 - 10) // 3))
    for e in range(1, 4):
        for c in range(8):
            if s == 2 * SPG * (e - 1) - 8 + 4 * c:
                out.append(("K", 8 * e + c))
            if s == 2 * SPG * (e - 1) + 38 + 4 * c:
                out.append(("V", 8 * e + c))
    for g in range(NG):
        if s == SPG * (g - 1) - LEAD - (1 if g == 0 else 2):
            out.append(("QS", g))
        if s == SPG * g - 3:
            out.append(("QT", g))
        if s == SPG * (g + 1) + 4:
            out.append(("OT", g))
    return out


AUX = [(s, kind, i) for s in range(S0, SEND + 8) for kind, i in aux_of(s)]
AUX_NO = {(kind, i): n for n, (s, kind, i) in enumerate(AUX)}
assert len(AUX_NO) == 24 + 32 + 8 + 3 * NG


def units_of(s):
    first = UPG + 2 * (s + LEAD)
    return range(max(first, 0), max(min(first + 2, UPG * NG), 0))


def build(nc, t_in, out, stop=None):
    with ExitStack() as ctx:
        def sb(name, shape, dt=F32):
            return ctx.enter_context(nc.sbuf_tensor(name, shape, dt))

        def sem(name):
            return ctx.enter_context(nc.semaphore(name))

        ps = ctx.enter_context(nc.psum_tensor("ps", [P, 8, 512], F32))

        identf = sb("identf", [P, P])
        identb = sb("identb", [P, P], BF16)
        onesf = sb("onesf", [P, P])
        X = sb("X", [P, RT, D])
        lnx = sb("lnx", [P, RT, D])
        lnT = sb("lnT", [P, KT, B * L])
        bst = sb("bst", [P, RT, 6])
        mv = sb("mv", [P, RT, 2])
        ve = sb("ve", [P, RT])
        sd = sb("sd", [P, RT])
        rs = sb("rs", [P, RT])

        wq = sb("wq", [P, KT, D])
        wo = sb("wo", [P, KT, D])
        wk = sb("wk", [P, D])
        wv = sb("wv", [P, D])
        bqr = sb("bqr", [1, D])
        bor = sb("bor", [1, D])
        bkc = sb("bkc", [P, 2])
        bvb = sb("bvb", [P, D])
        big = sb("big", [P, 2, GH, NK], BF16)
        stack = big
        ctxn = stack[:, 1, :, :].rearrange("p j n -> p (j n)").bitcast(F32).rearrange(
            "p (b t c) -> p b t c", b=B, c=DC)
        ctxT = sb("ctxT", [P, B, NK])
        kpt = sb("kpt", [P, 3, NK], BF16)
        kh, km, kl = kpt[:, 0, :], kpt[:, 1, :], kpt[:, 2, :]
        kparts = {"h": kh, "m": km, "l": kl}
        kr = sb("kr", [P, 2, 512])
        Vg = sb("Vg", [P, 2, TPB * GH * VW + 32 - VW])
        PT = sb("PT", [P, 3, GH * L])
        qf = lnx
        qpt = sb("qpt", [P, 3, RT, D], BF16)
        qh, qm, ql = qpt[:, 0], qpt[:, 1], qpt[:, 2]
        qparts = {"h": qh, "m": qm, "l": ql}
        Qg = sb("Qg", [P, 2, 2 * GH, P], BF16)
        QS = sb("QS", [P, 2, 2 * GH * P], BF16)
        QT = sb("QT", [P, 2, 2 * GH * P], BF16)
        mx = sb("mx", [P, 2, 2 * GH, 8])
        nm = sb("nm", [P, 2 * GH])
        nr = sb("nr", [P, 2 * GH])
        OTs = sb("OTs", [P, L])
        rec = sb("rec", [P, 2, GH])
        att = sb("att", [P, RT, D])

        ST = [ps[:, 0:2, :], ps[:, 2:4, :]]
        SM = [ps[:, 4, :], ps[:, 5, :]]
        ACC = ps[:, 6, :]
        AUXB = ps[:, 7, :]

        def max_bank(n):
            return [SM[0], SM[1], ps[:, 0, :], ps[:, 1, :], ps[:, 2, :], ps[:, 3, :]][n % 6 if n < UPG else n % 2]

        s_x = sem("s_x")
        s_w1 = sem("s_w1")
        s_ctx = [sem(f"s_ctx{i}") for i in range(8)]
        s_const = sem("s_const")
        s_vg1 = sem("s_vg1")
        s_ones1 = sem("s_ones1")
        s_wk = sem("s_wk")
        s_wq = sem("s_wq")
        s_k = sem("s_k")
        s_kh = sem("s_kh")
        s_km = sem("s_km")
        s_kr = sem("s_kr")
        s_pool = sem("s_pool")
        s_dve = sem("s_dve")
        s_act = sem("s_act")
        s_var = sem("s_var")
        s_std = sem("s_std")
        s_ln = sem("s_ln")
        s_lnT = sem("s_lnT")
        s_lnTc = sem("s_lnTc")
        s_q = sem("s_q")
        s_qf = sem("s_qf")
        s_qp = sem("s_qp")
        s_ct = sem("s_ct")
        s_ctc = sem("s_ctc")
        s_stack = [[sem(f"s_stack{p}{h}") for h in range(2)] for p in range(2)]
        s_stackp = [[sem(f"s_stackp{p}{h}") for h in range(2)] for p in range(2)]
        s_ones = sem("s_ones")
        s_sm = sem("s_sm")
        s_red = sem("s_red")
        s_st = sem("s_st")
        s_exp = sem("s_exp")
        s_pv = sem("s_pv")
        s_acc = sem("s_acc")
        s_aux = sem("s_aux")
        s_auxd = sem("s_auxd")
        s_khd = sem("s_khd")
        s_kl = sem("s_kl")
        s_qg = sem("s_qg")
        s_mp = sem("s_mp")
        s_out = sem("s_out")

        count = {"dve": 0, "act": 0, "pool": 0}

        def link_dve(ins):
            count["dve"] += 1
            ins.then_inc(s_dve, 1)
            nc.vector.wait_ge(s_dve, count["dve"])

        def link_act(ins):
            count["act"] += 1
            ins.then_inc(s_act, 1)
            nc.scalar.wait_ge(s_act, count["act"])

        def link_pool(ins):
            count["pool"] += 1
            ins.then_inc(s_pool, 1)
            nc.gpsimd.wait_ge(s_pool, count["pool"])

        xin = t_in["x"].rearrange("b (r p) d -> p (b r) d", p=P)
        cin = t_in["ctx_512"].rearrange("b (p t) c -> p b t c", p=P)

        def view(tensor_words, at, shape, dt=F32):
            n = 1
            for x in shape[1:]:
                n *= x
            words = n if dt == F32 else n // 2
            v = tensor_words[:, at:at + words]
            if dt != F32:
                v = v.bitcast(dt)
            if len(shape) == 2:
                return v
            names = "abcd"[:len(shape) - 1]
            return v.rearrange(f"p ({' '.join(names)}) -> p {' '.join(names)}",
                               **{c: x for c, x in zip(names, shape[1:])})

        bigw = big.rearrange("p a j n -> p (a j n)").bitcast(F32)
        ctxw = ctxT.rearrange("p b n -> p (b n)")
        kw_ = kpt.rearrange("p a n -> p (a n)").bitcast(F32)
        vgw = Vg.rearrange("p g n -> p (g n)")
        ptw = PT.rearrange("p a n -> p (a n)")
        QN = view(bigw, 0, [P, RT, H, P], BF16)
        KN = view(bigw, 4096, [P, RT, H, P], BF16)
        FQ = view(bigw, 8192, [P, RT, H, P], BF16)
        FK = view(bigw, 12288, [P, RT, H, P], BF16)
        wqkvT = view(bigw, 12288, [P, KT, 3 * D])
        w1 = view(ctxw, 0, [P, E, KT, FF])
        w2 = view(bigw, 8192, [P, E, FF // P, D])
        QK = view(kw_, 0, [P, RT, 2 * D])
        fq = view(kw_, 2048, [P, RT, H, M])
        fk = view(kw_, 3584, [P, RT, H, M])
        FKL = view(kw_, 5120, [P, RT, H, M], BF16)
        PG = view(kw_, 0, [P, 2, GH * L])
        As = view(kw_, 2048, [P, RT, H, VW])
        Gs = view(kw_, 3136, [P, RT, H, VW])
        xT = view(vgw, 0, [P, 2, KT, B * L])
        xsq = view(vgw, 2048, [P, 2, KT, B * L])
        KSg = view(vgw, 0, [P, 2, 2 * GH * P], BF16)
        FQT = view(vgw, 1024, [P, 2, 2 * GH * P], BF16)
        FKT = view(vgw, 2048, [P, 2, 2 * GH * P], BF16)
        FKLT = view(vgw, 3072, [P, 2, 2 * GH * P], BF16)
        V2 = view(qpt.rearrange("p a r d -> p (a r d)").bitcast(F32), 0, [P, RT, H * VW + 32 - VW])
        hT = view(kw_, 0, [P, 2, FF // P, B * L])
        acc = view(ptw, 0, [P, RT, D])
        krw = kr.rearrange("p a n -> p (a n)")
        wraw = view(bigw, 0, [P, 8, D])
        woT2 = view(ptw, 2048, [P, KT, D])
        projb = view(ptw, 1024, [P, 2, 8 * M])
        OTg = view(ptw, 2560, [P, L])
        wn1 = view(ptw, 1024, [P, D])
        wn2 = view(ptw, 1280, [P, D])
        gate = view(ptw, 1536, [P, KT, E])
        lowb = view(ptw, 1600, [P, 2, P], BF16)
        maskq = view(krw, 0, [P, 2, L], F16)
        maskk = view(krw, 256, [P, 2, L], F16)
        wmask = view(krw, 512, [P, 2, L])
        small = Qg.rearrange("p a r n -> p (a r n)").bitcast(F32)
        identh = sb("identh", [P, P], F16)
        rows = sb("rows", [1, 6 * D + 128])

        def load_slots(eng, g, half, slots, signal):
            if g == 0 and signal is s_stack[0][half]:
                eng.wait_ge(s_km, 4 * half + 4)
            else:
                eng.wait_ge(s_kl, 8 * (g // 2) + 4 * half + 4)
            if g >= 2:
                eng.wait_ge(s_st, SPG * (g - 2) + 16 * (half + 1))
            elif g == 1 and half == 0:
                eng.wait_ge(s_auxd, AUX_NO["C", 7] + 1)
            for j in range(GH):
                r = 64 * (g % 2) + DH * j
                for n in slots:
                    eng.dma_start(stack[DH * n:DH * n + DH, g % 2, j, 2048 * half:2048 * half + 2048],
                                  kparts[KSLOT[n]][r:r + DH, 2048 * half:2048 * half + 2048]).then_inc(signal, 16)

        def load_slots_sp(sp, g, half):
            load_slots(sp, g, half, range(SPS), s_stack[g % 2][half])

        def load_slots_pool(pool, g, half):
            load_slots(pool, g, half, range(SPS, NS), s_stackp[g % 2][half])

        def group_rows(pool, g):
            b, hg = divmod(g, 4)
            pool.wait_ge(s_qp, b + 1)
            if g >= 2:
                pool.wait_ge(s_auxd, AUX_NO["QT", g - 2] + 1)
            for n in range(NS):
                o = Qg[:, g % 2, :, DH * n:DH * n + DH].rearrange("p (j q) d -> p q j d", q=2)
                src = qparts[QSLOT[n]][:, 2 * b:2 * b + 2, 64 * hg:64 * hg + 64].rearrange(
                    "p q (j d) -> p q j d", d=DH)
                for q in range(2):
                    ins = pool.tensor_copy(o[:, q], src[:, q])
            ins.then_inc(s_qg, 1)

        CB = [ps[:, i, :] for i in range(2)]
        KB = [ps[:, 2 + i, :] for i in range(2)]
        LB = [ps[:, 4 + i, :] for i in range(2)]
        QB = [ps[:, 6 + i, 0:256] for i in range(2)]
        NCT = TPB // 4
        with nc.Block() as block:
            @block.sync
            def _(sp):
                def chunk(i):
                    b, q = divmod(i, 4)
                    sp.dma_start(ctxn[:, b, 8 * q:8 * q + 8, :], cin[:, b, 8 * q:8 * q + 8, :]).then_inc(s_ctx[i], 16)

                sp.dma_start(X[:, :, :], xin).then_inc(s_x, 16)
                for i in range(4):
                    chunk(i)
                sp.dma_start(wv[:, :], t_in["L0_xattn_Wv"]).then_inc(s_w1, 16)
                sp.dma_start(bvb[:, :], t_in["L0_xattn_bv"].partition_broadcast(P)).then_inc(s_w1, 16)
                sp.dma_start(wo[:, :, :], t_in["L0_xattn_Wo"].rearrange("(k p) n -> p k n", p=P)).then_inc(s_w1, 16)
                sp.dma_start(bor[:, :], t_in["L0_xattn_bo"].rearrange("(a n) -> a n", a=1)).then_inc(s_w1, 16)
                for i in range(4, 8):
                    chunk(i)
                sp.wait_ge(s_vg1, 1)
                ones = stack[SROWS:MROWS, 0, 0, 0:512]
                sp.dma_start(stack[SROWS:MROWS, 0, :, :].rearrange("p j (c n) -> p (j c) n", n=512)[:, 1:32, :],
                             ones.unsqueeze(1).broadcast_to([3, 31, 512])).then_inc(s_ones, 16)
                load_slots_sp(sp, 0, 0)

            @block.gpsimd
            def _(pool):
                pool.memset(onesf[:, :], 1.0).then_inc(s_const, 1)
                link_pool(pool.memset(identf[:, :], 0.0))
                link_pool(pool.affine_select(out=identf[:, :], in_=identf[:, :], compare_op=ALU.not_equal, fill=1.0,
                                             base=0, pattern=[[-1, P]], channel_multiplier=1))
                pool.tensor_copy(identb[:, :], identf[:, :]).then_inc(s_const, 1)
                pool.memset(Qg[:, :, :, :], 0.0).then_inc(s_const, 1)
                for c in range(NCT):
                    pool.wait_ge(s_km, c + 1)
                    sl = slice(512 * c, 512 * c + 512)
                    pool.tensor_tensor(kl[:, sl], kr[:, c % 2, :], km[:, sl], ALU.subtract).then_inc(s_kl, 1)
                    if c == 5:
                        pool.wait_ge(s_const, 3)
                        group_rows(pool, 0)
                load_slots_pool(pool, 0, 0)

            @block.scalar
            def _(act):
                act.dma_start(wk[:, :], t_in["L0_xattn_Wk"]).then_inc(s_wk, 16)
                act.dma_start(bkc[:, :], t_in["L0_xattn_bk"].rearrange("(k p) -> p k", p=P),
                              allow_slow_non_contiguous=True).then_inc(s_wk, 16)
                act.dma_start(wq[:, :, :], t_in["L0_xattn_Wq"].rearrange("(k p) n -> p k n", p=P)).then_inc(s_wq, 16)
                act.dma_start(bqr[:, :], t_in["L0_xattn_bq"].rearrange("(a n) -> a n", a=1)).then_inc(s_wq, 16)
                act.wait_ge(s_var, 1)
                act.activation(sd[:, :], ve[:, :], ACT.Sqrt).then_inc(s_std, 1)
                for k in range(KT):
                    act.wait_ge(s_lnT, k + 1)
                    act.activation(lnT[:, k, :], LB[k], ACT.Copy).then_inc(s_lnTc, 1)
                act.wait_ge(s_wk, 32)
                for c in range(NCT + 1):
                    if c < NCT:
                        act.wait_ge(s_k, c + 1)
                        act.activation(kh[:, 512 * c:512 * c + 512], KB[c % 2], ACT.Identity,
                                       bias=bkc[:, 0:1]).then_inc(s_kh, 1)
                    if c >= 1:
                        act.wait_ge(s_kr, c)
                        act.activation(km[:, 512 * c - 512:512 * c], kr[:, (c - 1) % 2, :], ACT.Copy).then_inc(s_km, 1)
                    if 3 <= c < 3 + RT:
                        act.wait_ge(s_q, c - 2)
                        act.activation(qf[:, c - 3, :], QB[(c - 3) % 2], ACT.Copy).then_inc(s_qf, 1)

            @block.vector
            def _(dve):
                dve.memset(stack[SROWS:MROWS, 0, 0, 0:512], 1.0).then_inc(s_vg1, 1)
                dve.memset(Vg[:, :, :], 1.0).then_inc(s_vg1, 1)
                dve.wait_ge(s_x, 16)
                for R in range(RT):
                    link_dve(dve.bn_stats(bst[:, R, :], X[:, R, :]))
                    link_dve(dve.bn_aggr(mv[:, R, :], bst[:, R, :]))
                dve.tensor_scalar(ve[:, :], mv[:, :, 1], 1e-5, None, ALU.add).then_inc(s_var, 1)
                dve.wait_ge(s_std, 1)
                link_dve(dve.reciprocal(rs[:, :], sd[:, :]))
                for R in range(RT):
                    dve.tensor_scalar(lnx[:, R, :], X[:, R, :], mv[:, R, 0:1], rs[:, R:R + 1],
                                      ALU.subtract, ALU.mult).then_inc(s_ln, 1)
                for c in range(NCT + 1):
                    if c < NCT:
                        dve.wait_ge(s_ct, c + 1)
                        dve.tensor_copy(ctxT[:, 0, 512 * c:512 * c + 512], CB[c % 2]).then_inc(s_ctc, 1)
                    if c >= 1:
                        dve.wait_ge(s_kh, c)
                        if c >= 3:
                            dve.wait_ge(s_kl, c - 2)
                        dve.scalar_tensor_tensor(out=kr[:, (c - 1) % 2, :], in0=KB[(c - 1) % 2], scalar=bkc[:, 0:1],
                                                 in1=kh[:, 512 * c - 512:512 * c], op0=ALU.add,
                                                 op1=ALU.subtract).then_inc(s_kr, 1)
                    if c in (5, NCT):
                        dve.wait_ge(s_qf, 2 if c == 5 else RT)
                        t = slice(0, 2) if c == 5 else slice(2, 4)
                        link_dve(dve.tensor_copy(qh[:, t, :], qf[:, t, :]))
                        link_dve(dve.tensor_tensor(qf[:, t, :], qf[:, t, :], qh[:, t, :], ALU.subtract))
                        link_dve(dve.tensor_copy(qm[:, t, :], qf[:, t, :]))
                        dve.tensor_tensor(ql[:, t, :], qf[:, t, :], qm[:, t, :], ALU.subtract).then_inc(s_qp, 1)
            @block.tensor
            def _(pe):
                pe.wait_ge(s_const, 2)
                pe.wait_ge(s_ln, RT)
                for k in range(KT):
                    for R in range(RT):
                        mm = pe.transpose(LB[k][:, P * R:P * R + P], lnx[:, R, P * k:P * k + P], identf[:, :])
                    mm.then_inc(s_lnT, 1)
                pe.wait_ge(s_wk, 32)
                for c in range(NCT + 1):
                    if c < NCT:
                        if c % 2 == 0:
                            pe.wait_ge(s_ctx[c // 2], 16)
                        if c >= 2:
                            pe.wait_ge(s_ctc, c - 1)
                        for i in range(4):
                            mm = pe.transpose(CB[c % 2][:, P * i:P * i + P], ctxn[:, 0, 4 * c + i, :], identf[:, :])
                        mm.then_inc(s_ct, 1)
                    if c >= 1:
                        pe.wait_ge(s_ctc, c)
                        if c >= 3:
                            pe.wait_ge(s_kr, c - 2)
                        pe.matmul(KB[(c - 1) % 2], wk[:, 0:P], ctxT[:, 0, 512 * c - 512:512 * c],
                                  start=True, stop=True).then_inc(s_k, 1)
                    if 2 <= c < 2 + RT:
                        R = c - 2
                        if R == 0:
                            pe.wait_ge(s_wq, 32)
                            pe.wait_ge(s_lnTc, KT)
                        if R >= 2:
                            pe.wait_ge(s_qf, R - 1)
                        for k in range(KT):
                            pe.matmul(QB[R % 2], lnT[:, k, P * R:P * R + P], wq[:, k, :], start=(k == 0), stop=False)
                        pe.matmul(QB[R % 2], onesf[0:1, :], bqr[:, :], start=False, stop=True).then_inc(s_q, 1)

        with nc.Block() as block:
            @block.sync
            def _(sp):
                load_slots_sp(sp, 0, 1)
                sp.wait_ge(s_auxd, AUX_NO["C", 7] + 1)
                sp.dma_start(stack[SROWS:MROWS, 1, :, :], stack[SROWS:MROWS, 0, :, :]).then_inc(s_ones1, 16)
                for g in range(1, NG):
                    for half in range(2):
                        load_slots_sp(sp, g, half)

            @block.gpsimd
            def _(pool):
                load_slots_pool(pool, 0, 1)
                for s in range(S0, SEND):
                    for kind, i in aux_of(s):
                        if kind == "K":
                            c = i % 8
                            pool.wait_ge(s_auxd, AUX_NO[kind, i] + 1)
                            sl = slice(512 * c, 512 * c + 512)
                            if i >= 8:
                                for par in range(2):
                                    pool.wait_ge(s_stack[par][c // 4], SPI * (i // 8))
                                    pool.wait_ge(s_stackp[par][c // 4], PLI * (i // 8))
                            link_pool(pool.tensor_copy(km[:, sl], kr[:, i % 2, :]))
                            pool.tensor_tensor(kl[:, sl], kr[:, i % 2, :], km[:, sl], ALU.subtract).then_inc(s_kl, 1)
                    for g in range(1, NG):
                        if s == SPG * (g - 1) - LEAD - 25:
                            group_rows(pool, g)
                    g, r = divmod(s + 2 * SPG, SPG)
                    if s == -28:
                        load_slots_pool(pool, 1, 0)
                        load_slots_pool(pool, 1, 1)
                    if s >= 0 and r == 16 and g < NG:
                        load_slots_pool(pool, g, 0)
                    if s > 0 and r == 0 and g - 1 < NG:
                        load_slots_pool(pool, g - 1, 1)

            @block.scalar
            def _(act):
                for s in range(S0, SEND + 8):
                    if 0 <= s < SEND:
                        act.wait_ge(s_st, s + 1)
                        if s >= 3:
                            act.wait_ge(s_pv, s - 2)
                        act.activation(PT[:, s % 3, :], ST[s % 2], ACT.Exp, scale=SCALE).then_inc(s_exp, 1)
                    if s > SPG and s % SPG == 1:
                        g = s // SPG - 1
                        act.wait_ge(s_pv, SPG * (g + 1))
                        if g >= 1:
                            act.wait_ge(s_auxd, AUX_NO["OT", g - 1] + 1)
                        act.activation(OTs[:, :], ACC[:, 0:L], ACT.Copy).then_inc(s_acc, 1)
                    for kind, i in aux_of(s):
                        if kind == "C":
                            act.wait_ge(s_aux, AUX_NO[kind, i] + 1)
                            act.activation(ctxT[:, 1, 512 * i:512 * i + 512], AUXB, ACT.Copy).then_inc(s_auxd, 1)
                        if kind == "K":
                            half, c = (i // 8) % 2, i % 8
                            act.wait_ge(s_aux, AUX_NO[kind, i] + 1)
                            if i >= 8:
                                for par in range(2):
                                    act.wait_ge(s_stack[par][c // 4], SPI * (i // 8))
                                    act.wait_ge(s_stackp[par][c // 4], PLI * (i // 8))
                            act.activation(kh[:, 512 * c:512 * c + 512], AUXB, ACT.Identity,
                                           bias=bkc[:, half:half + 1]).then_inc(s_khd, 1)
                        if kind == "V":
                            hf, v = divmod(i, 8)
                            act.wait_ge(s_aux, AUX_NO[kind, i] + 1)
                            for gg in range(2):
                                if hf >= 1:
                                    act.wait_ge(s_pv, SPG * (2 * hf - 2 + gg) + 4 * v + 4)
                                o = Vg[:, gg, 4 * v * GH * VW:(4 * v + 4) * GH * VW].rearrange(
                                    "p (t j d) -> p t j d", t=4, d=VW)
                                src = AUXB.rearrange("p (t g j d) -> p t g j d", t=4, g=2, d=DH)
                                ins = act.activation(o[:, :, :, 0:DH], src[:, :, gg], ACT.Copy)
                            ins.then_inc(s_auxd, 1)

            @block.vector
            def _(dve):
                for s in range(S0, SEND + 8):
                    for n in units_of(s):
                        g, u = divmod(n, UPG)
                        dve.wait_ge(s_sm, n + 1)
                        dve.tensor_reduce(mx[:, g % 2, u % 8, u // 8:u // 8 + 1], max_bank(n), AX.X,
                                          ALU.max).then_inc(s_red, 1)
                        if u == UPG - 1:
                            dve.wait_ge(s_red, n + 1)
                            q = Qg[:, g % 2, :, :]
                            link_dve(dve.tensor_reduce(nm[:, :], mx[:, g % 2, :, :], AX.X, ALU.max, negate=True))
                            link_dve(dve.tensor_copy(q[:, :, SROWS], nm[:, :]))
                            link_dve(dve.tensor_tensor(nr[:, :], nm[:, :], q[:, :, SROWS], ALU.subtract))
                            link_dve(dve.tensor_copy(q[:, :, SROWS + 1], nr[:, :]))
                            dve.tensor_tensor(q[:, :, SROWS + 2], nr[:, :], q[:, :, SROWS + 1],
                                              ALU.subtract).then_inc(s_mp, 1)
                    for kind, i in aux_of(s):
                        a = AUX_NO[kind, i]
                        if kind == "K":
                            dve.wait_ge(s_khd, i - 7)
                            if i >= 2:
                                dve.wait_ge(s_kl, i - 1)
                            half, c = (i // 8) % 2, i % 8
                            dve.scalar_tensor_tensor(out=kr[:, i % 2, :], in0=AUXB, scalar=bkc[:, half:half + 1],
                                                     in1=kh[:, 512 * c:512 * c + 512], op0=ALU.add,
                                                     op1=ALU.subtract).then_inc(s_auxd, 1)
                        if kind in ("QS", "QT"):
                            dve.wait_ge(s_aux, a + 1)
                            dve.tensor_copy((QS if kind == "QS" else QT)[:, i % 2, :],
                                            AUXB.bitcast(BF16)).then_inc(s_auxd, 1)
                        if kind == "OT":
                            b, hg = divmod(i, 4)
                            dve.wait_ge(s_aux, a + 1)
                            o = AUXB[:, 0:2 * P].rearrange("p (q j d) -> p q j d", q=2, d=32)
                            link_dve(dve.reciprocal(rec[:, :, :], o[:, :, :, DH]))
                            dst = att[:, 2 * b:2 * b + 2, 64 * hg:64 * hg + 64].rearrange("p q (j d) -> p q j d", d=DH)
                            for q in range(2):
                                ins = dve.tensor_tensor(dst[:, q], o[:, q, :, 0:DH],
                                                        rec[:, q, :].unsqueeze(2).broadcast_to([P, GH, DH]), ALU.mult)
                            ins.then_inc(s_auxd, 1)

            @block.tensor
            def _(pe):
                pe.wait_ge(s_w1, 64)
                pe.wait_ge(s_ones, 16)
                for s in range(S0, SEND + 8):
                    if 0 <= s < SEND:
                        g, t = divmod(s, SPG)
                        if s >= 2:
                            pe.wait_ge(s_exp, s - 1)
                        if t == 0:
                            pe.wait_ge(s_auxd, AUX_NO["QT", g] + 1)
                        if s == SPG:
                            pe.wait_ge(s_ones1, 16)
                        for j in range(GH):
                            mm = pe.matmul(ST[s % 2][:, j // 2, 256 * (j % 2):256 * (j % 2) + 256],
                                           stack[0:MROWS, g % 2, j, P * t:P * t + P],
                                           QT[0:MROWS, g % 2, L * j:L * j + L], start=True, stop=True)
                        mm.then_inc(s_st, 1)
                    if 2 <= s < SEND + 2:
                        g, t = divmod(s - 2, SPG)
                        pe.wait_ge(s_exp, s - 1)
                        if t == 0 and g >= 1:
                            pe.wait_ge(s_acc, g)
                        if t % 4 == 0:
                            pe.wait_ge(s_auxd, AUX_NO["V", 8 * (g // 2) + t // 4] + 1)
                        for j in range(GH):
                            v0 = (GH * t + j) * VW
                            mm = pe.matmul(ACC[32 * j:32 * j + 32, 0:L], Vg[:, g % 2, v0:v0 + 32],
                                           PT[:, (s - 2) % 3, L * j:L * j + L], start=(t == 0), stop=(t == SPG - 1))
                        mm.then_inc(s_pv, 1)
                    for n in units_of(s):
                        g, u = divmod(n, UPG)
                        c, r = divmod(u, 8)
                        if u == 0:
                            pe.wait_ge(s_auxd, AUX_NO["QS", g] + 1)
                        if u % 32 == 0:
                            pe.wait_ge(s_stack[g % 2][u // 32], SPI * (g // 2 + 1))
                            pe.wait_ge(s_stackp[g % 2][u // 32], PLI * (g // 2 + 1))
                        m = 6 if n < UPG else 2
                        if n >= m:
                            pe.wait_ge(s_red, n - m + 1)
                        pe.matmul(max_bank(n), QS[0:SROWS, g % 2, P * r:P * r + P],
                                  stack[0:SROWS, g % 2, r // 2, 512 * c:512 * c + 512],
                                  start=True, stop=True).then_inc(s_sm, 1)
                    for kind, i in aux_of(s):
                        a = AUX_NO[kind, i]
                        if a:
                            pe.wait_ge(s_auxd, a)
                        if kind == "C":
                            if i % 2 == 0:
                                pe.wait_ge(s_ctx[4 + i // 2], 16)
                            for q in range(4):
                                mm = pe.transpose(AUXB[:, P * q:P * q + P], ctxn[:, 1, 4 * i + q, :], identf[:, :])
                        if kind == "K":
                            b, half = divmod(i // 8, 2)
                            c = i % 8
                            mm = pe.matmul(AUXB, wk[:, P * half:P * half + P], ctxT[:, b, 512 * c:512 * c + 512],
                                           start=True, stop=True)
                        if kind == "V":
                            b, half = divmod(i // 8, 2)
                            for q in range(4):
                                t = 4 * (i % 8) + q
                                mm = pe.matmul(AUXB[:, P * q:P * q + P], ctxT[:, b, P * t:P * t + P],
                                               wv[:, P * half:P * half + P], start=True, stop=True)
                        if kind in ("QS", "QT"):
                            pe.wait_ge(s_qg if kind == "QS" else s_mp, i + 1)
                            for r in range(2 * GH):
                                mm = pe.transpose(AUXB.bitcast(BF16)[:, P * r:P * r + P], Qg[:, i % 2, r, :],
                                                  identb[:, :])
                        if kind == "OT":
                            pe.wait_ge(s_acc, i + 1)
                            for q in range(2):
                                mm = pe.transpose(AUXB[:, P * q:P * q + P], OTs[:, P * q:P * q + P], identf[:, :])
                        mm.then_inc(s_aux, 1)

        def store_x(src):
            with nc.Block() as block:
                @block.sync
                def _(sp):
                    sp.dma_start(out.rearrange("b (r p) d -> p (b r) d", p=P), src).then_inc(s_out, 16)
                    sp.wait_ge(s_out, 16)
                    if stop in ("x1", "x2"):
                        sp.wait_ge(s_wl3, 128 if stop == "x2" else 112)
                        sp.wait_ge(s_wl4, 128)

        if stop == "att":
            return store_x(att[:, :, :])

        bqkv = rows[:, 0:3 * D]
        b_out2 = rows[:, 3 * D:4 * D]
        b_q3 = rows[:, 4 * D:5 * D]
        b_o3 = rows[:, 5 * D:6 * D]

        qls = small[:, 0:64].rearrange("p (r h) -> p r h", h=H)
        mkx = small[:, 64:128]
        kls = small[:, 128:160].rearrange("p (b h) -> p b h", h=H)
        nmall = small[:, 160:224].rearrange("p (r h) -> p r h", h=H)
        t0 = small[:, 224:288].rearrange("p (r h) -> p r h", h=H)
        t1 = small[:, 288:352].rearrange("p (r h) -> p r h", h=H)
        t2 = small[:, 352:416].rearrange("p (r h) -> p r h", h=H)
        t3 = small[:, 416:480].rearrange("p (r h) -> p r h", h=H)
        mkc = small[0:64, 480:481]
        mkr = small[0:1, 484:516]
        nrs = small[:, 516:524].rearrange("p (q j) -> p q j", j=GH)
        bkv = rows[:, 6 * D:6 * D + 128]

        s_wl = sem("s_wl")
        s_wp = sem("s_wp")
        s_wl3 = sem("s_wl3")
        s_wl4 = sem("s_wl4")
        s_wT = sem("s_wT")
        s_wTc = sem("s_wTc")
        s_cst2 = sem("s_cst2")
        s_attb = sem("s_attb")
        s_aT = sem("s_aT")
        s_aTc = sem("s_aTc")
        s_op = sem("s_op")
        s_xn = sem("s_xn")
        s_qkv = sem("s_qkv")
        s_qkvc = sem("s_qkvc")
        s_xt = sem("s_xt")
        s_xtc = sem("s_xtc")
        s_sq = sem("s_sq")
        s_f = sem("s_f")
        s_fr = sem("s_fr")
        s_fs = sem("s_fs")
        s_fe = sem("s_fe")
        s_mk = sem("s_mk")
        s_mkT = sem("s_mkT")
        s_mkc = sem("s_mkc")
        s_p = sem("s_p")
        s_ph = sem("s_ph")
        s_pc = sem("s_pc")
        s_b = sem("s_b")

        PB = [ps[:, i, 0:D] for i in (0, 1, 6, 7)]

        def ln_dve(dve, n, eps):
            for R in range(RT):
                link_dve(dve.bn_stats(bst[:, R, :], X[:, R, :]))
                link_dve(dve.bn_aggr(mv[:, R, :], bst[:, R, :]))
            dve.tensor_scalar(ve[:, :], mv[:, :, 1], eps, None, ALU.add).then_inc(s_var, 1)
            dve.wait_ge(s_std, n + 1)
            link_dve(dve.reciprocal(rs[:, :], sd[:, :]))
            for R in range(RT):
                dve.tensor_scalar(lnx[:, R, :], X[:, R, :], mv[:, R, 0:1], rs[:, R:R + 1],
                                  ALU.subtract, ALU.mult).then_inc(s_ln, 1)

        def ln_act(act, n):
            act.wait_ge(s_var, n + 1)
            act.activation(sd[:, :], ve[:, :], ACT.Sqrt).then_inc(s_std, 1)

        def rows_T_pe(pe, n, src):
            for k in range(KT):
                for R in range(RT):
                    mm = pe.transpose(LB[k][:, P * R:P * R + P], src[:, R, P * k:P * k + P], identf[:, :])
                mm.then_inc(s_lnT, 1)

        def rows_T_act(act, n):
            for k in range(KT):
                act.wait_ge(s_lnT, KT * n + k + 1)
                act.activation(lnT[:, k, :], LB[k], ACT.Copy).then_inc(s_lnTc, 1)

        def project_pe(pe, n, w, brow):
            for R in range(RT):
                o = PB[R]
                for k in range(KT):
                    pe.matmul(o, lnT[:, k, P * R:P * R + P], w[:, k, :], start=(k == 0), stop=False)
                pe.matmul(o, onesf[0:1, :], brow, start=False, stop=True).then_inc(s_op, 1)

        def residual_dve(dve, n):
            for R in range(RT):
                dve.wait_ge(s_op, RT * n + R + 1)
                link_dve(dve.tensor_tensor(X[:, R, :], X[:, R, :], PB[R],
                                           ALU.add))

        WB = [ps[:, 2, :], ps[:, 3, :]]
        with nc.Block() as block:
            @block.sync
            def _(sp):
                sp.dma_start(wraw[:, 0:6, :], t_in["L0_attn_Wqkv_w"].rearrange("(w p) k -> p w k", p=P)).then_inc(s_wl, 16)
                sp.dma_start(wraw[:, 6:8, :], t_in["L0_attn_out_w"].rearrange("(w p) k -> p w k", p=P)).then_inc(s_wl, 16)
                sp.dma_start(bqkv, t_in["L0_attn_Wqkv_b"].rearrange("(a n) -> a n", a=1)).then_inc(s_wl, 16)
                sp.dma_start(b_out2, t_in["L0_attn_out_b"].rearrange("(a n) -> a n", a=1)).then_inc(s_wl, 16)
                sp.dma_start(b_q3, t_in["L0_ffn_qb"].rearrange("(a n) -> a n", a=1)).then_inc(s_wl3, 16)
                sp.dma_start(b_o3, t_in["L0_ffn_ob"].rearrange("(a n) -> a n", a=1)).then_inc(s_wl3, 16)
                sp.dma_start(bkv[:, 0:64], t_in["L0_ffn_kb"].rearrange("(a n) -> a n", a=1)).then_inc(s_wl3, 16)
                sp.dma_start(bkv[:, 64:128], t_in["L0_ffn_vb"].rearrange("(a n) -> a n", a=1)).then_inc(s_wl3, 16)
                sp.dma_start(wq[:, :, :], t_in["L0_ffn_qw"].rearrange("(k p) n -> p k n", p=P)).then_inc(s_wl3, 16)
                kvw = t_in["L0_ffn_kw"].rearrange("(k p) n -> p k n", p=P)
                sp.dma_start(wk.rearrange("p (k n) -> p k n", k=4)[:, 0:2, :], kvw).then_inc(s_wl3, 16)
                sp.dma_start(wk.rearrange("p (k n) -> p k n", k=4)[:, 2:4, :],
                             t_in["L0_ffn_vw"].rearrange("(k p) n -> p k n", p=P)).then_inc(s_wl3, 16)
                for e in range(E):
                    sp.dma_start(w1[:, e, :, :], t_in["L0_ffn_w1"][e].rearrange("(k p) f -> p k f", p=P)).then_inc(s_wl4, 16)
                sp.wait_ge(s_cst2, 1)
                for j in range(8):
                    sp.dma_start(projb[DH * j:DH * j + DH, 0, M * j:M * j + M],
                                 t_in["L0_attn_proj"].rearrange("m d -> d m"),
                                 allow_slow_non_contiguous=True).then_inc(s_wp, 16)

            @block.gpsimd
            def _(pool):
                pool.memset(projb[:, :, :], 0.0).then_inc(s_cst2, 1)
                pool.memset(V2[:, :, :], 1.0).then_inc(s_b, 1)
                pool.wait_ge(s_cst2, 1)
                link_pool(pool.memset(projb[:, 1, :], -0.125))
                dg = projb[:, 1, :].rearrange("p (j m) -> p j m", m=M)
                link_pool(pool.affine_select(out=dg, in_=dg, compare_op=ALU.is_ge, fill=0.0, base=0,
                                             pattern=[[-DH, 8], [0, M]], channel_multiplier=1))
                pool.affine_select(out=dg, in_=dg, compare_op=ALU.is_ge, fill=0.0, base=DH - 1,
                                   pattern=[[DH, 8], [0, M]], channel_multiplier=-1).then_inc(s_cst2, 1)
                link_pool(pool.memset(maskq[:, :, :], 0.0))
                link_pool(pool.memset(maskk[:, :, :], 0.0))
                link_pool(pool.memset(wmask[:, :, :], 1.0))
                link_pool(pool.affine_select(out=maskq[:, :, :], in_=maskq[:, :, :], compare_op=ALU.is_ge,
                                             fill=-40000.0, base=0, pattern=[[P, 2], [-1, L]], channel_multiplier=1))
                link_pool(pool.affine_select(out=maskk[:, :, :], in_=maskk[:, :, :], compare_op=ALU.is_ge,
                                             fill=-40000.0, base=0, pattern=[[-P, 2], [1, L]], channel_multiplier=-1))
                link_pool(pool.affine_select(out=wmask[:, :, :], in_=wmask[:, :, :], compare_op=ALU.is_ge,
                                             fill=0.0, base=0, pattern=[[-P, 2], [1, L]], channel_multiplier=-1))
                link_pool(pool.affine_select(out=maskq[:, :, :], in_=maskq[:, :, :], compare_op=ALU.is_ge,
                                             fill=-40000.0, base=128, pattern=[[-P, 2], [1, L]],
                                             channel_multiplier=-1))
                link_pool(pool.affine_select(out=maskk[:, :, :], in_=maskk[:, :, :], compare_op=ALU.is_ge,
                                             fill=-40000.0, base=128, pattern=[[P, 2], [-1, L]],
                                             channel_multiplier=1))
                pool.tensor_copy(identh[:, :], identf[:, :]).then_inc(s_cst2, 1)
                pool.wait_ge(s_wT, 8)
                pool.memset(QN[:, :, :, SROWS:P], 0.0).then_inc(s_b, 1)
                pool.memset(KN[:, :, :, SROWS:P], 1.0).then_inc(s_b, 1)
                def slot(T, n, w=DH):
                    return T[:, :, :, w * n:w * n + w]
                pool.wait_ge(s_ph, 1)
                for n in (2, 5):
                    for R in range(RT):
                        pool.tensor_copy(slot(QN, n)[:, R], slot(QN, 0)[:, R]).then_inc(s_pc, 1)
                pool.wait_ge(s_ph, 2)
                for n in (1, 4):
                    for R in range(RT):
                        pool.tensor_copy(slot(KN, n)[:, R], slot(KN, 0)[:, R]).then_inc(s_pc, 1)
                pool.wait_ge(s_p, 2)
                for R in range(RT):
                    pool.tensor_copy(slot(QN, 3)[:, R], slot(QN, 1)[:, R]).then_inc(s_pc, 1)
                    pool.tensor_copy(slot(KN, 3)[:, R], slot(KN, 2)[:, R]).then_inc(s_pc, 1)
                pool.wait_ge(s_qkv, 2 * RT)
                pool.memset(FQ[:, :, :, 5 * M:P], 0.0).then_inc(s_b, 1)
                pool.memset(FK[:, :, :, 5 * M:P], 0.0).then_inc(s_b, 1)
                pool.wait_ge(s_p, 3)
                for R in range(RT):
                    pool.tensor_copy(slot(FQ, 2, M)[:, R], slot(FQ, 0, M)[:, R]).then_inc(s_pc, 1)
                    pool.tensor_copy(slot(FQ, 3, M)[:, R], slot(FQ, 1, M)[:, R]).then_inc(s_pc, 1)
                pool.wait_ge(s_p, 4)
                for R in range(RT):
                    pool.tensor_copy(slot(FK, 1, M)[:, R], slot(FK, 0, M)[:, R]).then_inc(s_pc, 1)
                    pool.tensor_copy(slot(FK, 4, M)[:, R], slot(FK, 0, M)[:, R]).then_inc(s_pc, 1)
                    pool.tensor_copy(slot(FK, 3, M)[:, R], slot(FK, 2, M)[:, R]).then_inc(s_pc, 1)

            @block.scalar
            def _(act):
                rows_T_act(act, 1)
                for w in range(8):
                    act.wait_ge(s_wT, w + 1)
                    o = wqkvT[:, :, P * w:P * w + P] if w < 6 else woT2[:, :, P * (w - 6):P * (w - 6) + P]
                    act.activation(o, WB[w % 2][:, 0:2 * P].rearrange("p (k n) -> p k n", k=KT), ACT.Copy).then_inc(s_wTc, 1)
                ln_act(act, 1)
                rows_T_act(act, 2)
                for R in range(RT):
                    act.wait_ge(s_qkv, 2 * R + 1)
                    act.activation(QK[:, R, :], ps[:, 2 * (R % 2), :], ACT.Copy).then_inc(s_qkvc, 1)
                    act.wait_ge(s_qkv, 2 * R + 2)
                    if R == 0:
                        act.wait_ge(s_b, 1)
                    act.activation(V2[:, R, 0:H * VW].rearrange("p (h d) -> p h d", d=VW)[:, :, 0:DH],
                                   ps[:, 2 * (R % 2) + 1, 0:D].rearrange("p (h d) -> p h d", d=DH),
                                   ACT.Copy).then_inc(s_qkvc, 1)
                act.wait_ge(s_qkvc, 2 * RT)
                for side, T in enumerate((QN, KN)):
                    act.activation(T[:, :, :, 0:DH], QK[:, :, D * side:D * side + D].rearrange(
                        "p r (h d) -> p r h d", d=DH), ACT.Copy).then_inc(s_ph, 1)
                for n in range(4):
                    side, k = divmod(n, KT)
                    act.wait_ge(s_xt, n + 1)
                    act.activation(xsq[:, side, k, :], ps[:, 4 + n, :], ACT.Square).then_inc(s_sq, 1)
                for side, f in enumerate((fq, fk)):
                    act.wait_ge(s_fs, side + 1)
                    act.activation(f[:, :, :, :], f[:, :, :, :], ACT.Exp).then_inc(s_fe, 1)

            @block.vector
            def _(dve):
                dve.wait_ge(s_w1, 64)
                for R in range(RT):
                    ins = dve.tensor_tensor(att[:, R, :], att[:, R, :], bvb[:, :], ALU.add)
                ins.then_inc(s_attb, 1)
                residual_dve(dve, 0)
                ln_dve(dve, 1, 1e-5)
                dve.wait_ge(s_cst2, 3)
                sc = acc[:, 0:2, :]
                link_dve(dve.tensor_scalar(sc, maskk[:, :, :], 0.0, 0.25, ALU.is_equal, ALU.mult))
                link_dve(dve.tensor_tensor(wmask[:, :, :], wmask[:, :, :], sc, ALU.subtract))
                for n in range(4):
                    side, k = divmod(n, KT)
                    dve.wait_ge(s_sq, n + 1)
                    dve.tensor_scalar(xT[:, side, k, :], ps[:, 4 + n, :], 0.5, None, ALU.mult).then_inc(s_xtc, 1)
                for side, f in enumerate((fq, fk)):
                    for R in range(RT):
                        pf = ps[:, R, 0:H * M].rearrange("p (h m) -> p h m", m=M)
                        dve.wait_ge(s_f, RT * side + R + 1)
                        if side == 0:
                            link_dve(dve.tensor_reduce(qls[:, R, :], pf, AX.X, ALU.max))
                            ins = dve.tensor_tensor(f[:, R, :, :], pf,
                                                    qls[:, R, :].unsqueeze(2).broadcast_to([P, H, M]), ALU.subtract)
                            ins.then_inc(s_fr, 1)
                        else:
                            dve.tensor_reduce(mkx[:, H * R:H * R + H], pf, AX.X, ALU.max).then_inc(s_mk, 1)
                    if side == 0:
                        dve.wait_ge(s_fr, RT)
                        dve.sem_inc(s_fs, 1)
                dve.wait_ge(s_mkT, 1)
                dve.tensor_reduce(mkc, ps[0:64, 4, 0:P], AX.X, ALU.max).then_inc(s_mkc, 1)
                dve.wait_ge(s_mkT, 2)
                dve.tensor_reduce(mkr.rearrange("p (b h) -> p b h", b=B),
                                  ps[0:1, 5, 0:64].rearrange("p (b q h) -> p b h q", b=B, q=2),
                                  AX.X, ALU.max).then_inc(s_mkc, 1)
                dve.wait_ge(s_mkT, 3)
                link_dve(dve.tensor_copy(kls, ps[:, 6, 0:32].rearrange("p (b h) -> p b h", b=B)))
                for R in range(RT):
                    pf = ps[:, R, 0:H * M].rearrange("p (h m) -> p h m", m=M)
                    ins = dve.tensor_tensor(fk[:, R, :, :], pf,
                                            kls[:, R // 2, :].unsqueeze(2).broadcast_to([P, H, M]), ALU.subtract)
                    link_dve(ins)
                dve.sem_inc(s_fs, 1)
                for side, (T, sm_, sl_) in enumerate(((QN, 1, 4), (KN, 2, 5))):
                    dve.wait_ge(s_ph, side + 1)
                    q = QK[:, :, D * side:D * side + D].rearrange("p r (h d) -> p r h d", d=DH)
                    for R in range(RT):
                        link_dve(dve.tensor_tensor(q[:, R], q[:, R], T[:, R, :, 0:DH], ALU.subtract))
                        link_dve(dve.tensor_copy(T[:, R, :, DH * sm_:DH * sm_ + DH], q[:, R]))
                        ins = dve.tensor_tensor(T[:, R, :, DH * sl_:DH * sl_ + DH], q[:, R],
                                                T[:, R, :, DH * sm_:DH * sm_ + DH], ALU.subtract)
                        if R < RT - 1:
                            link_dve(ins)
                    ins.then_inc(s_p, 1)
                dve.wait_ge(s_qkv, 2 * RT)
                dve.wait_ge(s_b, 5)
                for side, (f, T, h_, m_, l_) in enumerate(((fq, FQ, 0, 1, None), (fk, FK, 0, 2, None))):
                    dve.wait_ge(s_fe, side + 1)
                    link_dve(dve.tensor_scalar(f[:, :, :, :], f[:, :, :, :], 1e-4, None, ALU.add))
                    for R in range(RT):
                        link_dve(dve.tensor_copy(T[:, R, :, 0:M], f[:, R]))
                        link_dve(dve.tensor_tensor(f[:, R], f[:, R], T[:, R, :, 0:M], ALU.subtract))
                        link_dve(dve.tensor_copy(T[:, R, :, M * m_:M * m_ + M], f[:, R]))
                        lo = T[:, R, :, 4 * M:5 * M] if side == 0 else FKL[:, R]
                        ins = dve.tensor_tensor(lo, f[:, R], T[:, R, :, M * m_:M * m_ + M], ALU.subtract)
                        if R < RT - 1:
                            link_dve(ins)
                    ins.then_inc(s_p, 1)

            @block.tensor
            def _(pe):
                pe.wait_ge(s_attb, 1)
                rows_T_pe(pe, 1, att)
                pe.wait_ge(s_lnTc, 2 * KT)
                project_pe(pe, 0, wo, bor[:, :])
                pe.wait_ge(s_wl, 64)
                for w in range(8):
                    if w >= 2:
                        pe.wait_ge(s_wTc, w - 1)
                    for k in range(KT):
                        mm = pe.transpose(WB[w % 2][:, P * k:P * k + P], wraw[:, w, P * k:P * k + P], identf[:, :])
                    mm.then_inc(s_wT, 1)
                pe.wait_ge(s_ln, 2 * RT)
                rows_T_pe(pe, 2, lnx)
                pe.wait_ge(s_lnTc, 3 * KT)
                pe.wait_ge(s_wp, 16 * 8)
                pe.wait_ge(s_wTc, 8)
                for R in range(RT):
                    if R >= 2:
                        pe.wait_ge(s_qkvc, 2 * R - 2)
                    for part, (lo, hi) in enumerate(((0, 2 * D), (2 * D, 3 * D))):
                        o = ps[:, 2 * (R % 2) + part, 0:hi - lo]
                        for k in range(KT):
                            pe.matmul(o, lnT[:, k, P * R:P * R + P], wqkvT[:, k, lo:hi], start=(k == 0), stop=False)
                        pe.matmul(o, onesf[0:1, :], bqkv[:, lo:hi], start=False, stop=True).then_inc(s_qkv, 1)
                pe.wait_ge(s_qkvc, 2 * RT)
                for n in range(4):
                    side, k = divmod(n, KT)
                    for R in range(RT):
                        mm = pe.transpose(ps[:, 4 + n, P * R:P * R + P],
                                          QK[:, R, D * side + P * k:D * side + P * k + P], identf[:, :])
                    mm.then_inc(s_xt, 1)
                pe.wait_ge(s_xtc, 4)
                pe.wait_ge(s_sq, 4)
                pe.wait_ge(s_cst2, 2)
                for side in range(2):
                    for R in range(RT):
                        if side == 1:
                            pe.wait_ge(s_fr, R + 1)
                        for k in range(KT):
                            o = ps[:, R, 8 * M * k:8 * M * k + 8 * M]
                            pe.matmul(o, xT[:, side, k, P * R:P * R + P], projb[:, 0, :], start=True, stop=False)
                            mm = pe.matmul(o, xsq[:, side, k, P * R:P * R + P], projb[:, 1, :],
                                           start=False, stop=True)
                        mm.then_inc(s_f, 1)
                pe.wait_ge(s_mk, RT)
                pe.transpose(ps[0:64, 4, 0:P], mkx, identf[:, :]).then_inc(s_mkT, 1)
                pe.wait_ge(s_mkc, 1)
                pe.transpose(ps[0:1, 5, 0:64], mkc, identf[0:64, 0:64]).then_inc(s_mkT, 1)
                pe.wait_ge(s_mkc, 2)
                pe.matmul(ps[:, 6, 0:32], onesf[0:1, :], mkr, start=True, stop=True).then_inc(s_mkT, 1)

        if stop == "x1":
            return store_x(X[:, :, :])

        ts = {n: sem(n) for n in ("a_t", "a_td_act", "a_td_dve", "a_s", "a_sr", "a_mp", "a_st", "a_exp", "a_gm",
                                  "a_pv", "a_pg", "a_acc", "a_accg")}
        base = {n: 0 for n in ts}

        def attention(masked):
            def turn_T(i):
                out = []
                if 0 <= i - 1 < NG:
                    out += [("QT", i - 1, "dve")]
                if i < NG:
                    out += [("Q", i, "dve"), ("K", i, "act")]
                if i >= 2:
                    out += [("O", i - 2, "dve")]
                if masked and i < NG:
                    out += [("FQ", i, "act")]
                if masked and i >= 2:
                    out += [("OG", i - 2, "dve")]
                if masked and i < NG:
                    out += [("FK", i, "act"), ("FKL", i, "act")]
                return out
            uses = [u for i in range(NG + 2) for u in turn_T(i)]
            use_no = {u[:2]: n for n, u in enumerate(uses)}

            def after(name, n):
                return ts[name], base_at[name] + n

            def read(n):
                who = uses[n][2]
                return after("a_td_" + who, sum(u[2] == who for u in uses[:n + 1]))

            def bank(n):
                return ps[:, n % 2, :]

            base_at = dict(base)
            NKJ = GH if masked else 1
            PTn = PT[:, 0:2, :]
            src = {"Q": QN, "QT": QN, "K": KN, "FQ": FQ, "FK": FK}
            dst = {"Q": QS, "QT": QT, "K": KSg, "FQ": FQT, "FK": FKT, "FKL": FKLT}

            sg = []
            for i in range(NG + 1):
                if i < NG:
                    sg += [("S", i, 0), ("S", i, 1)]
                if masked and i >= 1:
                    sg += [("G", i - 1, 0), ("G", i - 1, 1)]
            sg_no = {u: n for n, u in enumerate(sg)}

            with nc.Block() as block:
                if masked:
                    @block.sync
                    def _(sp):
                        sp.dma_start(wo[:, :, :], t_in["L0_ffn_ow"].rearrange("(k p) n -> p k n", p=P)).then_inc(s_wl3, 16)
                else:
                    @block.sync
                    def _(sp):
                        for e in range(E):
                            sp.dma_start(w2[:, e, :, :], t_in["L0_ffn_w2"][e].rearrange("(k p) f -> p k f", p=P))\
                              .then_inc(s_wl4, 16)

                @block.tensor
                def _(pe):
                    def rows_T(kind, g):
                        n = use_no[kind, g]
                        if n >= 2:
                            pe.wait_ge(*read(n - 2))
                        b, hg = divmod(g, 4)
                        o = bank(n).bitcast(BF16)
                        if kind == "QT":
                            pe.wait_ge(*after("a_mp", g + 1))
                        for j in range(NKJ if kind == "K" else GH):
                            for q in range(2):
                                r = 2 * j + q
                                h = 4 * hg + j
                                if kind == "K" and not masked:
                                    h = hg
                                if kind == "FKL":
                                    mm = pe.transpose(o[0:M, P * r:P * r + P], FKL[:, 2 * b + q, h, :], identb[:, :])
                                else:
                                    mm = pe.transpose(o[:, P * r:P * r + P], src[kind][:, 2 * b + q, h, :], identb[:, :])
                        mm.then_inc(ts["a_t"], 1)

                    def sums_T(kind, g):
                        n = use_no[kind, g]
                        pe.wait_ge(*read(n - 2))
                        pe.wait_ge(*after("a_acc" if kind == "O" else "a_accg", g + 1))
                        o_ = OTs if kind == "O" else OTg
                        for q in range(2):
                            mm = pe.transpose(bank(n)[:, P * q:P * q + P], o_[:, P * q:P * q + P], identf[:, :])
                        mm.then_inc(ts["a_t"], 1)

                    def sg_bank(u):
                        n = sg_no[u]
                        if n >= 1:
                            pe.wait_ge(*after("a_sr", n))
                        return ps[:, 2:4, :]

                    def scores_q(g, q):
                        o = sg_bank(("S", g, q))
                        if q == 0:
                            pe.wait_ge(*read(use_no["Q", g]))
                            pe.wait_ge(*read(use_no["K", g]))
                        for a in range(2):
                            if masked:
                                pe.matmul(o[:, a, :], identh[:, :],
                                          maskq[:, q, :].unsqueeze(1).broadcast_to([P, 2, L]),
                                          start=True, stop=False, skip_group_check=True)
                            for jj in range(2):
                                j = 2 * a + jj
                                jk = j if masked else 0
                                mm = pe.matmul(o[:, a, L * jj:L * jj + L],
                                               QS[0:SROWS, g % 2, P * (2 * j + q):P * (2 * j + q) + P],
                                               KSg[0:SROWS, g % 2, L * jk:L * jk + L],
                                               start=not masked, stop=True, skip_group_check=True)
                        mm.then_inc(ts["a_s"], 1)

                    def scores_k(g, k):
                        if k == 0:
                            pe.wait_ge(*read(use_no["QT", g]))
                        if 2 * g + k >= 1:
                            pe.wait_ge(*after("a_exp", 2 * g + k))
                        for a in range(2):
                            o = ps[:, 4 + a, :]
                            if masked:
                                pe.matmul(o, identh[:, :],
                                          maskk[:, k, :].unsqueeze(1).broadcast_to([P, 2, L]),
                                          start=True, stop=False, skip_group_check=True)
                            for jj in range(2):
                                j = 2 * a + jj
                                jk = j if masked else 0
                                mm = pe.matmul(o[:, L * jj:L * jj + L],
                                               KSg[0:MROWS, g % 2, P * (2 * jk + k):P * (2 * jk + k) + P],
                                               QT[0:MROWS, g % 2, L * j:L * j + L],
                                               start=not masked, stop=True, skip_group_check=True)
                        mm.then_inc(ts["a_st"], 1)

                    def features(g, k):
                        o = sg_bank(("G", g, k))
                        if k == 0:
                            for kind in ("FQ", "FK", "FKL"):
                                pe.wait_ge(*read(use_no[kind, g]))
                        for j in range(GH):
                            oj = o[:, j // 2, L * (j % 2):L * (j % 2) + L]
                            r = P * (2 * j + k)
                            pe.matmul(oj, FKT[0:5 * M, g % 2, r:r + P], FQT[0:5 * M, g % 2, L * j:L * j + L],
                                      start=True, stop=False)
                            mm = pe.matmul(oj, FKLT[0:M, g % 2, r:r + P], FQT[0:M, g % 2, L * j:L * j + L],
                                           start=False, stop=True)
                        mm.then_inc(ts["a_s"], 1)

                    def sums(g, k, part):
                        pe.wait_ge(*after("a_gm" if part else "a_exp", 2 * g + k + 1))
                        if k == 0 and g >= 1:
                            pe.wait_ge(*after("a_accg" if part else "a_acc", g))
                        b, hg = divmod(g, 4)
                        for j in range(GH):
                            h = 4 * hg + j if masked else hg
                            mm = pe.matmul(ps[32 * j:32 * j + 32, 6 + part, 0:L],
                                           V2[:, 2 * b + k, VW * h:VW * h + 32],
                                           (PG if part else PTn)[:, k, L * j:L * j + L],
                                           start=(k == 0), stop=(k == 1))
                        mm.then_inc(ts["a_pg" if part else "a_pv"], 1)

                    for i in range(NG + 2):
                        g, o = i - 1, i - 2
                        has_g = 0 <= g < NG
                        if has_g:
                            rows_T("QT", g)
                        if i < NG:
                            rows_T("Q", i)
                            rows_T("K", i)
                        if has_g:
                            scores_k(g, 0)
                        if masked and o >= 0:
                            sums(o, 0, 1)
                            sums(o, 1, 1)
                        if i < NG:
                            scores_q(i, 0)
                        if o >= 0:
                            sums_T("O", o)
                        if has_g:
                            scores_k(g, 1)
                        if masked and i < NG:
                            rows_T("FQ", i)
                        if i < NG:
                            scores_q(i, 1)
                        if has_g:
                            sums(g, 0, 0)
                        if masked and o >= 0:
                            sums_T("OG", o)
                        if masked and i < NG:
                            rows_T("FK", i)
                        if masked and has_g:
                            features(g, 0)
                        if has_g:
                            sums(g, 1, 0)
                        if masked and i < NG:
                            rows_T("FKL", i)
                        if masked and has_g:
                            features(g, 1)

                def copy_T(eng, kind, g):
                    n = use_no[kind, g]
                    eng.wait_ge(*after("a_t", n + 1))
                    pr = M if kind == "FKL" else P
                    w = 2 * P * (NKJ if kind == "K" else GH)
                    o, i_ = dst[kind][0:pr, g % 2, 0:w], bank(n).bitcast(BF16)[0:pr, 0:w]
                    if uses[n][2] == "act":
                        eng.activation(o, i_, ACT.Copy).then_inc(ts["a_td_act"], 1)
                    else:
                        eng.tensor_copy(o, i_).then_inc(ts["a_td_dve"], 1)

                @block.scalar
                def _(act):
                    def exps(g, k):
                        act.wait_ge(*after("a_st", 2 * g + k + 1))
                        if g >= 1:
                            act.wait_ge(*after("a_pv", 2 * g - 1 + k))
                        act.activation(PTn[:, k, :], ps[:, 4:6, :], ACT.Exp, scale=SCALE).then_inc(ts["a_exp"], 1)

                    for i in range(NG + 2):
                        g, o = i - 1, i - 2
                        has_g = 0 <= g < NG
                        if i < NG:
                            copy_T(act, "K", i)
                        if has_g:
                            exps(g, 0)
                        if masked and o >= 0:
                            act.wait_ge(*after("a_pg", 2 * o + 2))
                            if o >= 1:
                                act.wait_ge(*read(use_no["OG", o - 1]))
                            act.activation(OTg[:, :], ps[:, 7, 0:L], ACT.Copy).then_inc(ts["a_accg"], 1)
                        if masked and i < NG:
                            if i >= 2:
                                act.wait_ge(*after("a_s", sg_no["G", i - 2, 1] + 1))
                            copy_T(act, "FQ", i)
                        if has_g:
                            exps(g, 1)
                        if masked and i < NG:
                            copy_T(act, "FK", i)
                        if has_g:
                            act.wait_ge(*after("a_pv", 2 * g + 2))
                            if g >= 1:
                                act.wait_ge(*read(use_no["O", g - 1]))
                            act.activation(OTs[:, :], ps[:, 6, 0:L], ACT.Copy).then_inc(ts["a_acc"], 1)
                        if masked and i < NG:
                            copy_T(act, "FKL", i)

                @block.vector
                def _(dve):
                    def maxima(g, q):
                        b, hg = divmod(g, 4)
                        n = sg_no["S", g, q]
                        dve.wait_ge(*after("a_s", n + 1))
                        dve.tensor_reduce(nmall[:, 2 * b + q, 4 * hg:4 * hg + 4],
                                          ps[:, 2:4, :].rearrange("p a (j n) -> p (a j) n", n=L),
                                          AX.X, ALU.max, negate=True).then_inc(ts["a_sr"], 1)

                    def masked_features(g, k):
                        n = sg_no["G", g, k]
                        dve.wait_ge(*after("a_s", n + 1))
                        if g >= 1:
                            dve.wait_ge(*after("a_pg", 2 * g - 1 + k))
                        dve.tensor_tensor(PG[:, k, :].rearrange("p (j n) -> p j n", n=L),
                                          ps[:, 2:4, :].rearrange("p a (j n) -> p (a j) n", n=L),
                                          wmask[:, k, :].unsqueeze(1).broadcast_to([P, GH, L]),
                                          ALU.mult).then_inc(ts["a_gm"], 1)
                        dve.wait_ge(*after("a_gm", 2 * g + k + 1))
                        dve.sem_inc(ts["a_sr"], 1)

                    def outputs(kind, g):
                        b, hg = divmod(g, 4)
                        n = use_no[kind, g]
                        dve.wait_ge(*after("a_t", n + 1))
                        o = bank(n)[:, 0:2 * P].rearrange("p (q j d) -> p q j d", q=2, d=32)
                        S_ = As if kind == "O" else Gs
                        for q in range(2):
                            ins = dve.tensor_copy(S_[:, 2 * b + q, 4 * hg:4 * hg + 4, :], o[:, q, :, 0:VW])
                        ins.then_inc(ts["a_td_dve"], 1)

                    for i in range(NG + 2):
                        g, o = i - 1, i - 2
                        has_g = 0 <= g < NG
                        if has_g:
                            if g >= 2:
                                dve.wait_ge(*after("a_st", 2 * g - 2))
                            copy_T(dve, "QT", g)
                        if i < NG:
                            copy_T(dve, "Q", i)
                            maxima(i, 0)
                        if o >= 0:
                            outputs("O", o)
                        if i < NG:
                            b, hg = divmod(i, 4)
                            maxima(i, 1)
                            dve.wait_ge(*after("a_sr", sg_no["S", i, 1] + 1))
                            nm_ = nmall[:, 2 * b:2 * b + 2, 4 * hg:4 * hg + 4]
                            q_ = QN[:, 2 * b:2 * b + 2, 4 * hg:4 * hg + 4, :]
                            link_dve(dve.tensor_copy(q_[:, :, :, SROWS], nm_))
                            link_dve(dve.tensor_tensor(nrs, nm_, q_[:, :, :, SROWS], ALU.subtract))
                            link_dve(dve.tensor_copy(q_[:, :, :, SROWS + 1], nrs))
                            dve.tensor_tensor(q_[:, :, :, SROWS + 2], nrs, q_[:, :, :, SROWS + 1],
                                              ALU.subtract).then_inc(ts["a_mp"], 1)
                        if masked and o >= 0:
                            outputs("OG", o)
                        if masked and has_g:
                            masked_features(g, 0)
                            masked_features(g, 1)

            base["a_t"] += len(uses)
            for who in ("act", "dve"):
                base["a_td_" + who] += sum(u[2] == who for u in uses)
            for name in ("a_s", "a_sr"):
                base[name] += len(sg)
            for name in ("a_mp", "a_acc"):
                base[name] += NG
            for name in ("a_st", "a_exp", "a_pv"):
                base[name] += 2 * NG
            if masked:
                base["a_gm"] += 2 * NG
                base["a_pg"] += 2 * NG
                base["a_accg"] += NG

        attention(True)

        s5 = {n: sem(n) for n in ("c_ln1", "c_e1", "c_l2", "c_g", "c_q", "c_qc", "c_ph", "c_p", "c_pc", "c_v", "c_vc")}
        A16 = As[:, :, :, DH]
        Y = Gs[:, :, :, DH]
        with nc.Block() as block:
            @block.vector
            def _(dve):
                link_dve(dve.tensor_scalar(t1, Y, 1e-24, None, ALU.max))
                for R in range(RT):
                    ins = dve.tensor_tensor(t2[:, R, :], qls[:, R, :], kls[:, R // 2, :], ALU.add)
                link_dve(ins)
                dve.sem_inc(s5["c_ln1"], 1)
                dve.wait_ge(s5["c_l2"], 2)
                link_dve(dve.scalar_tensor_tensor(out=t0, in0=nmall, scalar=-SCALE, in1=t0, op0=ALU.mult, op1=ALU.add))
                link_dve(dve.tensor_tensor(t1, t1, t2, ALU.add))
                link_dve(dve.tensor_tensor(t3, t0, t1, ALU.max))
                link_dve(dve.tensor_tensor(t0, t0, t3, ALU.subtract))
                dve.tensor_tensor(t1, t1, t3, ALU.subtract).then_inc(s5["c_ln1"], 1)
                dve.wait_ge(s5["c_l2"], 4)
                dve.tensor_tensor(t0, t0, t1, ALU.add).then_inc(s5["c_ln1"], 1)
                dve.wait_ge(s5["c_l2"], 5)
                link_dve(dve.tensor_tensor(t0, t0, t3, ALU.add))
                dve.tensor_tensor(t0, t2, t0, ALU.subtract).then_inc(s5["c_ln1"], 1)
                link_dve(dve.reciprocal(t1, A16))
                dve.wait_ge(s5["c_l2"], 6)
                for R in range(RT):
                    a_ = att[:, R, :].rearrange("p (h d) -> p h d", d=DH)
                    link_dve(dve.tensor_tensor(a_, As[:, R, :, 0:DH], t1[:, R, :].unsqueeze(2).broadcast_to([P, H, DH]),
                                               ALU.mult))
                    g_ = Gs[:, R, :, 0:DH]
                    link_dve(dve.tensor_tensor(g_, g_, t0[:, R, :].unsqueeze(2).broadcast_to([P, H, DH]), ALU.mult))
                    ins = dve.tensor_tensor(a_, a_, g_, ALU.add)
                    link_dve(ins)
                dve.sem_inc(s_attb, 1)
                residual_dve(dve, 1)
                ln_dve(dve, 2, 1e-5)
                for R in range(RT):
                    dve.wait_ge(s5["c_v"], R + 1)
                    v_ = V2[:, R, 0:GH * VW].rearrange("p (h d) -> p h d", d=VW)
                    dve.tensor_copy(v_[:, :, 0:DH], ps[:, R, 256 + 64:256 + 128].rearrange("p (h d) -> p h d", d=DH))\
                       .then_inc(s5["c_vc"], 1)
                for side in range(2):
                    nh = H if side == 0 else GH
                    T, sm_, sl_ = (QN, 1, 4) if side == 0 else (KN, 2, 5)
                    dve.wait_ge(s5["c_ph"], RT)
                    for R in range(RT):
                        q = QK[:, R, D * side:D * side + DH * nh].rearrange("p (h d) -> p h d", d=DH)
                        link_dve(dve.tensor_tensor(q, q, T[:, R, 0:nh, 0:DH], ALU.subtract))
                        link_dve(dve.tensor_copy(T[:, R, 0:nh, DH * sm_:DH * sm_ + DH], q))
                        link_dve(dve.tensor_tensor(T[:, R, 0:nh, DH * sl_:DH * sl_ + DH], q,
                                                   T[:, R, 0:nh, DH * sm_:DH * sm_ + DH], ALU.subtract))
                dve.sem_inc(s5["c_p"], 1)

            @block.scalar
            def _(act):
                act.wait_ge(s5["c_ln1"], 1)
                act.activation(t0, A16, ACT.Ln).then_inc(s5["c_l2"], 1)
                act.activation(t1, t1, ACT.Ln).then_inc(s5["c_l2"], 1)
                act.wait_ge(s5["c_ln1"], 2)
                act.activation(t0, t0, ACT.Exp).then_inc(s5["c_l2"], 1)
                act.activation(t1, t1, ACT.Exp).then_inc(s5["c_l2"], 1)
                act.wait_ge(s5["c_ln1"], 3)
                act.activation(t0, t0, ACT.Ln).then_inc(s5["c_l2"], 1)
                act.wait_ge(s5["c_ln1"], 4)
                act.activation(t0, t0, ACT.Exp).then_inc(s5["c_l2"], 1)
                rows_T_act(act, 3)
                ln_act(act, 2)
                rows_T_act(act, 4)
                for R in range(RT):
                    act.wait_ge(s5["c_vc"], R + 1)
                    link_act(act.activation(QK[:, R, 0:D + 64], ps[:, R, 0:D + 64], ACT.Copy))
                    act.activation(QN[:, R, :, 0:DH], QK[:, R, 0:D].rearrange("p (h d) -> p h d", d=DH), ACT.Copy)
                    link_act(act.activation(KN[:, R, 0:GH, 0:DH], QK[:, R, D:D + 64].rearrange("p (h d) -> p h d", d=DH),
                                            ACT.Copy))
                    act.sem_inc(s5["c_ph"], 1)

            @block.gpsimd
            def _(pool):
                def slot(T, R, n, nh):
                    return T[:, R, 0:nh, DH * n:DH * n + DH]
                pool.wait_ge(s5["c_ph"], RT)
                for R in range(RT):
                    for n in (2, 5):
                        pool.tensor_copy(slot(QN, R, n, H), slot(QN, R, 0, H)).then_inc(s5["c_pc"], 1)
                    for n in (1, 4):
                        pool.tensor_copy(slot(KN, R, n, GH), slot(KN, R, 0, GH)).then_inc(s5["c_pc"], 1)
                pool.wait_ge(s5["c_p"], 1)
                for R in range(RT):
                    pool.tensor_copy(slot(QN, R, 3, H), slot(QN, R, 1, H)).then_inc(s5["c_pc"], 1)
                    pool.tensor_copy(slot(KN, R, 3, GH), slot(KN, R, 2, GH)).then_inc(s5["c_pc"], 1)

            @block.tensor
            def _(pe):
                pe.wait_ge(s_attb, 2)
                rows_T_pe(pe, 3, att)
                pe.wait_ge(s_lnTc, 4 * KT)
                project_pe(pe, 1, woT2, b_out2)
                pe.wait_ge(s_ln, 3 * RT)
                rows_T_pe(pe, 4, lnx)
                pe.wait_ge(s_lnTc, 5 * KT)
                pe.wait_ge(s_wl3, 128)
                kv = wk.rearrange("p (k n) -> p k n", k=4)
                for R in range(RT):
                    for lo, w, br in ((0, lambda k: wq[:, k, :], b_q3), (D, lambda k: kv[:, k, :], bkv[:, 0:64]),
                                      (D + 64, lambda k: kv[:, 2 + k, :], bkv[:, 64:128])):
                        hi = lo + br.shape[1]
                        for k in range(KT):
                            pe.matmul(ps[:, R, lo:hi], lnT[:, k, P * R:P * R + P], w(k), start=(k == 0), stop=False)
                        mm = pe.matmul(ps[:, R, lo:hi], onesf[0:1, :], br, start=False, stop=True)
                    mm.then_inc(s5["c_v"], 1)

        if stop == "x2":
            return store_x(X[:, :, :])
        attention(False)

        s7 = {n: sem(n) for n in ("m_wn", "m_dr", "m_ar", "m_ln", "m_lg", "m_sg", "m_M", "m_rk", "m_h", "m_g", "m_y",
                                  "m_acc", "m_c")}
        src_ = lnx

        def c8(at):
            return small[:, at:at + RT * E].rearrange("p (r e) -> p r e", e=E)

        def c1(at):
            return small[:, at:at + RT]

        pr, Ma, Mb, wt, ec, tmp = c8(0), c8(32), c8(64), c8(96), c8(128), c8(160)
        Mbf = small[:, 192:208].bitcast(BF16).rearrange("p (r e) -> p r e", e=E)
        top1, top2, rcp, cm = c1(224), c1(228), c1(232), c1(236)

        def bc(x):
            return x.unsqueeze(2).broadcast_to([P, RT, E])

        def rms_dve(dve, n, srcT, dstT, wn, k):
            for R in range(RT):
                link_dve(dve.bn_stats(bst[:, R, :], srcT[:, R, :]))
                link_dve(dve.bn_aggr(mv[:, R, :], bst[:, R, :]))
            link_dve(dve.tensor_tensor(ve[:, :], mv[:, :, 0], mv[:, :, 0], ALU.mult))
            link_dve(dve.scalar_tensor_tensor(out=ve[:, :], in0=ve[:, :], scalar=1e-6, in1=mv[:, :, 1],
                                              op0=ALU.add, op1=ALU.add))
            dve.sem_inc(s_var, 1)
            dve.wait_ge(s_std, n + 1)
            link_dve(dve.reciprocal(rs[:, :], sd[:, :]))
            for R in range(RT):
                link_dve(dve.scalar_tensor_tensor(out=dstT[:, R, :], in0=srcT[:, R, :], scalar=rs[:, R:R + 1],
                                                  in1=wn[:, :], op0=ALU.mult, op1=ALU.mult))
            dve.sem_inc(s7["m_ln"], 1)

        with nc.Block() as block:
            @block.sync
            def _(sp):
                sp.dma_start(wn1[:, :], t_in["L0_ffn_norm1_w"].partition_broadcast(P)).then_inc(s7["m_wn"], 16)
                sp.dma_start(wn2[:, :], t_in["L0_ffn_norm2_w"].partition_broadcast(P)).then_inc(s7["m_wn"], 16)
                sp.dma_start(gate[:, :, :], t_in["L0_ffn_gate_w"].rearrange("(k p) e -> p k e", p=P)).then_inc(s7["m_wn"], 16)
                sp.wait_ge(s7["m_ln"], 3)
                sp.dma_start(out.rearrange("b (r p) d -> p (b r) d", p=P), X[:, :, :]).then_inc(s_out, 16)
                sp.wait_ge(s_out, 16)

            @block.gpsimd
            def _(pool):
                link_pool(pool.memset(lowb[:, :, :], 1.0))
                link_pool(pool.affine_select(out=lowb[:, 0, :], in_=lowb[:, 0, :], compare_op=ALU.is_gt, fill=0.0,
                                             base=0, pattern=[[1, P]], channel_multiplier=-1))
                link_pool(pool.iota(ec[:, :, :], pattern=[[0, RT], [-1, E]], base=E, channel_multiplier=0,
                                    allow_small_or_imprecise_dtypes=True))
                pool.sem_inc(s7["m_c"], 1)

            @block.vector
            def _(dve):
                link_dve(dve.reciprocal(t1, A16))
                for R in range(RT):
                    a_ = att[:, R, :].rearrange("p (h d) -> p h d", d=DH)
                    link_dve(dve.tensor_tensor(a_, As[:, R, :, 0:DH], t1[:, R, :].unsqueeze(2).broadcast_to([P, H, DH]),
                                               ALU.mult))
                dve.sem_inc(s_attb, 1)
                for R in range(RT):
                    dve.wait_ge(s_op, RT * 2 + R + 1)
                    link_dve(dve.tensor_tensor(lnx[:, R, :], lnx[:, R, :], PB[R],
                                               ALU.add))
                dve.wait_ge(s7["m_wn"], 48)
                rms_dve(dve, 3, lnx, lnx, wn1, 0)
                dve.wait_ge(s7["m_sg"], 1)
                dve.wait_ge(s7["m_c"], 1)
                for first, (top, Mx) in enumerate(((top1, Ma), (top2, Mb))):
                    link_dve(dve.tensor_reduce(top, pr, AX.X, ALU.max))
                    link_dve(dve.tensor_tensor(tmp, pr, bc(top), ALU.is_equal))
                    link_dve(dve.tensor_tensor(tmp, tmp, ec, ALU.mult))
                    link_dve(dve.tensor_reduce(cm, tmp, AX.X, ALU.max))
                    link_dve(dve.tensor_tensor(Mx, tmp, bc(cm), ALU.is_equal))
                    if first == 0:
                        link_dve(dve.scalar_tensor_tensor(out=pr, in0=Ma, scalar=-4.0, in1=pr, op0=ALU.mult, op1=ALU.add))
                link_dve(dve.scalar_tensor_tensor(out=rcp, in0=top1, scalar=1e-6, in1=top2, op0=ALU.add, op1=ALU.add))
                link_dve(dve.reciprocal(rcp, rcp))
                link_dve(dve.tensor_tensor(tmp, Ma, bc(top1), ALU.mult))
                link_dve(dve.tensor_tensor(wt, Mb, bc(top2), ALU.mult))
                link_dve(dve.tensor_tensor(wt, wt, tmp, ALU.add))
                link_dve(dve.tensor_tensor(wt, wt, bc(rcp), ALU.mult))
                link_dve(dve.tensor_tensor(Mbf, Ma, Mb, ALU.add))
                dve.sem_inc(s7["m_M"], 1)
                dve.wait_ge(s7["m_rk"], 1)
                link_dve(dve.tensor_scalar(tmp, ps[:, 7, 0:RT * E].rearrange("p (r e) -> p r e", e=E), float(CAP), None,
                                           ALU.is_lt))
                link_dve(dve.tensor_tensor(wt, wt, tmp, ALU.mult))
                link_dve(dve.memset(acc[:, :, :], 0.0))
                for e in range(E):
                    for R in range(RT):
                        if R % 2 == 0:
                            dve.wait_ge(s7["m_y"], 2 * e + R // 2 + 1)
                        ins = dve.scalar_tensor_tensor(out=acc[:, R, :], in0=ps[:, 4 + 2 * (e % 2) + R // 2, 256 * (R % 2):256 * (R % 2) + 256],
                                                       scalar=wt[:, R, e:e + 1], in1=acc[:, R, :], op0=ALU.mult,
                                                       op1=ALU.add)
                        ins.then_inc(s7["m_acc"], 1)
                    dve.wait_ge(s7["m_acc"], RT * (e + 1))
                for R in range(RT):
                    link_dve(dve.tensor_tensor(lnx[:, R, :], lnx[:, R, :], acc[:, R, :], ALU.add))
                rms_dve(dve, 4, lnx, lnx, wn2, 1)
                for R in range(RT):
                    link_dve(dve.tensor_tensor(X[:, R, :], X[:, R, :], lnx[:, R, :], ALU.add))
                dve.sem_inc(s7["m_ln"], 1)

            @block.scalar
            def _(act):
                rows_T_act(act, 5)
                ln_act(act, 3)
                rows_T_act(act, 6)
                act.wait_ge(s7["m_lg"], 1)
                act.activation(pr, ps[:, 6, 0:RT * E].rearrange("p (r e) -> p r e", e=E), ACT.Sigmoid).then_inc(s7["m_sg"], 1)
                for e in range(E):
                    for f in range(FF // P):
                        n = 4 * e + f
                        act.wait_ge(s7["m_h"], n + 1)
                        if e >= 2:
                            act.wait_ge(s7["m_y"], 2 * (e - 1))
                        act.activation(hT[:, e % 2, f, :], ps[:, n % 4, :], ACT.Gelu).then_inc(s7["m_g"], 1)
                ln_act(act, 4)

            @block.tensor
            def _(pe):
                pe.wait_ge(s_attb, 3)
                rows_T_pe(pe, 5, att)
                pe.wait_ge(s_lnTc, 6 * KT)
                project_pe(pe, 2, wo, b_o3)
                pe.wait_ge(s7["m_ln"], 1)
                rows_T_pe(pe, 6, lnx)
                pe.wait_ge(s_lnTc, 7 * KT)
                for R in range(RT):
                    for k in range(KT):
                        mm = pe.matmul(ps[:, 6, E * R:E * R + E], lnT[:, k, P * R:P * R + P], gate[:, k, :],
                                       start=(k == 0), stop=(k == KT - 1))
                mm.then_inc(s7["m_lg"], 1)

                def up(e):
                    for f in range(FF // P):
                        n = 4 * e + f
                        if n >= 4:
                            pe.wait_ge(s7["m_g"], n - 3)
                        for k in range(KT):
                            mm = pe.matmul(ps[:, n % 4, :], w1[:, e, k, P * f:P * f + P], lnT[:, k, :],
                                           start=(k == 0), stop=(k == KT - 1))
                        mm.then_inc(s7["m_h"], 1)

                pe.wait_ge(s_wl4, 256)
                up(0)
                pe.wait_ge(s7["m_M"], 1)
                for R in range(RT):
                    for r in range(R + 1):
                        mm = pe.matmul(ps[:, 7, E * R:E * R + E], lowb[:, 0 if r == R else 1, :], Mbf[:, r, :],
                                       start=(r == 0), stop=(r == R))
                mm.then_inc(s7["m_rk"], 1)
                for e in range(E):
                    if e + 1 < E:
                        up(e + 1)
                    for R in range(RT):
                        if e == 1 and R == 0:
                            pe.wait_ge(s7["m_acc"], 1)
                        if R % 2 == 0 and e >= 2:
                            pe.wait_ge(s7["m_acc"], RT * (e - 1))
                        if R == 0:
                            pe.wait_ge(s7["m_g"], 4 * (e + 1))
                        for f in range(FF // P):
                            mm = pe.matmul(ps[:, 4 + 2 * (e % 2) + R // 2, 256 * (R % 2):256 * (R % 2) + 256],
                                           hT[:, e % 2, f, P * R:P * R + P], w2[:, e, f, :],
                                           start=(f == 0), stop=(f == FF // P - 1))
                        if R % 2 == 1:
                            mm.then_inc(s7["m_y"], 1)


_INS = ['x', 'ctx_512', 'L0_xattn_Wq', 'L0_xattn_bq', 'L0_xattn_Wk', 'L0_xattn_bk', 'L0_xattn_Wv', 'L0_xattn_bv',
        'L0_xattn_Wo', 'L0_xattn_bo', 'L0_attn_Wqkv_w', 'L0_attn_Wqkv_b', 'L0_attn_proj', 'L0_attn_out_w',
        'L0_attn_out_b', 'L0_ffn_qw', 'L0_ffn_qb', 'L0_ffn_kw', 'L0_ffn_kb', 'L0_ffn_vw', 'L0_ffn_vb', 'L0_ffn_ow',
        'L0_ffn_ob', 'L0_ffn_gate_w', 'L0_ffn_w1', 'L0_ffn_w2', 'L0_ffn_norm1_w', 'L0_ffn_norm2_w']


def kernel(**inputs):
    import numpy as _np
    import concourse.bacc as _bacc
    from concourse import mybir as _mybir
    from concourse.bass_utils import run_bass_kernel_spmd as _run

    nc = _bacc.Bacc("TRN2", target_bir_lowering=False, num_devices=1)
    arrays, aps = {}, {}
    for name in _INS:
        a = _np.ascontiguousarray(inputs[name])
        arrays[f"in_{name}_dram"] = a
        aps[name] = nc.dram_tensor(f"in_{name}_dram", a.shape, _mybir.dt.from_np(a.dtype), kind="ExternalInput").ap()
    out = nc.dram_tensor("out_0_dram", (B, L, D), F32, kind="ExternalOutput").ap()
    build(nc, aps, out)
    r = _run(nc, [arrays], core_ids=[0])
    return r.results[0]["out_0_dram"]
```

```python
from contextlib import ExitStack

import concourse.bass as bass
from concourse import mybir

F32 = mybir.dt.float32
BF16 = mybir.dt.bfloat16
F16 = mybir.dt.float16
ALU = mybir.AluOpType
ACT = mybir.ActivationFunctionType
AX = mybir.AxisListType

P = 128
B, L, D = 2, 256, 256
H, DH = 16, 16
NK, DC = 4096, 128
RT = B * L // P
KT = D // P
GH = 4
NG = B * H // GH
M = 24
E, FF, CAP = 8, 512, 160
TPB = NK // P
VW = DH + 1
SCALE = 0.25

QSLOT = "hmhmlh"
KSLOT = "hhmmhl"
NS = len(QSLOT)
SROWS = NS * DH
MROWS = SROWS + 3
SPS = 5
SPI, PLI = 16 * GH * SPS, 16 * GH * (NS - SPS)

LEAD = 5
SPG = TPB
UPG = 64
S0 = -(SPG + LEAD) - 1
SEND = NG * SPG


K_STEPS = (-6, -2, 1, 5, 9, 13, 17, 21)
V_STEPS = (38, 42, 46, 50, 54, 71, 79, 87)


def aux_of(s):
    out = []
    if 1 <= s - S0 < 9:
        out.append(("C", s - S0 - 1))
    if s - S0 >= 10 and (s - S0 - 10) % 3 == 0 and (s - S0 - 10) // 3 < 8:
        out.append(("V", (s - S0 - 10) // 3))
    for e in range(1, 4):
        for c in range(8):
            if s == 2 * SPG * (e - 1) + K_STEPS[c] + 1:
                out.append(("K", 8 * e + c))
            if s == 2 * SPG * (e - 1) + V_STEPS[c] + 1:
                out.append(("V", 8 * e + c))
    for g in range(NG):
        if s == SPG * (g - 1) - LEAD - (1 if g == 0 else 2):
            out.append(("QS", g))
        if s == SPG * g - 3:
            out.append(("QT", g))
        if s == SPG * (g + 1) + 4:
            out.append(("OT", g))
    return out


AUX = [(s, kind, i) for s in range(S0, SEND + 8) for kind, i in aux_of(s)]
AUX_NO = {(kind, i): n for n, (s, kind, i) in enumerate(AUX)}
assert len(AUX_NO) == 24 + 32 + 8 + 3 * NG


def units_of(s):
    first = UPG + 2 * (s + LEAD)
    return range(max(first, 0), max(min(first + 2, UPG * NG), 0))


def build(nc, t_in, out):
    with ExitStack() as ctx:
        def sb(name, shape, dt=F32):
            return ctx.enter_context(nc.sbuf_tensor(name, shape, dt))

        def sem(name):
            return ctx.enter_context(nc.semaphore(name))

        ps = ctx.enter_context(nc.psum_tensor("ps", [P, 8, 512], F32))

        identf = sb("identf", [P, P])
        identb = sb("identb", [P, P], BF16)
        onesf = sb("onesf", [P, P])
        X = sb("X", [P, RT, D])
        lnx = sb("lnx", [P, RT, D])
        lnT = sb("lnT", [P, KT, B * L])
        bst = sb("bst", [P, RT, 6])
        mv = sb("mv", [P, RT, 2])
        ve = sb("ve", [P, RT])
        sd = sb("sd", [P, RT])
        rs = sb("rs", [P, RT])

        wq = sb("wq", [P, KT, D])
        wo = sb("wo", [P, KT, D])
        wk = sb("wk", [P, D])
        wv = sb("wv", [P, D])
        bqr = sb("bqr", [1, D])
        bor = sb("bor", [P, D])
        bkc = sb("bkc", [P, 2])
        bvb = sb("bvb", [P, D])
        big = sb("big", [P, 2, GH, NK], BF16)
        stack = big
        ctxn = stack[:, 1, :, :].rearrange("p j n -> p (j n)").bitcast(F32).rearrange(
            "p (b t c) -> p b t c", b=B, c=DC)
        ctxT = sb("ctxT", [P, B, NK])
        kpt = sb("kpt", [P, 3, NK], BF16)
        kh, km, kl = kpt[:, 0, :], kpt[:, 1, :], kpt[:, 2, :]
        kparts = {"h": kh, "m": km, "l": kl}
        kr = sb("kr", [P, 2, 512])
        Vg = sb("Vg", [P, 2, TPB * GH * VW + 32 - VW])
        PT = sb("PT", [P, 3, GH * L])
        qf = lnx
        qpt = sb("qpt", [P, 3, RT, D], BF16)
        qh, qm, ql = qpt[:, 0], qpt[:, 1], qpt[:, 2]
        qparts = {"h": qh, "m": qm, "l": ql}
        Qg = sb("Qg", [P, 2, 2 * GH, P], BF16)
        QS = sb("QS", [P, 2, 2 * GH * P], BF16)
        QT = sb("QT", [P, 2, 2 * GH * P], BF16)
        mx = sb("mx", [P, 2, 2 * GH, 8])
        nm = sb("nm", [P, 2 * GH])
        nr = sb("nr", [P, 2 * GH])
        OTs = sb("OTs", [P, L])
        rec = sb("rec", [P, 2, GH])
        att = sb("att", [P, RT, D])

        ST = [ps[:, 0:2, :], ps[:, 2:4, :]]
        SM = [ps[:, 4, :], ps[:, 5, :]]
        ACC = ps[:, 6, :]
        AUXB = ps[:, 7, :]

        def max_bank(n):
            return [SM[0], SM[1], ps[:, 0, :], ps[:, 1, :], ps[:, 2, :], ps[:, 3, :]][n % 6 if n < UPG else n % 2]

        s_x_in = sem("s_x_in")
        s_wvo_in = sem("s_wvo_in")
        s_ctx = [sem(f"s_ctx{i}") for i in range(8)]
        s_const = sem("s_const")
        s_ones_seed = sem("s_ones_seed")
        s_ones_odd = sem("s_ones_odd")
        s_wk_in = sem("s_wk_in")
        s_wq_in = sem("s_wq_in")
        s_k_made = sem("s_k_made")
        s_k_high = sem("s_k_high")
        s_k_mid = sem("s_k_mid")
        s_k_rest = sem("s_k_rest")
        s_pool_own = sem("s_pool_own")
        s_dve_own = sem("s_dve_own")
        s_act_own = sem("s_act_own")
        s_var = sem("s_var")
        s_std = sem("s_std")
        s_rows_normed = sem("s_rows_normed")
        s_rowsT = sem("s_rowsT")
        s_rowsT_read = sem("s_rowsT_read")
        s_q_made = sem("s_q_made")
        s_q_read = sem("s_q_read")
        s_q_parts = sem("s_q_parts")
        s_ctxT = sem("s_ctxT")
        s_ctxT_read = sem("s_ctxT_read")
        s_slots_sp = [[sem(f"s_slots_sp{p}{h}") for h in range(2)] for p in range(2)]
        s_slots_pool = [[sem(f"s_slots_pool{p}{h}") for h in range(2)] for p in range(2)]
        s_ones_even = sem("s_ones_even")
        s_max_scores = sem("s_max_scores")
        s_max_reduced = sem("s_max_reduced")
        s_scores = sem("s_scores")
        s_probs = sem("s_probs")
        s_sums = sem("s_sums")
        s_sums_read = sem("s_sums_read")
        s_spare_full = sem("s_spare_full")
        s_spare_read = sem("s_spare_read")
        s_spare_k_high = sem("s_spare_k_high")
        s_k_parts = sem("s_k_parts")
        s_q_slots = sem("s_q_slots")
        s_max_parts = sem("s_max_parts")
        s_out_stored = sem("s_out_stored")

        count = {"dve": 0, "act": 0, "pool": 0}

        def link_dve(ins):
            count["dve"] += 1
            ins.then_inc(s_dve_own, 1)
            nc.vector.wait_ge(s_dve_own, count["dve"])

        def link_act(ins):
            count["act"] += 1
            ins.then_inc(s_act_own, 1)
            nc.scalar.wait_ge(s_act_own, count["act"])

        def link_pool(ins):
            count["pool"] += 1
            ins.then_inc(s_pool_own, 1)
            nc.gpsimd.wait_ge(s_pool_own, count["pool"])

        xin = t_in["x"].rearrange("b (r p) d -> p (b r) d", p=P)
        cin = t_in["ctx_512"].rearrange("b (p t) c -> p b t c", p=P)

        def view(tensor_words, at, shape, dt=F32):
            n = 1
            for x in shape[1:]:
                n *= x
            words = n if dt == F32 else n // 2
            v = tensor_words[:, at:at + words]
            if dt != F32:
                v = v.bitcast(dt)
            if len(shape) == 2:
                return v
            names = "abcd"[:len(shape) - 1]
            return v.rearrange(f"p ({' '.join(names)}) -> p {' '.join(names)}",
                               **{c: x for c, x in zip(names, shape[1:])})

        bigw = big.rearrange("p a j n -> p (a j n)").bitcast(F32)
        ctxw = ctxT.rearrange("p b n -> p (b n)")
        kw_ = kpt.rearrange("p a n -> p (a n)").bitcast(F32)
        vgw = Vg.rearrange("p g n -> p (g n)")
        ptw = PT.rearrange("p a n -> p (a n)")
        QN = view(bigw, 0, [P, RT, H, P], BF16)
        KN = view(bigw, 4096, [P, RT, H, P], BF16)
        FQ = view(bigw, 8192, [P, RT, H, P], BF16)
        FK = view(bigw, 12288, [P, RT, H, P], BF16)
        wqkvT = view(ctxw, 512, [P, KT, 3 * D])
        projb = view(ctxw, 0, [P, 8 * M])
        w1 = view(ctxw, 0, [P, E, KT, FF])
        w2 = view(bigw, 8192, [P, E, FF // P, D])
        QK = view(kw_, 0, [P, RT, 2 * D])
        fq = view(kw_, 2048, [P, RT, H, M])
        fk = view(kw_, 3584, [P, RT, H, M])
        FKL = view(kw_, 5120, [P, RT, H, M], BF16)
        PG = view(kw_, 0, [P, 2, GH * L])
        As = view(kw_, 2048, [P, RT, H, VW])
        Gs = view(kw_, 3136, [P, RT, H, VW])
        xT = view(vgw, 0, [P, 2, KT, B * L])
        xsq = view(vgw, 2048, [P, RT, 2 * D])
        KSg = view(vgw, 0, [P, 2, 2 * GH * P], BF16)
        FQT = view(vgw, 1024, [P, 2, 2 * GH * P], BF16)
        FKT = view(vgw, 2048, [P, 2, 2 * GH * P], BF16)
        FKLT = view(vgw, 3072, [P, 2, 2 * GH * P], BF16)
        V2 = view(qpt.rearrange("p a r d -> p (a r d)").bitcast(F32), 0, [P, RT, H * VW + 32 - VW])
        hT = view(kw_, 0, [P, 2, FF // P, B * L])
        acc = view(ptw, 0, [P, RT, D])
        krw = kr.rearrange("p a n -> p (a n)")
        wraw = view(kw_, 2048, [P, 8, D])
        woT2 = view(ptw, 2048, [P, KT, D])
        OTg = view(ptw, 2560, [P, L])
        wn1 = view(ptw, 1024, [P, D])
        wn2 = view(ptw, 1280, [P, D])
        gate = view(ptw, 1536, [P, KT, E])
        lowb = view(ptw, 1600, [P, 2, P], BF16)
        maskq = view(krw, 0, [P, 2, L], F16)
        maskk = view(krw, 256, [P, 2, L], F16)
        wmask = view(krw, 512, [P, 2, L])
        small = Qg.rearrange("p a r n -> p (a r n)").bitcast(F32)
        identh = sb("identh", [P, P], F16)
        biases = sb("biases", [P, 6 * D + 128])

        s_w2_in = sem("s_w2_in")
        s_proj_in = sem("s_proj_in")
        s_w3_in = sem("s_w3_in")
        s_experts_in = sem("s_experts_in")
        s_wT = sem("s_wT")
        s_wT_read = sem("s_wT_read")
        s_proj_zero = sem("s_proj_zero")
        s_heads_out = sem("s_heads_out")
        s_aT = sem("s_aT")
        s_aTc = sem("s_aTc")
        s_projected = sem("s_projected")
        s_xn = sem("s_xn")
        s_qkv_made = sem("s_qkv_made")
        s_qk_read = sem("s_qk_read")
        s_qkT = sem("s_qkT")
        s_qkT_read = sem("s_qkT_read")
        s_squares = sem("s_squares")
        s_logs = sem("s_logs")
        s_logs_q = sem("s_logs_q")
        s_logs_done = sem("s_logs_done")
        s_feat_exp = sem("s_feat_exp")
        s_kmax_rows = sem("s_kmax_rows")
        s_kmaxT = sem("s_kmaxT")
        s_kmax_reduced = sem("s_kmax_reduced")
        s_qk_lower = sem("s_qk_lower")
        s_qk_high = sem("s_qk_high")
        s_v_read = sem("s_v_read")
        s_feat_high = sem("s_feat_high")
        s_feat_lower = sem("s_feat_lower")
        s_feat_all = sem("s_feat_all")
        s_eps_made = sem("s_eps_made")

        bqkv = biases[:, 0:3 * D]
        b_out2 = biases[:, 3 * D:4 * D]
        b_o3 = biases[:, 4 * D:5 * D]
        b_qkv3 = biases[:, 5 * D:6 * D + 128]

        def row_stats(dve, rows):
            for R in range(RT):
                ins = dve.bn_stats(bst[:, R, :], rows[:, R, :])
            link_dve(ins)
            for R in range(RT):
                ins = dve.bn_aggr(mv[:, R, :], bst[:, R, :])
            link_dve(ins)

        def load_slots(eng, g, half, slots, signal):
            eng.wait_ge(s_k_parts, 8 * (g // 2) + 4 * half + 4)
            if g >= 2:
                eng.wait_ge(s_scores, SPG * (g - 2) + 16 * (half + 1))
            elif g == 1 and half == 0:
                eng.wait_ge(s_spare_read, AUX_NO["C", 7] + 1)
            for j in range(GH):
                r = 64 * (g % 2) + DH * j
                for n in slots:
                    eng.dma_start(stack[DH * n:DH * n + DH, g % 2, j, 2048 * half:2048 * half + 2048],
                                  kparts[KSLOT[n]][r:r + DH, 2048 * half:2048 * half + 2048]).then_inc(signal, 16)

        def load_slots_sp(sp, g, half):
            load_slots(sp, g, half, range(SPS), s_slots_sp[g % 2][half])

        def load_slots_pool(pool, g, half):
            load_slots(pool, g, half, range(SPS, NS), s_slots_pool[g % 2][half])

        def wait_loaded(eng, g, half):
            more = PLI if g % 2 == 0 and half == 0 else 0
            eng.wait_ge(s_slots_sp[g % 2][half], SPI * (g // 2 + 1) + more)
            if PLI * (g // 2 + 1) > more:
                eng.wait_ge(s_slots_pool[g % 2][half], PLI * (g // 2 + 1) - more)

        def group_rows(pool, g):
            b, hg = divmod(g, 4)
            pool.wait_ge(s_q_parts, b + 1)
            if g >= 2:
                pool.wait_ge(s_spare_read, AUX_NO["QT", g - 2] + 1)
            for n in range(NS):
                o = Qg[:, g % 2, :, DH * n:DH * n + DH].rearrange("p (j q) d -> p q j d", q=2)
                src = qparts[QSLOT[n]][:, 2 * b:2 * b + 2, 64 * hg:64 * hg + 64].rearrange(
                    "p q (j d) -> p q j d", d=DH)
                for q in range(2):
                    ins = pool.tensor_copy(o[:, q], src[:, q])
            ins.then_inc(s_q_slots, 1)

        CB = [ps[:, i, :] for i in range(2)]
        KB = [ps[:, 2 + i, :] for i in range(2)]
        LB = [ps[:, 4 + i, :] for i in range(2)]
        QB = [ps[:, 6 + i, 0:256] for i in range(2)]
        NCT = TPB // 4
        with nc.Block() as block:
            @block.sync
            def _(sp):
                def chunk(i):
                    b, q = divmod(i, 4)
                    sp.dma_start(ctxn[:, b, 8 * q:8 * q + 8, :], cin[:, b, 8 * q:8 * q + 8, :]).then_inc(s_ctx[i], 16)

                sp.dma_start(X[:, :, :], xin).then_inc(s_x_in, 16)
                for i in range(4):
                    chunk(i)
                sp.dma_start(wv[:, :], t_in["L0_xattn_Wv"]).then_inc(s_wvo_in, 16)
                sp.dma_start(bvb[:, :], t_in["L0_xattn_bv"].partition_broadcast(P)).then_inc(s_wvo_in, 16)
                sp.dma_start(wo[:, :, :], t_in["L0_xattn_Wo"].rearrange("(k p) n -> p k n", p=P)).then_inc(s_wvo_in, 16)
                sp.dma_start(bor[:, :], t_in["L0_xattn_bo"].partition_broadcast(P)).then_inc(s_wvo_in, 16)
                for i in range(4, 8):
                    chunk(i)
                sp.wait_ge(s_ones_seed, 1)
                ones = stack[SROWS:MROWS, 0, 0, 0:512]
                sp.dma_start(stack[SROWS:MROWS, 0, :, :].rearrange("p j (c n) -> p (j c) n", n=512)[:, 1:32, :],
                             ones.unsqueeze(1).broadcast_to([3, 31, 512])).then_inc(s_ones_even, 16)
                for part, made in (("h", s_k_high), ("m", s_k_mid), ("l", s_k_parts)):
                    sp.wait_ge(made, 4)
                    for j in range(GH):
                        for n in range(NS):
                            if KSLOT[n] == part:
                                sp.dma_start(stack[DH * n:DH * n + DH, 0, j, 0:2048],
                                             kparts[part][DH * j:DH * j + DH, 0:2048]).then_inc(s_slots_sp[0][0], 16)

            @block.gpsimd
            def _(pool):
                pool.memset(onesf[:, :], 1.0).then_inc(s_const, 1)
                link_pool(pool.memset(identf[:, :], 0.0))
                link_pool(pool.affine_select(out=identf[:, :], in_=identf[:, :], compare_op=ALU.not_equal, fill=1.0,
                                             base=0, pattern=[[-1, P]], channel_multiplier=1))
                pool.tensor_copy(identb[:, :], identf[:, :]).then_inc(s_const, 1)
                pool.memset(Qg[:, :, :, :], 0.0).then_inc(s_const, 1)
                for c in range(NCT - 2):
                    pool.wait_ge(s_k_mid, c + 1)
                    sl = slice(512 * c, 512 * c + 512)
                    pool.tensor_tensor(kl[:, sl], kr[:, c % 2, :], km[:, sl], ALU.subtract).then_inc(s_k_parts, 1)
                pool.wait_ge(s_const, 3)
                group_rows(pool, 0)

            @block.scalar
            def _(act):
                act.dma_start(wk[:, :], t_in["L0_xattn_Wk"]).then_inc(s_wk_in, 16)
                act.dma_start(bkc[:, :], t_in["L0_xattn_bk"].rearrange("(k p) -> p k", p=P),
                              allow_slow_non_contiguous=True).then_inc(s_wk_in, 16)
                act.dma_start(wq[:, :, :], t_in["L0_xattn_Wq"].rearrange("(k p) n -> p k n", p=P)).then_inc(s_wq_in, 16)
                act.dma_start(bqr[:, :], t_in["L0_xattn_bq"].rearrange("(a n) -> a n", a=1)).then_inc(s_wq_in, 16)
                act.wait_ge(s_var, 1)
                act.activation(sd[:, :], ve[:, :], ACT.Sqrt).then_inc(s_std, 1)
                for k in range(KT):
                    act.wait_ge(s_rowsT, k + 1)
                    act.activation(lnT[:, k, :], LB[k], ACT.Copy).then_inc(s_rowsT_read, 1)
                act.wait_ge(s_wk_in, 32)
                for c in range(NCT + 1):
                    if c < NCT:
                        act.wait_ge(s_k_made, c + 1)
                        act.activation(kh[:, 512 * c:512 * c + 512], KB[c % 2], ACT.Identity,
                                       bias=bkc[:, 0:1]).then_inc(s_k_high, 1)
                    if c >= 1:
                        act.wait_ge(s_k_rest, c)
                        act.activation(km[:, 512 * c - 512:512 * c], kr[:, (c - 1) % 2, :], ACT.Copy).then_inc(s_k_mid, 1)
                    if 3 <= c < 3 + RT:
                        act.wait_ge(s_q_made, c - 2)
                        act.activation(qf[:, c - 3, :], QB[(c - 3) % 2], ACT.Copy).then_inc(s_q_read, 1)

            @block.vector
            def _(dve):
                dve.memset(stack[SROWS:MROWS, 0, 0, 0:512], 1.0).then_inc(s_ones_seed, 1)
                dve.memset(Vg[:, :, :], 1.0).then_inc(s_ones_seed, 1)
                dve.wait_ge(s_x_in, 16)
                row_stats(dve, X)
                dve.tensor_scalar(ve[:, :], mv[:, :, 1], 1e-5, None, ALU.add).then_inc(s_var, 1)
                dve.wait_ge(s_std, 1)
                link_dve(dve.reciprocal(rs[:, :], sd[:, :]))
                for R in range(RT):
                    dve.tensor_scalar(lnx[:, R, :], X[:, R, :], mv[:, R, 0:1], rs[:, R:R + 1],
                                      ALU.subtract, ALU.mult).then_inc(s_rows_normed, 1)
                for c in range(NCT + 1):
                    if c < NCT:
                        dve.wait_ge(s_ctxT, c + 1)
                        dve.tensor_copy(ctxT[:, 0, 512 * c:512 * c + 512], CB[c % 2]).then_inc(s_ctxT_read, 1)
                    if c >= 1:
                        dve.wait_ge(s_k_high, c)
                        if c >= 3:
                            dve.wait_ge(s_k_parts, c - 2)
                        dve.scalar_tensor_tensor(out=kr[:, (c - 1) % 2, :], in0=KB[(c - 1) % 2], scalar=bkc[:, 0:1],
                                                 in1=kh[:, 512 * c - 512:512 * c], op0=ALU.add,
                                                 op1=ALU.subtract).then_inc(s_k_rest, 1)
                    if c in (5, NCT):
                        dve.wait_ge(s_q_read, 2 if c == 5 else RT)
                        t = slice(0, 2) if c == 5 else slice(2, 4)
                        link_dve(dve.tensor_copy(qh[:, t, :], qf[:, t, :]))
                        link_dve(dve.tensor_tensor(qf[:, t, :], qf[:, t, :], qh[:, t, :], ALU.subtract))
                        link_dve(dve.tensor_copy(qm[:, t, :], qf[:, t, :]))
                        dve.tensor_tensor(ql[:, t, :], qf[:, t, :], qm[:, t, :], ALU.subtract).then_inc(s_q_parts, 1)
                dve.wait_ge(s_k_parts, NCT - 2)
                for c in range(NCT - 2, NCT):
                    dve.wait_ge(s_k_mid, c + 1)
                    sl = slice(512 * c, 512 * c + 512)
                    dve.tensor_tensor(kl[:, sl], kr[:, c % 2, :], km[:, sl], ALU.subtract).then_inc(s_k_parts, 1)
            @block.tensor
            def _(pe):
                pe.wait_ge(s_const, 2)
                pe.wait_ge(s_rows_normed, RT)
                for k in range(KT):
                    for R in range(RT):
                        mm = pe.transpose(LB[k][:, P * R:P * R + P], lnx[:, R, P * k:P * k + P], identf[:, :])
                    mm.then_inc(s_rowsT, 1)
                pe.wait_ge(s_wk_in, 32)
                for c in range(NCT + 1):
                    if c < NCT:
                        if c % 2 == 0:
                            pe.wait_ge(s_ctx[c // 2], 16)
                        if c >= 2:
                            pe.wait_ge(s_ctxT_read, c - 1)
                        for i in range(4):
                            mm = pe.transpose(CB[c % 2][:, P * i:P * i + P], ctxn[:, 0, 4 * c + i, :], identf[:, :])
                        mm.then_inc(s_ctxT, 1)
                    if c >= 1:
                        pe.wait_ge(s_ctxT_read, c)
                        if c >= 3:
                            pe.wait_ge(s_k_rest, c - 2)
                        pe.matmul(KB[(c - 1) % 2], wk[:, 0:P], ctxT[:, 0, 512 * c - 512:512 * c],
                                  start=True, stop=True).then_inc(s_k_made, 1)
                    if 2 <= c < 2 + RT:
                        R = c - 2
                        if R == 0:
                            pe.wait_ge(s_wq_in, 32)
                            pe.wait_ge(s_rowsT_read, KT)
                        if R >= 2:
                            pe.wait_ge(s_q_read, R - 1)
                        for k in range(KT):
                            pe.matmul(QB[R % 2], lnT[:, k, P * R:P * R + P], wq[:, k, :], start=(k == 0), stop=False)
                        pe.matmul(QB[R % 2], onesf[0:1, :], bqr[:, :], start=False, stop=True).then_inc(s_q_made, 1)

        with nc.Block() as block:
            @block.sync
            def _(sp):
                load_slots_sp(sp, 0, 1)
                sp.wait_ge(s_spare_read, AUX_NO["C", 7] + 1)
                sp.dma_start(stack[SROWS:MROWS, 1, :, :], stack[SROWS:MROWS, 0, :, :]).then_inc(s_ones_odd, 16)
                for g in range(1, NG):
                    for half in range(2):
                        load_slots_sp(sp, g, half)
                    if g == 1:
                        for dst_, name in ((bqkv, "attn_Wqkv_b"), (b_out2, "attn_out_b")):
                            sp.dma_start(dst_, t_in["L0_" + name].partition_broadcast(P)).then_inc(s_w2_in, 16)
                        for dst_, name in ((b_o3, "ffn_ob"), (b_qkv3[:, 0:D], "ffn_qb"),
                                           (b_qkv3[:, D:D + 64], "ffn_kb"), (b_qkv3[:, D + 64:D + 128], "ffn_vb")):
                            sp.dma_start(dst_, t_in["L0_" + name].partition_broadcast(P)).then_inc(s_w3_in, 16)
                        sp.dma_start(wq[:, :, :], t_in["L0_ffn_qw"].rearrange("(k p) n -> p k n", p=P)).then_inc(s_w3_in, 16)
                for par in range(2):
                    for half in range(2):
                        wait_loaded(sp, NG - 2 + par, half)
                sp.dma_start(wraw[:, 0:6, :], t_in["L0_attn_Wqkv_w"].rearrange("(w p) k -> p w k", p=P)).then_inc(s_w2_in, 16)
                sp.dma_start(wraw[:, 6:8, :], t_in["L0_attn_out_w"].rearrange("(w p) k -> p w k", p=P)).then_inc(s_w2_in, 16)
                kv3 = wk.rearrange("p (k n) -> p k n", k=KT)
                sp.dma_start(kv3[:, :, 0:64], t_in["L0_ffn_kw"].rearrange("(k p) n -> p k n", p=P)).then_inc(s_w3_in, 16)
                sp.dma_start(kv3[:, :, 64:128], t_in["L0_ffn_vw"].rearrange("(k p) n -> p k n", p=P)).then_inc(s_w3_in, 16)
                sp.wait_ge(s_proj_zero, 1)
                for j in range(8):
                    sp.dma_start(projb[DH * j:DH * j + DH, M * j:M * j + M],
                                 t_in["L0_attn_proj"].rearrange("m d -> d m"),
                                 allow_slow_non_contiguous=True).then_inc(s_proj_in, 16)

            @block.gpsimd
            def _(pool):
                load_slots_pool(pool, 0, 1)
                for s in range(S0, SEND):
                    for kind, i in aux_of(s):
                        if kind == "K":
                            c = i % 8
                            pool.wait_ge(s_spare_read, AUX_NO[kind, i] + 1)
                            sl = slice(512 * c, 512 * c + 512)
                            if i >= 8:
                                for par in range(2):
                                    wait_loaded(pool, 2 * (i // 8) - 2 + par, c // 4)
                            link_pool(pool.tensor_copy(km[:, sl], kr[:, i % 2, :]))
                            pool.tensor_tensor(kl[:, sl], kr[:, i % 2, :], km[:, sl], ALU.subtract).then_inc(s_k_parts, 1)
                    for g in range(1, NG):
                        if s == SPG * (g - 1) - LEAD - 25:
                            group_rows(pool, g)
                    g, r = divmod(s + 2 * SPG, SPG)
                    if s == -28:
                        load_slots_pool(pool, 1, 0)
                        load_slots_pool(pool, 1, 1)
                    if s >= 0 and r == 16 and g < NG:
                        load_slots_pool(pool, g, 0)
                    if s > 0 and r == 0 and g - 1 < NG:
                        load_slots_pool(pool, g - 1, 1)
                pool.wait_ge(s_spare_read, AUX_NO["V", 31] + 1)
                pool.memset(projb, 0.0).then_inc(s_proj_zero, 1)
                pool.wait_ge(s_k_parts, 32)
                link_pool(pool.memset(maskq[:, :, :], 0.0))
                link_pool(pool.memset(maskk[:, :, :], 0.0))
                link_pool(pool.memset(wmask[:, :, :], 1.0))
                link_pool(pool.affine_select(out=maskq[:, :, :], in_=maskq[:, :, :], compare_op=ALU.is_ge,
                                             fill=-40000.0, base=0, pattern=[[P, 2], [-1, L]], channel_multiplier=1))
                link_pool(pool.affine_select(out=maskk[:, :, :], in_=maskk[:, :, :], compare_op=ALU.is_ge,
                                             fill=-40000.0, base=0, pattern=[[-P, 2], [1, L]], channel_multiplier=-1))
                link_pool(pool.affine_select(out=wmask[:, :, :], in_=wmask[:, :, :], compare_op=ALU.is_ge,
                                             fill=0.0, base=0, pattern=[[-P, 2], [1, L]], channel_multiplier=-1))
                link_pool(pool.affine_select(out=maskq[:, :, :], in_=maskq[:, :, :], compare_op=ALU.is_ge,
                                             fill=-40000.0, base=128, pattern=[[-P, 2], [1, L]],
                                             channel_multiplier=-1))
                link_pool(pool.affine_select(out=maskk[:, :, :], in_=maskk[:, :, :], compare_op=ALU.is_ge,
                                             fill=-40000.0, base=128, pattern=[[P, 2], [-1, L]],
                                             channel_multiplier=1))
                pool.tensor_copy(identh[:, :], identf[:, :])
                pool.wait_ge(s_q_slots, NG)
                link_pool(pool.memset(V2[:, :, :], 1.0))
                link_pool(pool.tensor_tensor(X[:, :, :], X[:, :, :], bor[:, :].unsqueeze(1).broadcast_to([P, RT, D]), ALU.add))
                pool.wait_ge(s_scores, SPG * (NG - 1))
                pool.memset(QN[:, :, :, SROWS:P], 0.0)
                pool.memset(KN[:, :, :, SROWS:P], 1.0)
                for g in range(NG):
                    b, hg = divmod(g, 4)
                    pool.wait_ge(s_spare_read, AUX_NO["OT", g] + 1)
                    a_ = att[:, 2 * b:2 * b + 2, 64 * hg:64 * hg + 64]
                    pool.tensor_tensor(a_, a_, bvb[:, 64 * hg:64 * hg + 64].unsqueeze(1).broadcast_to([P, 2, 64]), ALU.add)

            @block.scalar
            def _(act):
                for s in range(S0, SEND + 8):
                    if 0 <= s < SEND:
                        act.wait_ge(s_scores, s + 1)
                        if s >= 3:
                            act.wait_ge(s_sums, s - 2)
                        act.activation(PT[:, s % 3, :], ST[s % 2], ACT.Exp, scale=SCALE).then_inc(s_probs, 1)
                    if s > SPG and s % SPG == 1:
                        g = s // SPG - 1
                        act.wait_ge(s_sums, SPG * (g + 1))
                        if g >= 1:
                            act.wait_ge(s_spare_read, AUX_NO["OT", g - 1] + 1)
                        act.activation(OTs[:, :], ACC[:, 0:L], ACT.Copy).then_inc(s_sums_read, 1)
                    for kind, i in aux_of(s):
                        if kind == "C":
                            act.wait_ge(s_spare_full, AUX_NO[kind, i] + 1)
                            act.activation(ctxT[:, 1, 512 * i:512 * i + 512], AUXB, ACT.Copy).then_inc(s_spare_read, 1)
                        if kind == "K":
                            half, c = (i // 8) % 2, i % 8
                            act.wait_ge(s_spare_full, AUX_NO[kind, i] + 1)
                            if i >= 8:
                                for par in range(2):
                                    wait_loaded(act, 2 * (i // 8) - 2 + par, c // 4)
                            act.activation(kh[:, 512 * c:512 * c + 512], AUXB, ACT.Identity,
                                           bias=bkc[:, half:half + 1]).then_inc(s_spare_k_high, 1)
                        if kind == "V":
                            hf, v = divmod(i, 8)
                            act.wait_ge(s_spare_full, AUX_NO[kind, i] + 1)
                            for gg in range(2):
                                if hf >= 1:
                                    act.wait_ge(s_sums, SPG * (2 * hf - 2 + gg) + 4 * v + 4)
                                o = Vg[:, gg, 4 * v * GH * VW:(4 * v + 4) * GH * VW].rearrange(
                                    "p (t j d) -> p t j d", t=4, d=VW)
                                src = AUXB.rearrange("p (t g j d) -> p t g j d", t=4, g=2, d=DH)
                                ins = act.activation(o[:, :, :, 0:DH], src[:, :, gg], ACT.Copy)
                            ins.then_inc(s_spare_read, 1)

            @block.vector
            def _(dve):
                for s in range(S0, SEND + 8):
                    for n in units_of(s):
                        g, u = divmod(n, UPG)
                        if n >= UPG:
                            dve.wait_ge(s_max_scores, n + 1)
                            dve.tensor_reduce(mx[:, g % 2, u % 8, u // 8:u // 8 + 1], max_bank(n), AX.X,
                                              ALU.max).then_inc(s_max_reduced, 1)
                        elif n % 2:
                            dve.wait_ge(s_max_scores, n + 1)
                            at = (4, 0, 2)[n // 2 % 3]
                            dve.tensor_reduce(mx[:, 0, u % 8 - 1:u % 8 + 1, u // 8], ps[:, at:at + 2, :], AX.X,
                                              ALU.max).then_inc(s_max_reduced, 2)
                        if u == UPG - 1:
                            dve.wait_ge(s_max_reduced, n + 1)
                            q = Qg[:, g % 2, :, :]
                            link_dve(dve.tensor_reduce(nm[:, :], mx[:, g % 2, :, :], AX.X, ALU.max, negate=True))
                            link_dve(dve.tensor_copy(q[:, :, SROWS], nm[:, :]))
                            link_dve(dve.tensor_tensor(nr[:, :], nm[:, :], q[:, :, SROWS], ALU.subtract))
                            link_dve(dve.tensor_copy(q[:, :, SROWS + 1], nr[:, :]))
                            dve.tensor_tensor(q[:, :, SROWS + 2], nr[:, :], q[:, :, SROWS + 1],
                                              ALU.subtract).then_inc(s_max_parts, 1)
                    for kind, i in aux_of(s):
                        a = AUX_NO[kind, i]
                        if kind == "K":
                            dve.wait_ge(s_spare_k_high, i - 7)
                            if i >= 2:
                                dve.wait_ge(s_k_parts, i - 1)
                            half, c = (i // 8) % 2, i % 8
                            dve.scalar_tensor_tensor(out=kr[:, i % 2, :], in0=AUXB, scalar=bkc[:, half:half + 1],
                                                     in1=kh[:, 512 * c:512 * c + 512], op0=ALU.add,
                                                     op1=ALU.subtract).then_inc(s_spare_read, 1)
                        if kind in ("QS", "QT"):
                            dve.wait_ge(s_spare_full, a + 1)
                            dve.tensor_copy((QS if kind == "QS" else QT)[:, i % 2, :],
                                            AUXB.bitcast(BF16)).then_inc(s_spare_read, 1)
                        if kind == "OT":
                            b, hg = divmod(i, 4)
                            dve.wait_ge(s_spare_full, a + 1)
                            o = AUXB[:, 0:2 * P].rearrange("p (q j d) -> p q j d", q=2, d=32)
                            link_dve(dve.reciprocal(rec[:, :, :], o[:, :, :, DH]))
                            dst = att[:, 2 * b:2 * b + 2, 64 * hg:64 * hg + 64].rearrange("p q (j d) -> p q j d", d=DH)
                            for q in range(2):
                                ins = dve.tensor_tensor(dst[:, q], o[:, q, :, 0:DH],
                                                        rec[:, q, :].unsqueeze(2).broadcast_to([P, GH, DH]), ALU.mult)
                            ins.then_inc(s_spare_read, 1)

            @block.tensor
            def _(pe):
                def maximum_unit(n):
                    g, u = divmod(n, UPG)
                    c, r = divmod(u, 8)
                    if u == 0:
                        pe.wait_ge(s_spare_read, AUX_NO["QS", g] + 1)
                    if u % 32 == 0:
                        wait_loaded(pe, g, u // 32)
                    m = 6 if n < UPG else 2
                    if n >= m:
                        pe.wait_ge(s_max_reduced, n - m + 1)
                    pe.matmul(max_bank(n), QS[0:SROWS, g % 2, P * r:P * r + P],
                              stack[0:SROWS, g % 2, r // 2, 512 * c:512 * c + 512],
                              start=True, stop=True).then_inc(s_max_scores, 1)

                def values(i, q):
                    b, half = divmod(i // 8, 2)
                    t = 4 * (i % 8) + q
                    return pe.matmul(AUXB[:, P * q:P * q + P], ctxT[:, b, P * t:P * t + P],
                                     wv[:, P * half:P * half + P], start=True, stop=True)

                def piece(kind, i, q):
                    if q == 0:
                        pe.wait_ge(s_spare_read, AUX_NO[kind, i])
                    if kind == "V":
                        mm = values(i, q)
                    else:
                        b, half = divmod(i // 8, 2)
                        at = 512 * (i % 8) + P * q
                        mm = pe.matmul(AUXB[:, P * q:P * q + P], wk[:, P * half:P * half + P], ctxT[:, b, at:at + P],
                                       start=True, stop=True)
                    if q == 3:
                        mm.then_inc(s_spare_full, 1)

                pe.wait_ge(s_wvo_in, 64)
                pe.wait_ge(s_ones_even, 16)
                for s in range(S0, SEND + 8):
                    if 0 <= s < SEND:
                        g, t = divmod(s, SPG)
                        if s >= 2:
                            pe.wait_ge(s_probs, s - 1)
                        if t == 0:
                            pe.wait_ge(s_spare_read, AUX_NO["QT", g] + 1)
                        if s == SPG:
                            pe.wait_ge(s_ones_odd, 16)
                        for j in range(GH):
                            mm = pe.matmul(ST[s % 2][:, j // 2, 256 * (j % 2):256 * (j % 2) + 256],
                                           stack[0:MROWS, g % 2, j, P * t:P * t + P],
                                           QT[0:MROWS, g % 2, L * j:L * j + L], start=True, stop=True)
                        mm.then_inc(s_scores, 1)
                    if 2 <= s < SEND + 2:
                        g, t = divmod(s - 2, SPG)
                        pe.wait_ge(s_probs, s - 1)
                        if t == 0 and g >= 1:
                            pe.wait_ge(s_sums_read, g)
                        if t % 4 == 0:
                            pe.wait_ge(s_spare_read, AUX_NO["V", 8 * (g // 2) + t // 4] + 1)
                        for j in range(GH):
                            v0 = (GH * t + j) * VW
                            mm = pe.matmul(ACC[32 * j:32 * j + 32, 0:L], Vg[:, g % 2, v0:v0 + 32],
                                           PT[:, (s - 2) % 3, L * j:L * j + L], start=(t == 0), stop=(t == SPG - 1))
                        mm.then_inc(s_sums, 1)
                    begun = [(kind, i, 0) for kind, i in aux_of(s + 1) if kind in "KV" and i >= 8]
                    ended = [(kind, i, 2) for kind, i in aux_of(s) if kind in "KV" and i >= 8]
                    pieces = [(kind, i, q + p) for kind, i, q in ended + begun for p in range(2)]
                    assert len(pieces) <= 2
                    for p in range(2):
                        for n in units_of(s)[p:p + 1]:
                            maximum_unit(n)
                        for kind, i, q in pieces[p:p + 1]:
                            piece(kind, i, q)
                    for kind, i in aux_of(s):
                        if kind in "KV" and i >= 8:
                            continue
                        a = AUX_NO[kind, i]
                        if a:
                            pe.wait_ge(s_spare_read, a)
                        if kind == "C":
                            if i % 2 == 0:
                                pe.wait_ge(s_ctx[4 + i // 2], 16)
                            for q in range(4):
                                mm = pe.transpose(AUXB[:, P * q:P * q + P], ctxn[:, 1, 4 * i + q, :], identf[:, :])
                        if kind == "V":
                            for q in range(4):
                                mm = values(i, q)
                        if kind in ("QS", "QT"):
                            pe.wait_ge(s_q_slots if kind == "QS" else s_max_parts, i + 1)
                            for r in range(2 * GH):
                                mm = pe.transpose(AUXB.bitcast(BF16)[:, P * r:P * r + P], Qg[:, i % 2, r, :],
                                                  identb[:, :])
                        if kind == "OT":
                            pe.wait_ge(s_sums_read, i + 1)
                            for q in range(2):
                                mm = pe.transpose(AUXB[:, P * q:P * q + P], OTs[:, P * q:P * q + P], identf[:, :])
                        mm.then_inc(s_spare_full, 1)


        qls = small[:, 0:64].rearrange("p (r h) -> p r h", h=H)
        mkx = small[:, 64:128]
        kls = small[:, 128:160].rearrange("p (b h) -> p b h", h=H)
        nmall = small[:, 160:224].rearrange("p (r h) -> p r h", h=H)
        t0 = small[:, 224:288].rearrange("p (r h) -> p r h", h=H)
        t1 = small[:, 288:352].rearrange("p (r h) -> p r h", h=H)
        t2 = small[:, 352:416].rearrange("p (r h) -> p r h", h=H)
        t3 = small[:, 416:480].rearrange("p (r h) -> p r h", h=H)
        mkc = small[0:64, 480:481]
        mkr = small[0:1, 484:516]
        nrs = small[:, 516:524].rearrange("p (q j) -> p q j", j=GH)
        small_eps = small[:, 528:529]
        sqs = small[:, 544:672].rearrange("p (r n h) -> p r n h", n=2, h=H)
        ksub = small[:, 672:736].rearrange("p (r h) -> p r h", h=H)

        PB = [ps[:, i, 0:D] for i in (0, 1, 6, 7)]

        RH = [slice(0, 2), slice(2, 4)]

        def half_stats(dve, rows, r):
            for R in (2 * r, 2 * r + 1):
                ins = dve.bn_stats(bst[:, R, :], rows[:, R, :])
            link_dve(ins)
            for R in (2 * r, 2 * r + 1):
                ins = dve.bn_aggr(mv[:, R, :], bst[:, R, :])
            link_dve(ins)

        def ln_dve(dve, n, r):
            t = RH[r]
            half_stats(dve, X, r)
            dve.tensor_scalar(ve[:, t], mv[:, t, 1], 1e-5, None, ALU.add).then_inc(s_var, 1)
            dve.wait_ge(s_std, 2 * n + r)
            link_dve(dve.reciprocal(rs[:, t], sd[:, t]))
            for R in (2 * r, 2 * r + 1):
                dve.tensor_scalar(lnx[:, R, :], X[:, R, :], mv[:, R, 0:1], rs[:, R:R + 1],
                                  ALU.subtract, ALU.mult).then_inc(s_rows_normed, 1)

        def ln_act(act, n, r):
            act.wait_ge(s_var, 2 * n + r)
            act.activation(sd[:, RH[r]], ve[:, RH[r]], ACT.Sqrt).then_inc(s_std, 1)

        def rows_T_pe(pe, src, r):
            for k in range(KT):
                for q in range(2):
                    mm = pe.transpose(LB[r][:, 2 * P * k + P * q:2 * P * k + P * q + P],
                                      src[:, 2 * r + q, P * k:P * k + P], identf[:, :])
            mm.then_inc(s_rowsT, 1)

        def rows_T_act(act, n, r):
            act.wait_ge(s_rowsT, 2 * n + r + 1)
            act.activation(lnT[:, :, 2 * P * r:2 * P * r + 2 * P], LB[r].rearrange("p (k n) -> p k n", k=KT),
                           ACT.Copy).then_inc(s_rowsT_read, 1)

        def project_pe(pe, w, R):
            for k in range(KT):
                mm = pe.matmul(PB[R], lnT[:, k, P * R:P * R + P], w[:, k, :], start=(k == 0), stop=(k == KT - 1))
            mm.then_inc(s_projected, 1)

        def residual_dve(dve, n, r, rows):
            for R in (2 * r, 2 * r + 1):
                dve.wait_ge(s_projected, RT * n + R + 1)
                ins = dve.tensor_tensor(rows[:, R, :], rows[:, R, :], PB[R], ALU.add)
            link_dve(ins)

        def slots_of(T, R, nh, first, step=1, w=DH):
            t = T[:, R, 0:nh, 0:P // w * w].rearrange("p h (s d) -> p h s d", d=w)
            return t[:, :, first:first + step + 1:step, :] if step > 1 else t[:, :, first, :]

        def both(x, nh, w=DH):
            return x.unsqueeze(2).broadcast_to([P, nh, 2, w])

        def high_act(act, R, nk, n):
            q_ = QK[:, R, 0:D].rearrange("p (h d) -> p h d", d=DH)
            k_ = QK[:, R, D:D + DH * nk].rearrange("p (h d) -> p h d", d=DH)
            act.wait_ge(s_qk_read, n)
            act.activation(slots_of(QN, R, H, 0), q_, ACT.Copy)
            act.activation(slots_of(KN, R, nk, 0), k_, ACT.Copy).then_inc(s_qk_high, 1)
            act.activation(slots_of(QN, R, H, 2, 3), both(q_, H), ACT.Copy)
            act.activation(slots_of(KN, R, nk, 1, 3), both(k_, nk), ACT.Copy)

        def lower_dve(dve, R, nk, n):
            q_ = QK[:, R, 0:D].rearrange("p (h d) -> p h d", d=DH)
            k_ = QK[:, R, D:D + DH * nk].rearrange("p (h d) -> p h d", d=DH)
            rest = att[:, 2 * (R % 2):2 * (R % 2) + 2, :].rearrange("p a n -> p (a n)")
            rq = rest[:, 0:D].rearrange("p (h d) -> p h d", d=DH)
            rk = rest[:, D:D + DH * nk].rearrange("p (h d) -> p h d", d=DH)
            dve.wait_ge(s_qk_high, n)
            dve.tensor_tensor(rq, q_, slots_of(QN, R, H, 0), ALU.subtract)
            link_dve(dve.tensor_tensor(rk, k_, slots_of(KN, R, nk, 0), ALU.subtract))
            dve.tensor_copy(slots_of(QN, R, H, 3), rq)
            link_dve(dve.tensor_copy(slots_of(KN, R, nk, 3), rk))
            dve.tensor_tensor(slots_of(QN, R, H, 4), rq, slots_of(QN, R, H, 3), ALU.subtract)
            link_dve(dve.tensor_tensor(slots_of(KN, R, nk, 5), rk, slots_of(KN, R, nk, 3), ALU.subtract))
            dve.sem_inc(s_qk_lower, 1)

        def middle_pool(pool, R, nk, n):
            pool.wait_ge(s_qk_lower, n)
            pool.tensor_copy(slots_of(QN, R, H, 1), slots_of(QN, R, H, 3))
            pool.tensor_copy(slots_of(KN, R, nk, 2), slots_of(KN, R, nk, 3))

        def features_high(act, r):
            t = RH[r]
            for side, (f, T) in enumerate(((fk, FK), (fq, FQ))):
                if r == 0:
                    act.wait_ge(s_logs_done, side + 1)
                act.activation(f[:, t], f[:, t], ACT.Exp).then_inc(s_feat_exp, 1)
                act.wait_ge(s_feat_exp, 2 * r + side + 1)
                act.activation(T[:, t, :, 0:M], f[:, t], ACT.Identity, bias=small_eps).then_inc(s_feat_high, 1)

        def features_lower(dve, side, r):
            f, T = ((fk, FK), (fq, FQ))[side]
            t = RH[r]
            dve.wait_ge(s_feat_high, 2 * r + side + 1)
            link_dve(dve.scalar_tensor_tensor(out=f[:, t], in0=f[:, t], scalar=1e-4, in1=T[:, t, :, 0:M],
                                              op0=ALU.add, op1=ALU.subtract))
            link_dve(dve.tensor_copy(T[:, t, :, 3 * M:4 * M], f[:, t]))
            lo = FKL[:, t] if side == 0 else T[:, t, :, 4 * M:5 * M]
            dve.tensor_tensor(lo, f[:, t], T[:, t, :, 3 * M:4 * M], ALU.subtract).then_inc(s_feat_lower, 1)

        def features_repeat(act, r):
            t = RH[r]
            act.wait_ge(s_feat_high, 2 * r + 2)
            for T, at in ((FK, (1, 4)), (FQ, (2,))):
                for c in at:
                    act.activation(T[:, t, :, M * c:M * c + M], T[:, t, :, 0:M], ACT.Copy)
            act.wait_ge(s_feat_lower, 2 * r + 2)
            act.activation(FQ[:, t, :, M:2 * M], FQ[:, t, :, 3 * M:4 * M], ACT.Copy).then_inc(s_feat_all, 1)

        def features_repeat_pool(pool, r):
            pool.wait_ge(s_feat_lower, 2 * r + 1)
            for R in range(2 * r, 2 * r + 2):
                ins = pool.tensor_copy(slots_of(FK, R, H, 2, 1, M), slots_of(FK, R, H, 3, 1, M))
            ins.then_inc(s_feat_all, 1)

        WB = [ps[:, 2, :], ps[:, 3, :]]
        QKB = [ps[:, i, :] for i in (2, 0, 6, 4)]
        VB = [ps[:, i, 0:D] for i in (3, 1, 7, 5)]
        with nc.Block() as block:
            @block.gpsimd
            def _(pool):
                pool.memset(FQ[:, :, :, 5 * M:P], 0.0)
                pool.memset(FK[:, :, :, 5 * M:P], 0.0)
                for R in range(RT):
                    middle_pool(pool, R, H, R + 1)
                pool.wait_ge(s_rows_normed, 2 * RT)
                pool.tensor_tensor(X[:, :, :], X[:, :, :], b_out2.unsqueeze(1).broadcast_to([P, RT, D]), ALU.add)
                features_repeat_pool(pool, 0)

            @block.scalar
            def _(act):
                rows_T_act(act, 1, 0)
                rows_T_act(act, 1, 1)
                for w in range(8):
                    if w == 4:
                        ln_act(act, 1, 0)
                    act.wait_ge(s_wT, w + 1)
                    o = wqkvT[:, :, P * w:P * w + P] if w < 6 else woT2[:, :, P * (w - 6):P * (w - 6) + P]
                    act.activation(o, WB[w % 2][:, 0:2 * P].rearrange("p (k n) -> p k n", k=KT),
                                   ACT.Copy).then_inc(s_wT_read, 1)
                rows_T_act(act, 2, 0)
                ln_act(act, 1, 1)
                rows_T_act(act, 2, 1)
                for R in range(RT):
                    high_act(act, R, H, R + 1)
                    act.activation(xsq[:, R, :], QK[:, R, :], ACT.Square).then_inc(s_squares, 1)
                for n in range(4):
                    side, k = divmod(n, KT)
                    act.wait_ge(s_qkT, n + 1)
                    act.activation(xT[:, side, k, :], ps[:, 4 + n, :], ACT.Copy, scale=0.5).then_inc(s_qkT_read, 1)
                features_high(act, 0)
                features_repeat(act, 0)

            @block.vector
            def _(dve):
                dve.memset(small_eps, 1e-4).then_inc(s_eps_made, 1)
                for r in range(2):
                    residual_dve(dve, 0, r, X)
                    ln_dve(dve, 1, r)
                sc = acc[:, 0:2, :]
                link_dve(dve.tensor_scalar(sc, maskk[:, :, :], 0.0, 0.25, ALU.is_equal, ALU.mult))
                link_dve(dve.tensor_tensor(wmask[:, :, :], wmask[:, :, :], sc, ALU.subtract))
                for R in range(RT + 1):
                    if R < RT:
                        dve.wait_ge(s_qkv_made, 2 * R + 1)
                        dve.tensor_tensor(QK[:, R, :], QKB[R], bqkv[:, 0:2 * D], ALU.add).then_inc(s_qk_read, 1)
                        dve.wait_ge(s_qkv_made, 2 * R + 2)
                        dve.tensor_tensor(V2[:, R, 0:H * VW].rearrange("p (h d) -> p h d", d=VW)[:, :, 0:DH],
                                          VB[R].rearrange("p (h d) -> p h d", d=DH),
                                          bqkv[:, 2 * D:3 * D].rearrange("p (h d) -> p h d", d=DH),
                                          ALU.add).then_inc(s_v_read, 1)
                    if 1 <= R < RT:
                        lower_dve(dve, R - 1, H, R)
                def logs(side, R):
                    return ps[:, 4 * side + R, 0:H * M].rearrange("p (h m) -> p h m", m=M)

                def less_max_q(R):
                    dve.wait_ge(s_logs, RT + R + 1)
                    link_dve(dve.tensor_reduce(qls[:, R, :], logs(1, R), AX.X, ALU.max))
                    dve.tensor_tensor(fq[:, R], logs(1, R), qls[:, R, :].unsqueeze(2).broadcast_to([P, H, M]),
                                      ALU.subtract).then_inc(s_logs_q, 1)

                for R in range(RT):
                    dve.wait_ge(s_squares, R + 1)
                    ins = dve.tensor_reduce(sqs[:, R], xsq[:, R, :].rearrange("p (n h d) -> p n h d", n=2, d=DH),
                                            AX.X, ALU.add)
                link_dve(ins)
                link_dve(dve.tensor_scalar(sqs, sqs, 0.125, None, ALU.mult))
                for R in range(RT):
                    dve.wait_ge(s_logs, R + 1)
                    ins = dve.tensor_reduce(mkx[:, H * R:H * R + H], logs(0, R), AX.X, ALU.max)
                link_dve(ins)
                mk_ = mkx.rearrange("p (r h) -> p r h", h=H)
                dve.tensor_tensor(mk_, mk_, sqs[:, :, 1], ALU.subtract).then_inc(s_kmax_rows, 1)
                lower_dve(dve, RT - 1, H, RT)
                dve.wait_ge(s_kmaxT, 1)
                dve.tensor_reduce(mkc, ps[0:64, 0, 384:384 + P], AX.X, ALU.max).then_inc(s_kmax_reduced, 1)
                less_max_q(0)
                dve.wait_ge(s_kmaxT, 2)
                dve.tensor_reduce(mkr.rearrange("p (b h) -> p b h", b=B),
                                  ps[0:1, 1, 384:448].rearrange("p (b q h) -> p b h q", b=B, q=2),
                                  AX.X, ALU.max).then_inc(s_kmax_reduced, 1)
                less_max_q(1)
                dve.wait_ge(s_kmaxT, 3)
                link_dve(dve.tensor_copy(kls, ps[:, 2, 384:416].rearrange("p (b h) -> p b h", b=B)))
                for b in range(B):
                    ins = dve.tensor_tensor(ksub[:, 2 * b:2 * b + 2], sqs[:, 2 * b:2 * b + 2, 1],
                                            kls[:, b, :].unsqueeze(1).broadcast_to([P, 2, H]), ALU.add)
                link_dve(ins)
                for R in range(RT):
                    ins = dve.tensor_tensor(fk[:, R], logs(0, R), ksub[:, R, :].unsqueeze(2).broadcast_to([P, H, M]),
                                            ALU.subtract)
                link_dve(ins)
                dve.sem_inc(s_logs_done, 1)
                less_max_q(2)
                less_max_q(3)
                dve.wait_ge(s_logs_q, RT)
                dve.sem_inc(s_logs_done, 1)
                link_dve(dve.tensor_tensor(qls, qls, sqs[:, :, 0], ALU.subtract))
                features_lower(dve, 0, 0)
                features_lower(dve, 1, 0)

            @block.tensor
            def _(pe):
                rows_T_pe(pe, att, 0)
                rows_T_pe(pe, att, 1)
                pe.wait_ge(s_w2_in, 64)
                for R in range(RT):
                    if R % 2 == 0:
                        pe.wait_ge(s_rowsT_read, 2 + R // 2 + 1)
                    project_pe(pe, wo, R)
                    for w in (2 * R, 2 * R + 1):
                        if w >= 2:
                            pe.wait_ge(s_wT_read, w - 1)
                        for k in range(KT):
                            mm = pe.transpose(WB[w % 2][:, P * k:P * k + P], wraw[:, w, P * k:P * k + P], identf[:, :])
                        mm.then_inc(s_wT, 1)
                for R in range(RT):
                    if R % 2 == 0:
                        r = R // 2
                        pe.wait_ge(s_rows_normed, RT + 2 * r + 2)
                        rows_T_pe(pe, lnx, r)
                        pe.wait_ge(s_rowsT_read, 4 + r + 1)
                        pe.wait_ge(s_wT_read, 8)
                    for o, lo, hi in ((QKB[R], 0, 2 * D), (VB[R], 2 * D, 3 * D)):
                        for k in range(KT):
                            mm = pe.matmul(o, lnT[:, k, P * R:P * R + P], wqkvT[:, k, lo:hi],
                                           start=(k == 0), stop=(k == KT - 1))
                        mm.then_inc(s_qkv_made, 1)
                for n in range(4):
                    side, k = divmod(n, KT)
                    if n == 0:
                        pe.wait_ge(s_qk_read, RT)
                        pe.wait_ge(s_v_read, RT)
                    for R in range(RT):
                        at = D * (1 - side) + P * k
                        mm = pe.transpose(ps[:, 4 + n, P * R:P * R + P], QK[:, R, at:at + P], identf[:, :])
                    mm.then_inc(s_qkT, 1)
                pe.wait_ge(s_proj_in, 16 * 8)
                for side in range(2):
                    pe.wait_ge(s_qkT_read, 2 * side + 2)
                    for R in range(RT):
                        for k in range(KT):
                            o = ps[:, 4 * side + R, 8 * M * k:8 * M * k + 8 * M]
                            mm = pe.matmul(o, xT[:, side, k, P * R:P * R + P], projb, start=True, stop=True)
                        mm.then_inc(s_logs, 1)
                        if side == 1 and R == 1:
                            pe.wait_ge(s_kmax_rows, 1)
                            pe.transpose(ps[0:64, 0, 384:384 + P], mkx, identf[:, :]).then_inc(s_kmaxT, 1)
                        if side == 1 and R == 2:
                            pe.wait_ge(s_kmax_reduced, 1)
                            pe.transpose(ps[0:1, 1, 384:448], mkc, identf[0:64, 0:64]).then_inc(s_kmaxT, 1)
                        if side == 1 and R == 3:
                            pe.wait_ge(s_kmax_reduced, 2)
                            pe.matmul(ps[:, 2, 384:416], onesf[0:1, :], mkr, start=True, stop=True).then_inc(s_kmaxT, 1)

        ts = {n: sem(n) for n in ("a_t", "a_td_act", "a_td_dve", "a_s", "a_sr", "a_mp", "a_st", "a_exp", "a_gm",
                                  "a_pv", "a_pg", "a_acc", "a_accg")}
        base = {n: 0 for n in ts}

        def attention(masked):
            def turn_T(i):
                out = []
                if 0 <= i - 1 < NG:
                    out += [("QT", i - 1, "dve")]
                if masked and i >= 2:
                    out += [("O", i - 2, "dve")]
                if masked and 0 <= i < NG:
                    out += [("FQ", i, "act")]
                if masked and i >= 2:
                    out += [("OG", i - 2, "dve")]
                if masked and 0 <= i < NG:
                    out += [("FK", i, "act")]
                if i + 1 < NG:
                    out += [("Q", i + 1, "dve" if masked else "act"), ("K", i + 1, "act")]
                if masked and 0 <= i < NG:
                    out += [("FKL", i, "act")]
                if not masked and i >= 2:
                    out += [("O", i - 2, "dve")]
                return out
            uses = [u for i in range(-1, NG + 2) for u in turn_T(i)]
            use_no = {u[:2]: n for n, u in enumerate(uses)}

            def after(name, n):
                return ts[name], base_at[name] + n

            def read(n):
                who = uses[n][2]
                return after("a_td_" + who, sum(u[2] == who for u in uses[:n + 1]))

            def bank(n):
                return ps[:, n % 2, :]

            base_at = dict(base)
            NKJ = GH if masked else 1
            KC = KSg if masked else KSg.rearrange("p a n -> p (a n)").rearrange("p (a n) -> p a n", n=2 * P)
            KBUF = 2 if masked else 4
            PTn = PT[:, 0:2, :]
            src = {"Q": QN, "QT": QN, "K": KN, "FQ": FQ, "FK": FK}
            dst = {"Q": QS, "QT": QT, "K": KC, "FQ": FQT, "FK": FKT, "FKL": FKLT}

            sg = []
            for i in range(NG + 1):
                for q in range(2):
                    if i < NG:
                        sg += [("S", i, q, 0), ("S", i, q, 1)]
                for k in range(2):
                    if masked and i >= 1:
                        sg += [("G", i - 1, k, 0), ("G", i - 1, k, 1)]
            sg_no = {u: n for n, u in enumerate(sg)}
            SGB = (2, 3) if masked else (2, 3, 7)

            def from_q(k):
                return P if k == 1 else 0

            with nc.Block() as block:
                if masked:
                    @block.gpsimd
                    def _(pool):
                        features_repeat_pool(pool, 1)

                    @block.sync
                    def _(sp):
                        for e in range(E):
                            sp.dma_start(w1[:, e, :, :], t_in["L0_ffn_w1"][e].rearrange("(k p) f -> p k f", p=P))\
                              .then_inc(s_experts_in, 16)
                        sp.dma_start(wo[:, :, :], t_in["L0_ffn_ow"].rearrange("(k p) n -> p k n", p=P)).then_inc(s_w3_in, 16)
                else:
                    @block.sync
                    def _(sp):
                        for e in range(E):
                            sp.dma_start(w2[:, e, :, :], t_in["L0_ffn_w2"][e].rearrange("(k p) f -> p k f", p=P))\
                              .then_inc(s_experts_in, 16)

                @block.tensor
                def _(pe):
                    def rows_T(kind, g):
                        n = use_no[kind, g]
                        if n >= 2:
                            pe.wait_ge(*read(n - 2))
                        b, hg = divmod(g, 4)
                        o = bank(n).bitcast(BF16)
                        if kind == "QT":
                            pe.wait_ge(*after("a_mp", g + 1))
                        if kind == "FQ" and g == NG // 2:
                            pe.wait_ge(s_feat_all, 4)
                        for j in range(NKJ if kind == "K" else GH):
                            for q in range(2):
                                r = 2 * j + q
                                h = 4 * hg + j
                                if kind == "K" and not masked:
                                    h = hg
                                if kind == "FKL":
                                    mm = pe.transpose(o[0:M, P * r:P * r + P], FKL[:, 2 * b + q, h, :], identb[:, :])
                                else:
                                    mm = pe.transpose(o[:, P * r:P * r + P], src[kind][:, 2 * b + q, h, :], identb[:, :])
                        mm.then_inc(ts["a_t"], 1)

                    def sums_T(kind, g):
                        n = use_no[kind, g]
                        pe.wait_ge(*read(n - 2))
                        pe.wait_ge(*after("a_acc" if kind == "O" else "a_accg", g + 1))
                        o_ = OTs if kind == "O" else OTg
                        for q in range(2):
                            mm = pe.transpose(bank(n)[:, P * q:P * q + P], o_[:, P * q:P * q + P], identf[:, :])
                        mm.then_inc(ts["a_t"], 1)

                    def sg_bank(u):
                        n = sg_no[u]
                        if n >= len(SGB):
                            pe.wait_ge(*after("a_sr", n - len(SGB) + 1))
                        return ps[:, SGB[n % len(SGB)], :]

                    def scores_q(g, q, a):
                        o = sg_bank(("S", g, q, a))
                        if q == 0 and a == 0:
                            pe.wait_ge(*read(use_no["Q", g]))
                            pe.wait_ge(*read(use_no["K", g]))
                        o = o.rearrange("p (j n) -> p j n", n=L)
                        if masked:
                            pe.matmul(o, identh[:, :], maskq[:, q, :].unsqueeze(1).broadcast_to([P, 2, L]),
                                      start=True, stop=False, skip_group_check=True)
                        for jj in range(2):
                            j = 2 * a + jj
                            jk = j if masked else 0
                            mm = pe.matmul(o[:, jj], QS[0:SROWS, g % 2, P * (2 * j + q):P * (2 * j + q) + P],
                                           KC[0:SROWS, g % KBUF, L * jk:L * jk + L],
                                           start=not masked, stop=True, skip_group_check=True)
                        mm.then_inc(ts["a_s"], 1)

                    def scores_k(g, k):
                        if k == 0:
                            pe.wait_ge(*read(use_no["QT", g]))
                        if 2 * g + k >= 1:
                            pe.wait_ge(*after("a_exp", 2 * g + k))
                        for a in range(2):
                            o = ps[:, 4 + a, :].rearrange("p (j n) -> p j n", n=L)
                            if masked:
                                pe.matmul(o, identh[:, :], maskk[:, k, :].unsqueeze(1).broadcast_to([P, 2, L]),
                                          start=True, stop=False, skip_group_check=True)
                            for jj in range(2):
                                j = 2 * a + jj
                                jk = j if masked else 0
                                mm = pe.matmul(o[:, jj], KC[0:MROWS, g % KBUF, P * (2 * jk + k):P * (2 * jk + k) + P],
                                               QT[0:MROWS, g % 2, L * j:L * j + L],
                                               start=not masked, stop=True, skip_group_check=True)
                        mm.then_inc(ts["a_st"], 1)

                    def features(g, k, a):
                        o = sg_bank(("G", g, k, a))
                        if k == 0 and a == 0:
                            for kind in ("FQ", "FK", "FKL"):
                                pe.wait_ge(*read(use_no[kind, g]))
                        for j in (2 * a, 2 * a + 1):
                            r = P * (2 * j + k)
                            oj = o[:, L * (j % 2) + from_q(k):L * (j % 2) + L]
                            qs = slice(L * j + from_q(k), L * j + L)
                            pe.matmul(oj, FKT[0:5 * M, g % 2, r:r + P], FQT[0:5 * M, g % 2, qs], start=True, stop=False)
                            mm = pe.matmul(oj, FKLT[0:M, g % 2, r:r + P], FQT[0:M, g % 2, qs], start=False, stop=True)
                        mm.then_inc(ts["a_s"], 1)

                    def sums(g, k, part):
                        if part:
                            pe.wait_ge(*after("a_gm", 4 * g + 2 * k + 2))
                        else:
                            pe.wait_ge(*after("a_exp", 2 * g + k + 1))
                        if k == 0 and g >= 1:
                            pe.wait_ge(*after("a_accg" if part else "a_acc", g))
                        b, hg = divmod(g, 4)
                        for j in range(GH):
                            h = 4 * hg + j if masked else hg
                            r = from_q(k) if part else 0
                            mm = pe.matmul(ps[32 * j:32 * j + 32, 6 + part, r:L],
                                           V2[:, 2 * b + k, VW * h:VW * h + 32],
                                           (PG if part else PTn)[:, k, L * j + r:L * j + L],
                                           start=(k == 0), stop=(k == 1), skip_group_check=bool(part))
                        mm.then_inc(ts["a_pg" if part else "a_pv"], 1)

                    rows_T("Q", 0)
                    rows_T("K", 0)
                    for i in range(NG + 2):
                        g, o = i - 1, i - 2
                        has_i, has_g, has_o = i < NG, 0 <= g < NG, o >= 0
                        if not masked:
                            if has_g:
                                rows_T("QT", g)
                            if has_i:
                                scores_q(i, 0, 0)
                                scores_q(i, 0, 1)
                                scores_q(i, 1, 0)
                            if has_o:
                                sums(o, 0, 0)
                            if has_g:
                                scores_k(g, 0)
                            if has_i:
                                scores_q(i, 1, 1)
                            if has_o:
                                sums(o, 1, 0)
                        else:
                            if has_i:
                                scores_q(i, 0, 0)
                                scores_q(i, 0, 1)
                            if has_g:
                                rows_T("QT", g)
                            if has_o:
                                sums(o, 0, 1)
                                sums(o, 1, 1)
                            if has_i:
                                scores_q(i, 1, 0)
                            if has_g:
                                scores_k(g, 0)
                            if has_o:
                                sums_T("O", o)
                            if has_i:
                                scores_q(i, 1, 1)
                        if masked and has_i:
                            rows_T("FQ", i)
                        if not masked and i + 1 < NG:
                            rows_T("Q", i + 1)
                            rows_T("K", i + 1)
                        if has_g:
                            scores_k(g, 1)
                        if not masked and has_o:
                            sums_T("O", o)
                        if masked and has_g:
                            features(g, 0, 0)
                        if masked and has_o:
                            sums_T("OG", o)
                        if masked and has_g:
                            features(g, 0, 1)
                        if masked and has_i:
                            rows_T("FK", i)
                        if masked and has_g:
                            sums(g, 0, 0)
                            features(g, 1, 0)
                        if masked and i + 1 < NG:
                            rows_T("Q", i + 1)
                            rows_T("K", i + 1)
                        if masked and has_g:
                            features(g, 1, 1)
                        if masked and has_i:
                            rows_T("FKL", i)
                        if masked and has_g:
                            sums(g, 1, 0)

                def copy_T(eng, kind, g):
                    n = use_no[kind, g]
                    eng.wait_ge(*after("a_t", n + 1))
                    pr = M if kind == "FKL" else P
                    w = 2 * P * (NKJ if kind == "K" else GH)
                    o, i_ = dst[kind][0:pr, g % (KBUF if kind == "K" else 2), 0:w], bank(n).bitcast(BF16)[0:pr, 0:w]
                    if uses[n][2] == "act":
                        eng.activation(o, i_, ACT.Copy).then_inc(ts["a_td_act"], 1)
                    else:
                        eng.tensor_copy(o, i_).then_inc(ts["a_td_dve"], 1)

                @block.scalar
                def _(act):
                    def exps(g, k):
                        act.wait_ge(*after("a_st", 2 * g + k + 1))
                        if g >= 1:
                            act.wait_ge(*after("a_pv", 2 * g - 1 + k))
                        act.activation(PTn[:, k, :], ps[:, 4:6, :], ACT.Exp, scale=SCALE).then_inc(ts["a_exp"], 1)

                    def sums_out(g):
                        act.wait_ge(*after("a_pv", 2 * g + 2))
                        if g >= 1:
                            act.wait_ge(*read(use_no["O", g - 1]))
                        act.activation(OTs[:, :], ps[:, 6, 0:L], ACT.Copy).then_inc(ts["a_acc"], 1)

                    if not masked:
                        copy_T(act, "Q", 0)
                    copy_T(act, "K", 0)
                    if masked:
                        features_high(act, 1)
                    for i in range(NG + 2):
                        g, o = i - 1, i - 2
                        has_g = 0 <= g < NG
                        if masked and i == 2:
                            features_repeat(act, 1)
                        if masked and o >= 0:
                            act.wait_ge(*after("a_pg", 2 * o + 2))
                            if o >= 1:
                                act.wait_ge(*read(use_no["OG", o - 1]))
                            act.activation(OTg[:, :], ps[:, 7, 0:L], ACT.Copy).then_inc(ts["a_accg"], 1)
                        if has_g:
                            exps(g, 0)
                        if not masked and o >= 0:
                            sums_out(o)
                        if masked and i < NG:
                            if i >= 2:
                                act.wait_ge(*after("a_s", sg_no["G", i - 2, 1, 1] + 1))
                            copy_T(act, "FQ", i)
                        if not masked and i + 1 < NG:
                            copy_T(act, "Q", i + 1)
                            copy_T(act, "K", i + 1)
                        if has_g:
                            exps(g, 1)
                        if masked and i < NG:
                            copy_T(act, "FK", i)
                        if masked and i + 1 < NG:
                            copy_T(act, "K", i + 1)
                        if masked and i < NG:
                            copy_T(act, "FKL", i)
                        if masked and has_g:
                            sums_out(g)

                @block.vector
                def _(dve):
                    def bank_of(u):
                        return ps[:, SGB[sg_no[u] % len(SGB)], :].rearrange("p (j n) -> p j n", n=L)

                    def maxima(g, q, a):
                        b, hg = divmod(g, 4)
                        u = ("S", g, q, a)
                        dve.wait_ge(*after("a_s", sg_no[u] + 1))
                        at = 4 * hg + 2 * a
                        dve.tensor_reduce(nmall[:, 2 * b + q, at:at + 2], bank_of(u),
                                          AX.X, ALU.max, negate=True).then_inc(ts["a_sr"], 1)

                    def masked_features(g, k, a):
                        u = ("G", g, k, a)
                        n = 4 * g + 2 * k + a
                        dve.wait_ge(*after("a_s", sg_no[u] + 1))
                        if g >= 1 and a == 0:
                            dve.wait_ge(*after("a_pg", 2 * g - 1 + k))
                        r = from_q(k)
                        dve.tensor_tensor(PG[:, k, 2 * L * a:2 * L * a + 2 * L].rearrange("p (j n) -> p j n", n=L)[:, :, r:L],
                                          bank_of(u)[:, :, r:L],
                                          wmask[:, k, r:L].unsqueeze(1).broadcast_to([P, 2, L - r]),
                                          ALU.mult).then_inc(ts["a_gm"], 1)
                        dve.wait_ge(*after("a_gm", n + 1))
                        dve.sem_inc(ts["a_sr"], 1)

                    def outputs(kind, g):
                        b, hg = divmod(g, 4)
                        n = use_no[kind, g]
                        dve.wait_ge(*after("a_t", n + 1))
                        o = bank(n)[:, 0:2 * P].rearrange("p (q j d) -> p q j d", q=2, d=32)
                        S_ = As if kind == "O" else Gs
                        for q in range(2):
                            ins = dve.tensor_copy(S_[:, 2 * b + q, 4 * hg:4 * hg + 4, :], o[:, q, :, 0:VW])
                        ins.then_inc(ts["a_td_dve"], 1)

                    if masked:
                        copy_T(dve, "Q", 0)
                    for i in range(NG + 2):
                        g, o = i - 1, i - 2
                        has_g = 0 <= g < NG
                        if has_g and g >= 2:
                            dve.wait_ge(*after("a_st", 2 * g - 2))
                        if has_g and not masked:
                            copy_T(dve, "QT", g)
                        if i < NG:
                            maxima(i, 0, 0)
                            maxima(i, 0, 1)
                        if has_g and masked:
                            copy_T(dve, "QT", g)
                        if i < NG:
                            maxima(i, 1, 0)
                        if o >= 0 and masked:
                            outputs("O", o)
                        if i < NG:
                            b, hg = divmod(i, 4)
                            maxima(i, 1, 1)
                            dve.wait_ge(*after("a_sr", sg_no["S", i, 1, 1] + 1))
                            nm_ = nmall[:, 2 * b:2 * b + 2, 4 * hg:4 * hg + 4]
                            q_ = QN[:, 2 * b:2 * b + 2, 4 * hg:4 * hg + 4, :]
                            link_dve(dve.tensor_copy(q_[:, :, :, SROWS], nm_))
                            link_dve(dve.tensor_tensor(nrs, nm_, q_[:, :, :, SROWS], ALU.subtract))
                            link_dve(dve.tensor_copy(q_[:, :, :, SROWS + 1], nrs))
                            dve.tensor_tensor(q_[:, :, :, SROWS + 2], nrs, q_[:, :, :, SROWS + 1],
                                              ALU.subtract).then_inc(ts["a_mp"], 1)
                        if o >= 0 and not masked:
                            outputs("O", o)
                        if masked and has_g:
                            masked_features(g, 0, 0)
                        if masked and o >= 0:
                            outputs("OG", o)
                        if masked and has_g:
                            masked_features(g, 0, 1)
                            masked_features(g, 1, 0)
                        if masked and i + 1 < NG:
                            copy_T(dve, "Q", i + 1)
                        if masked and has_g:
                            masked_features(g, 1, 1)
                        if masked and i < 2:
                            features_lower(dve, i, 1)

            base["a_t"] += len(uses)
            for who in ("act", "dve"):
                base["a_td_" + who] += sum(u[2] == who for u in uses)
            for name in ("a_s", "a_sr"):
                base[name] += len(sg)
            for name in ("a_mp", "a_acc"):
                base[name] += NG
            for name in ("a_st", "a_exp", "a_pv"):
                base[name] += 2 * NG
            if masked:
                base["a_gm"] += 4 * NG
                base["a_pg"] += 2 * NG
                base["a_accg"] += NG

        attention(True)

        def heads(T, r):
            return T[:, RH[r], :, 0:DH].rearrange("p r h d -> p (r h) d")

        def by_head(t, r):
            return t[:, RH[r], :].rearrange("p r h -> p (r h)").unsqueeze(2).broadcast_to([P, 2 * H, DH])

        s5 = {n: sem(n) for n in ("c_ln1", "c_l2", "c_v")}
        A16 = As[:, :, :, DH]
        Y = Gs[:, :, :, DH]
        with nc.Block() as block:
            @block.vector
            def _(dve):
                link_dve(dve.tensor_scalar(t1, Y, 1e-24, None, ALU.max))
                for R in range(RT):
                    ins = dve.tensor_tensor(t2[:, R, :], qls[:, R, :], kls[:, R // 2, :], ALU.add)
                link_dve(ins)
                dve.sem_inc(s5["c_ln1"], 1)
                dve.wait_ge(s5["c_l2"], 2)
                link_dve(dve.scalar_tensor_tensor(out=t0, in0=nmall, scalar=-SCALE, in1=t0, op0=ALU.mult, op1=ALU.add))
                link_dve(dve.tensor_tensor(t1, t1, t2, ALU.add))
                link_dve(dve.tensor_tensor(t3, t0, t1, ALU.max))
                link_dve(dve.tensor_tensor(t0, t0, t3, ALU.subtract))
                dve.tensor_tensor(t1, t1, t3, ALU.subtract)
                link_dve(dve.tensor_tensor(t2, t2, t3, ALU.subtract))
                dve.sem_inc(s5["c_ln1"], 1)

                a_ = [att[:, t, :].rearrange("p r (h d) -> p (r h) d", d=DH) for t in RH]
                link_dve(dve.reciprocal(t3, A16))
                for r in range(2):
                    ins = dve.tensor_tensor(a_[r], heads(As, r), by_head(t3, r), ALU.mult)
                link_dve(ins)
                dve.wait_ge(s5["c_l2"], 5)
                link_dve(dve.tensor_tensor(t0, t0, t1, ALU.add))
                link_dve(dve.reciprocal(t0, t0))
                link_dve(dve.tensor_tensor(t0, t0, t2, ALU.mult))
                for r in range(2):
                    link_dve(dve.tensor_tensor(heads(Gs, r), heads(Gs, r), by_head(t0, r), ALU.mult))
                    dve.tensor_tensor(a_[r], a_[r], heads(Gs, r), ALU.add).then_inc(s_heads_out, 1)
                for r in range(2):
                    residual_dve(dve, 1, r, X)
                    ln_dve(dve, 2, r)
                for R in range(RT + 1):
                    if R < RT:
                        dve.wait_ge(s5["c_v"], R + 1)
                        dve.tensor_tensor(QK[:, R, 0:D + 64], ps[:, R, 0:D + 64], b_qkv3[:, 0:D + 64], ALU.add)\
                           .then_inc(s_qk_read, 1)
                        v_ = V2[:, R, 0:GH * VW].rearrange("p (h d) -> p h d", d=VW)
                        dve.tensor_tensor(v_[:, :, 0:DH], ps[:, R, D + 64:D + 128].rearrange("p (h d) -> p h d", d=DH),
                                          b_qkv3[:, D + 64:D + 128].rearrange("p (h d) -> p h d", d=DH), ALU.add)
                    if R >= 1:
                        lower_dve(dve, R - 1, GH, RT + R)

            @block.scalar
            def _(act):
                act.wait_ge(s5["c_ln1"], 1)
                act.activation(t0, A16, ACT.Ln).then_inc(s5["c_l2"], 1)
                act.activation(t1, t1, ACT.Ln).then_inc(s5["c_l2"], 1)
                act.wait_ge(s5["c_ln1"], 2)
                act.activation(t0, t0, ACT.Exp).then_inc(s5["c_l2"], 1)
                act.activation(t1, t1, ACT.Exp).then_inc(s5["c_l2"], 1)
                act.activation(t2, t2, ACT.Exp).then_inc(s5["c_l2"], 1)
                rows_T_act(act, 3, 0)
                rows_T_act(act, 3, 1)
                for r in range(2):
                    ln_act(act, 2, r)
                    rows_T_act(act, 4, r)
                for R in range(RT):
                    high_act(act, R, GH, RT + R + 1)

            @block.gpsimd
            def _(pool):
                pool.wait_ge(s_rowsT, 5 * KT)
                pool.wait_ge(s_rows_normed, 3 * RT)
                pool.tensor_tensor(lnx[:, :, :], lnx[:, :, :], b_o3.unsqueeze(1).broadcast_to([P, RT, D]), ALU.add)
                for R in range(RT):
                    middle_pool(pool, R, GH, RT + R + 1)

            @block.tensor
            def _(pe):
                for r in range(2):
                    pe.wait_ge(s_heads_out, r + 1)
                    rows_T_pe(pe, att, r)
                for R in range(RT):
                    if R % 2 == 0:
                        pe.wait_ge(s_rowsT_read, 6 + R // 2 + 1)
                    project_pe(pe, woT2, R)
                pe.wait_ge(s_w3_in, 128)
                kv = wk.rearrange("p (k n) -> p k n", k=KT)
                for R in range(RT):
                    if R % 2 == 0:
                        r = R // 2
                        pe.wait_ge(s_rows_normed, 2 * RT + 2 * r + 2)
                        rows_T_pe(pe, lnx, r)
                        pe.wait_ge(s_rowsT_read, 8 + r + 1)
                    for lo, hi, w in ((0, D, wq), (D, D + 128, kv)):
                        for k in range(KT):
                            mm = pe.matmul(ps[:, R, lo:hi], lnT[:, k, P * R:P * R + P], w[:, k, :],
                                           start=(k == 0), stop=(k == KT - 1))
                    mm.then_inc(s5["c_v"], 1)

        attention(False)

        s7 = {n: sem(n) for n in ("m_wn", "m_ln", "m_lg", "m_sg", "m_M", "m_rk", "m_h", "m_g", "m_y",
                                  "m_acc", "m_c")}

        def c8(at):
            return small[:, at:at + RT * E].rearrange("p (r e) -> p r e", e=E)

        def c1(at):
            return small[:, at:at + RT]

        pr, Ma, Mb, wt, ec, tmp = c8(0), c8(32), c8(64), c8(96), c8(128), c8(160)
        Mbf = small[:, 192:208].bitcast(BF16).rearrange("p (r e) -> p r e", e=E)
        top1, top2, rcp, cm = c1(224), c1(228), c1(232), c1(236)

        def bc(x):
            return x.unsqueeze(2).broadcast_to([P, RT, E])

        def rms_dve(dve, n, r, rows, wn):
            t = RH[r]
            half_stats(dve, rows, r)
            link_dve(dve.tensor_tensor(ve[:, t], mv[:, t, 0], mv[:, t, 0], ALU.mult))
            dve.scalar_tensor_tensor(out=ve[:, t], in0=ve[:, t], scalar=1e-6, in1=mv[:, t, 1],
                                     op0=ALU.add, op1=ALU.add).then_inc(s_var, 1)
            dve.wait_ge(s_std, 2 * n + r)
            link_dve(dve.reciprocal(rs[:, t], sd[:, t]))
            for R in (2 * r, 2 * r + 1):
                ins = dve.scalar_tensor_tensor(out=rows[:, R, :], in0=rows[:, R, :], scalar=rs[:, R:R + 1],
                                               in1=wn[:, :], op0=ALU.mult, op1=ALU.mult)
            link_dve(ins)

        with nc.Block() as block:
            @block.sync
            def _(sp):
                sp.dma_start(wn1[:, :], t_in["L0_ffn_norm1_w"].partition_broadcast(P)).then_inc(s7["m_wn"], 16)
                sp.dma_start(wn2[:, :], t_in["L0_ffn_norm2_w"].partition_broadcast(P)).then_inc(s7["m_wn"], 16)
                sp.dma_start(gate[:, :, :], t_in["L0_ffn_gate_w"].rearrange("(k p) e -> p k e", p=P)).then_inc(s7["m_wn"], 16)
                for b, r in enumerate(RH):
                    sp.wait_ge(s7["m_ln"], 3 + b)
                    sp.dma_start(out[b].rearrange("(r p) d -> p r d", p=P), X[:, r, :]).then_inc(s_out_stored, 16)
                sp.wait_ge(s_out_stored, 32)

            @block.gpsimd
            def _(pool):
                link_pool(pool.memset(lowb[:, :, :], 1.0))
                link_pool(pool.affine_select(out=lowb[:, 0, :], in_=lowb[:, 0, :], compare_op=ALU.is_gt, fill=0.0,
                                             base=0, pattern=[[1, P]], channel_multiplier=-1))
                link_pool(pool.iota(ec[:, :, :], pattern=[[0, RT], [-1, E]], base=E, channel_multiplier=0,
                                    allow_small_or_imprecise_dtypes=True))
                pool.sem_inc(s7["m_c"], 1)

            @block.vector
            def _(dve):
                link_dve(dve.reciprocal(t1, A16))
                for r in range(2):
                    dve.tensor_tensor(att[:, RH[r], :].rearrange("p r (h d) -> p (r h) d", d=DH), heads(As, r),
                                      by_head(t1, r), ALU.mult).then_inc(s_heads_out, 1)
                dve.wait_ge(s7["m_wn"], 48)
                for r in range(2):
                    residual_dve(dve, 2, r, lnx)
                    rms_dve(dve, 3, r, lnx, wn1)
                    dve.sem_inc(s7["m_ln"], 1)
                dve.wait_ge(s7["m_sg"], 1)
                dve.wait_ge(s7["m_c"], 1)
                for first, (top, Mx) in enumerate(((top1, Ma), (top2, Mb))):
                    link_dve(dve.tensor_reduce(top, pr, AX.X, ALU.max))
                    link_dve(dve.tensor_tensor(tmp, pr, bc(top), ALU.is_equal))
                    link_dve(dve.tensor_tensor(tmp, tmp, ec, ALU.mult))
                    link_dve(dve.tensor_reduce(cm, tmp, AX.X, ALU.max))
                    link_dve(dve.tensor_tensor(Mx, tmp, bc(cm), ALU.is_equal))
                    if first == 0:
                        link_dve(dve.scalar_tensor_tensor(out=pr, in0=Ma, scalar=-4.0, in1=pr, op0=ALU.mult, op1=ALU.add))
                link_dve(dve.scalar_tensor_tensor(out=rcp, in0=top1, scalar=1e-6, in1=top2, op0=ALU.add, op1=ALU.add))
                link_dve(dve.reciprocal(rcp, rcp))
                link_dve(dve.tensor_tensor(tmp, Ma, bc(top1), ALU.mult))
                link_dve(dve.tensor_tensor(wt, Mb, bc(top2), ALU.mult))
                link_dve(dve.tensor_tensor(wt, wt, tmp, ALU.add))
                link_dve(dve.tensor_tensor(wt, wt, bc(rcp), ALU.mult))
                link_dve(dve.tensor_tensor(Mbf, Ma, Mb, ALU.add))
                dve.sem_inc(s7["m_M"], 1)
                dve.wait_ge(s7["m_rk"], 1)
                link_dve(dve.tensor_scalar(tmp, ps[:, 7, 0:RT * E].rearrange("p (r e) -> p r e", e=E), float(CAP), None,
                                           ALU.is_lt))
                link_dve(dve.tensor_tensor(wt, wt, tmp, ALU.mult))
                link_dve(dve.tensor_copy(acc[:, :, :], lnx[:, :, :]))
                for e in range(E):
                    for R in range(RT):
                        if R % 2 == 0:
                            dve.wait_ge(s7["m_y"], 2 * e + R // 2 + 1)
                        y_ = ps[:, 4 + 2 * (e % 2) + R // 2, D * (R % 2):D * (R % 2) + D]
                        ins = dve.scalar_tensor_tensor(out=acc[:, R, :], in0=y_,
                                                       scalar=wt[:, R, e:e + 1], in1=acc[:, R, :], op0=ALU.mult,
                                                       op1=ALU.add)
                        ins.then_inc(s7["m_acc"], 1)
                        if e == E - 1 and R % 2 == 1:
                            r = R // 2
                            dve.wait_ge(s7["m_acc"], RT * e + R + 1)
                            rms_dve(dve, 4, r, acc, wn2)
                            dve.tensor_tensor(X[:, RH[r], :], X[:, RH[r], :], acc[:, RH[r], :],
                                              ALU.add).then_inc(s7["m_ln"], 1)
                    dve.wait_ge(s7["m_acc"], RT * (e + 1))

            @block.scalar
            def _(act):
                rows_T_act(act, 5, 0)
                rows_T_act(act, 5, 1)
                for r in range(2):
                    ln_act(act, 3, r)
                    rows_T_act(act, 6, r)
                act.wait_ge(s7["m_lg"], 1)
                act.activation(pr, ps[:, 6, 0:RT * E].rearrange("p (r e) -> p r e", e=E), ACT.Sigmoid).then_inc(s7["m_sg"], 1)
                for e in range(E):
                    for f in range(FF // P):
                        n = 4 * e + f
                        act.wait_ge(s7["m_h"], n + 1)
                        if e >= 2:
                            act.wait_ge(s7["m_y"], 2 * (e - 1))
                        act.activation(hT[:, e % 2, f, :], ps[:, n % 4, :], ACT.Gelu).then_inc(s7["m_g"], 1)
                ln_act(act, 4, 0)
                ln_act(act, 4, 1)

            @block.tensor
            def _(pe):
                for r in range(2):
                    pe.wait_ge(s_heads_out, 2 + r + 1)
                    rows_T_pe(pe, att, r)
                for R in range(RT):
                    if R % 2 == 0:
                        pe.wait_ge(s_rowsT_read, 10 + R // 2 + 1)
                    project_pe(pe, wo, R)
                for r in range(2):
                    pe.wait_ge(s7["m_ln"], r + 1)
                    rows_T_pe(pe, lnx, r)
                pe.wait_ge(s_rowsT_read, 7 * KT)
                for R in range(RT):
                    for k in range(KT):
                        mm = pe.matmul(ps[:, 6, E * R:E * R + E], lnT[:, k, P * R:P * R + P], gate[:, k, :],
                                       start=(k == 0), stop=(k == KT - 1))
                mm.then_inc(s7["m_lg"], 1)

                def up(e):
                    for f in range(FF // P):
                        n = 4 * e + f
                        if n >= 4:
                            pe.wait_ge(s7["m_g"], n - 3)
                        for k in range(KT):
                            mm = pe.matmul(ps[:, n % 4, :], w1[:, e, k, P * f:P * f + P], lnT[:, k, :],
                                           start=(k == 0), stop=(k == KT - 1))
                        mm.then_inc(s7["m_h"], 1)

                pe.wait_ge(s_experts_in, 256)
                up(0)
                pe.wait_ge(s7["m_M"], 1)
                for R in range(RT):
                    for r in range(R + 1):
                        mm = pe.matmul(ps[:, 7, E * R:E * R + E], lowb[:, 0 if r == R else 1, :], Mbf[:, r, :],
                                       start=(r == 0), stop=(r == R))
                mm.then_inc(s7["m_rk"], 1)
                for e in range(E):
                    if e + 1 < E:
                        up(e + 1)
                    for R in range(RT):
                        if e == 1 and R == 0:
                            pe.wait_ge(s7["m_acc"], 1)
                        if R % 2 == 0 and e >= 2:
                            pe.wait_ge(s7["m_acc"], RT * (e - 1))
                        if R == 0:
                            pe.wait_ge(s7["m_g"], 4 * (e + 1))
                        for f in range(FF // P):
                            mm = pe.matmul(ps[:, 4 + 2 * (e % 2) + R // 2, 256 * (R % 2):256 * (R % 2) + 256],
                                           hT[:, e % 2, f, P * R:P * R + P], w2[:, e, f, :],
                                           start=(f == 0), stop=(f == FF // P - 1))
                        if R % 2 == 1:
                            mm.then_inc(s7["m_y"], 1)


_INS = ['x', 'ctx_512', 'L0_xattn_Wq', 'L0_xattn_bq', 'L0_xattn_Wk', 'L0_xattn_bk', 'L0_xattn_Wv', 'L0_xattn_bv',
        'L0_xattn_Wo', 'L0_xattn_bo', 'L0_attn_Wqkv_w', 'L0_attn_Wqkv_b', 'L0_attn_proj', 'L0_attn_out_w',
        'L0_attn_out_b', 'L0_ffn_qw', 'L0_ffn_qb', 'L0_ffn_kw', 'L0_ffn_kb', 'L0_ffn_vw', 'L0_ffn_vb', 'L0_ffn_ow',
        'L0_ffn_ob', 'L0_ffn_gate_w', 'L0_ffn_w1', 'L0_ffn_w2', 'L0_ffn_norm1_w', 'L0_ffn_norm2_w']


def kernel(**inputs):
    import numpy as _np
    import concourse.bacc as _bacc
    from concourse import mybir as _mybir
    from concourse.bass_utils import run_bass_kernel_spmd as _run

    nc = _bacc.Bacc("TRN2", target_bir_lowering=False, num_devices=1)
    arrays, aps = {}, {}
    for name in _INS:
        a = _np.ascontiguousarray(inputs[name])
        arrays[f"in_{name}_dram"] = a
        aps[name] = nc.dram_tensor(f"in_{name}_dram", a.shape, _mybir.dt.from_np(a.dtype), kind="ExternalInput").ap()
    out = nc.dram_tensor("out_0_dram", (B, L, D), F32, kind="ExternalOutput").ap()
    build(nc, aps, out)
    r = _run(nc, [arrays], core_ids=[0])
    return r.results[0]["out_0_dram"]
```
